# Optimizing a Trainium2 kernel written in Bass

```python
import numpy as np
import jax
import jax.numpy as jnp

def _softmax(x, axis=-1):
    return jax.nn.softmax(x, axis=axis)

def _gelu(x):
    return jax.nn.gelu(x, approximate=True)

def _silu(x):
    return jax.nn.silu(x)

def _sigmoid(x):
    return jax.nn.sigmoid(x)

def _layernorm(x, axis=-1, eps=1e-05):
    m = jnp.mean(x, axis=axis, keepdims=True)
    v = jnp.var(x, axis=axis, keepdims=True)
    return (x - m) / jnp.sqrt(v + eps)

def _scatter_add(tgt, idx, src, axis=0):
    return tgt.at[idx].add(src)

def _segment_sum(src, seg, n):
    return jax.ops.segment_sum(src, seg, n)
kernel_name = 'mk_cond_seq_d4_seqx_r8_5eca65'

def setup_inputs(seed: int=0):
    np.random.seed(seed)
    _w = jnp.asarray

    def _rec_inputs():
        import jax
        import jax.numpy as jnp
        _rk = jax.random.key(seed)
        x = -0.0002928 + 1 * jax.random.normal(jax.random.fold_in(_rk, 1), (32, 32, 128), jnp.float32)
        _lenS = 32 - jax.random.randint(jax.random.fold_in(_rk, 7), (32,), 0, max(1, 32 // 4) + 1, jnp.int32)
        _lenS2 = 32 - jax.random.randint(jax.random.fold_in(_rk, 8), (32,), 0, max(1, 32 // 4) + 1, jnp.int32)
        cond_1024 = 0.0061147 + 1.02565 * jax.random.normal(jax.random.fold_in(_rk, 11), (32, 128), jnp.float32)
        _validS = jnp.arange(32)[None, :] < _lenS[:, None]
        _validS2 = jnp.arange(32)[None, :] < _lenS2[:, None]
        _causal = jnp.tril(jnp.ones((32, 32), dtype=bool))
        mask_BxS_bf0 = jnp.logical_not(jnp.ones((32, 32), dtype=bool))
        mask_BxSxSx11_ik0 = jnp.where(jnp.ones((32, 32, 32, 11), dtype=bool), 0, 1).astype(jnp.int32)
        return (x, cond_1024, mask_BxS_bf0, mask_BxSxSx11_ik0)
    x, cond_1024, mask_BxS_bf0, mask_BxSxSx11_ik0 = _rec_inputs()

    def _L0_cond_setup():
        import jax, jax.numpy as jnp
        import numpy as np
        EPS = 1e-05

        def _sln(h, w, ln_g, ln_b, Wg, bg, Wb, bb):
            mu = jnp.mean(h, axis=-1, keepdims=True)
            var = jnp.mean((h - mu) ** 2, axis=-1, keepdims=True)
            ln = (h - mu) / jnp.sqrt(var + EPS) * ln_g + ln_b
            gamma = (w @ Wg.T + bg)[:, None, :]
            beta = (w @ Wb.T + bb)[:, None, :]
            return gamma * ln + beta
        key = jax.random.key(seed)
        ks = jax.random.split(key, 20)
        B, N, D = (4, 128, 128)
        F = 4 * D
        s = lambda fan: 1.0 / np.sqrt(fan)
        inp = {'hidden': jax.random.normal(ks[0], (B, N, D), jnp.float32), 'w': jax.random.normal(ks[1], (B, D), jnp.float32), 'ln_g': jnp.ones((D,), jnp.float32), 'ln_b': jnp.zeros((D,), jnp.float32), 'Wg': jax.random.normal(ks[2], (D, D), jnp.float32) * s(D), 'bg': jnp.zeros((D,), jnp.float32), 'Wb': jax.random.normal(ks[3], (D, D), jnp.float32) * s(D), 'bb': jnp.zeros((D,), jnp.float32), 'Wqkv': jax.random.normal(ks[4], (3 * D, D), jnp.float32) * s(D), 'bqkv': jnp.zeros((3 * D,), jnp.float32), 'Wp': jax.random.normal(ks[5], (D, D), jnp.float32) * s(D), 'bp': jnp.zeros((D,), jnp.float32), 'W1': jax.random.normal(ks[6], (F, D), jnp.float32) * s(D), 'b1': jnp.zeros((F,), jnp.float32), 'W2': jax.random.normal(ks[7], (D, F), jnp.float32) * s(F), 'b2': jnp.zeros((D,), jnp.float32), 'num_heads': 16}
        return inp
    _L0_cond_all = _L0_cond_setup()
    _L0_cond_in = {k: v for k, v in _L0_cond_all.items() if k in ('ln_g', 'ln_b', 'Wg', 'bg', 'Wb', 'bb', 'Wqkv', 'bqkv', 'Wp', 'bp', 'W1', 'b1', 'W2', 'b2')}
    del _L0_cond_all

    def _L1_cond_setup():
        import math
        import jax, jax.numpy as jnp
        import numpy as np
        H = 128
        NH = 16
        HD = H // NH
        CD = 128
        MLP = 512
        EPS = 1e-05

        def _layernorm(x):
            mu = jnp.mean(x, axis=-1, keepdims=True)
            var = jnp.var(x, axis=-1, keepdims=True)
            return (x - mu) * jax.lax.rsqrt(var + EPS)

        def _adaln(x, cond, W, b):
            ss = cond @ W.T + b
            scale, shift = jnp.split(ss, 2, axis=-1)
            return _layernorm(x) * (1.0 + scale[:, None, :]) + shift[:, None, :]
        key = jax.random.key(seed)
        ks = jax.random.split(key, 16)
        s = 0.02
        inp = {'x': jax.random.normal(ks[0], (2, 256, H), jnp.float32), 'cond': jax.random.normal(ks[1], (2, CD), jnp.float32), 'key_padding_mask': jnp.zeros((2, 256), dtype=bool), 'w_adaln1': jax.random.normal(ks[2], (2 * H, CD), jnp.float32) * s, 'b_adaln1': jnp.zeros((2 * H,), jnp.float32), 'w_adaln2': jax.random.normal(ks[3], (2 * H, CD), jnp.float32) * s, 'b_adaln2': jnp.zeros((2 * H,), jnp.float32), 'wq': jax.random.normal(ks[4], (H, H), jnp.float32) * s, 'bq': jnp.zeros((H,), jnp.float32), 'wk': jax.random.normal(ks[5], (H, H), jnp.float32) * s, 'bk': jnp.zeros((H,), jnp.float32), 'wv': jax.random.normal(ks[6], (H, H), jnp.float32) * s, 'bv': jnp.zeros((H,), jnp.float32), 'wo': jax.random.normal(ks[7], (H, H), jnp.float32) * s, 'bo': jnp.zeros((H,), jnp.float32), 'w1': jax.random.normal(ks[8], (MLP, H), jnp.float32) * s, 'b1': jnp.zeros((MLP,), jnp.float32), 'w2': jax.random.normal(ks[9], (H, MLP), jnp.float32) * s, 'b2': jnp.zeros((H,), jnp.float32)}
        return inp
    _L1_cond_all = _L1_cond_setup()
    _L1_cond_in = {k: v for k, v in _L1_cond_all.items() if k in ('w_adaln1', 'b_adaln1', 'w_adaln2', 'b_adaln2', 'wq', 'bq', 'wk', 'bk', 'wv', 'bv', 'wo', 'bo', 'w1', 'b1', 'w2', 'b2')}
    del _L1_cond_all

    def _L2_cond_setup():
        import jax, jax.numpy as jnp
        import numpy as np
        NONGT = 20
        H = 16
        NEG = -9000000000000000.0

        def _gat_attention(self_feat, cond_adj, label_bias, Wq, bq, Wk, bk, Wout, bout):
            B, N, F = self_feat.shape
            ng = min(NONGT, N)
            dh = F // H
            kv = self_feat[:, :ng]
            qh = (self_feat @ Wq.T + bq).reshape(B, N, H, dh)
            kh = (kv @ Wk.T + bk).reshape(B, ng, H, dh)
            aff = jnp.einsum('bnhd,bmhd->bnhm', qh, kh) * (1.0 / np.sqrt(dh))
            mask = cond_adj[:, :, None, :] > 0
            aff = jnp.where(mask, aff, NEG) + label_bias[:, :, None, :]
            w = jax.nn.softmax(aff, axis=-1)
            out_t = jnp.einsum('bnhm,bmf->bnhf', w, kv)
            out = jnp.einsum('bnhf,hgf->bnhg', out_t, Wout) + bout.reshape(H, F // H)
            return out.reshape(B, N, F)

        def _forward(v, q, adj, W_self, b_self, w_bias, b_bias, Wq, bq, Wk, bk, Wout, bout):
            adj_f = adj.astype(jnp.float32)
            exp_v = v
            row_zero = exp_v.sum(-1) == 0
            q_exp = jnp.where(row_zero[..., None], 0.0, q[:, None, :])
            vcq = jnp.concatenate([exp_v, q_exp], axis=-1)
            self_feat = vcq @ W_self.T + b_self
            output = self_feat
            for d in range(2):
                A = adj_f if d == 0 else jnp.swapaxes(adj_f, 1, 2)
                A = A[:, :, :NONGT, :]
                cond = A.sum(-1)
                vb = A @ w_bias + b_bias
                output = output + _gat_attention(self_feat, cond, vb, Wq[d], bq[d], Wk[d], bk[d], Wout[d], bout[d])
            rel = jax.nn.relu(output)
            return exp_v + rel
        key = jax.random.key(seed)
        ks = jax.random.split(key, 8)
        B, N, L, F, Q = (32, 36, 11, 128, 128)
        IN = F + Q
        s = 0.02
        return {'v': jax.random.normal(ks[0], (B, N, F), jnp.float32), 'q': jax.random.normal(ks[1], (B, Q), jnp.float32), 'adj': jax.random.randint(ks[2], (B, N, N, L), 0, 2, jnp.int32), 'W_self': jax.random.normal(ks[3], (F, IN), jnp.float32) * s, 'b_self': jnp.zeros((F,), jnp.float32), 'w_bias': jax.random.normal(ks[4], (L,), jnp.float32) * s, 'b_bias': jnp.zeros((), jnp.float32), 'Wq': jax.random.normal(ks[5], (2, F, F), jnp.float32) * s, 'bq': jnp.zeros((2, F), jnp.float32), 'Wk': jax.random.normal(ks[6], (2, F, F), jnp.float32) * s, 'bk': jnp.zeros((2, F), jnp.float32), 'Wout': jax.random.normal(ks[7], (2, H, F // H, F), jnp.float32) * s, 'bout': jnp.zeros((2, F), jnp.float32)}
    _L2_cond_all = _L2_cond_setup()
    _L2_cond_in = {k: v for k, v in _L2_cond_all.items() if k in ('W_self', 'b_self', 'w_bias', 'b_bias', 'Wq', 'bq', 'Wk', 'bk', 'Wout', 'bout')}
    del _L2_cond_all

    def _L3_cond_setup():
        import jax, jax.numpy as jnp
        import numpy as np
        B, N, D = (2, 256, 128)
        H, HD = (16, 64)
        E, DD = (8, 512)
        EPS = 1e-05

        def _ln(x, g, b):
            m = jnp.mean(x, axis=-1, keepdims=True)
            v = jnp.var(x, axis=-1, keepdims=True)
            return (x - m) * jax.lax.rsqrt(v + EPS) * g + b
        key = jax.random.key(seed)
        ks = jax.random.split(key, 16)
        s = 0.02
        return {'x': jax.random.normal(ks[0], (B, N, D), jnp.float32), 't': jax.random.normal(ks[1], (B, 1, D), jnp.float32), 'W_ada': jax.random.normal(ks[2], (D, D), jnp.float32) * s, 'b_ada': jnp.zeros((D,), jnp.float32), 'ln1_g': jnp.ones((D,), jnp.float32), 'ln1_b': jnp.zeros((D,), jnp.float32), 'Wqkv': jax.random.normal(ks[3], (3 * H * HD, D), jnp.float32) * s, 'qn_g': jnp.ones((HD,), jnp.float32), 'qn_b': jnp.zeros((HD,), jnp.float32), 'kn_g': jnp.ones((HD,), jnp.float32), 'kn_b': jnp.zeros((HD,), jnp.float32), 'Wout': jax.random.normal(ks[4], (D, H * HD), jnp.float32) * s, 'mlp_g': jnp.ones((D,), jnp.float32), 'mlp_b': jnp.zeros((D,), jnp.float32), 'Wgate': jax.random.normal(ks[5], (E, D), jnp.float32) * s, 'fc1s': jax.random.normal(ks[6], (E, DD, D), jnp.float32) * s, 'b1s': jnp.zeros((E, DD), jnp.float32), 'fc2s': jax.random.normal(ks[7], (E, D, DD), jnp.float32) * s, 'b2s': jnp.zeros((E, D), jnp.float32)}
    _L3_cond_all = _L3_cond_setup()
    _L3_cond_in = {k: v for k, v in _L3_cond_all.items() if k in ('W_ada', 'b_ada', 'ln1_g', 'ln1_b', 'Wqkv', 'qn_g', 'qn_b', 'kn_g', 'kn_b', 'Wout', 'mlp_g', 'mlp_b', 'Wgate', 'fc1s', 'b1s', 'fc2s', 'b2s')}
    del _L3_cond_all
    return {'x': x, 'cond_1024': cond_1024, 'mask_BxS_bf0': mask_BxS_bf0, 'mask_BxSxSx11_ik0': mask_BxSxSx11_ik0, 'L0_cond_ln_g': _L0_cond_in['ln_g'], 'L0_cond_ln_b': _L0_cond_in['ln_b'], 'L0_cond_Wg': _L0_cond_in['Wg'], 'L0_cond_bg': _L0_cond_in['bg'], 'L0_cond_Wb': _L0_cond_in['Wb'], 'L0_cond_bb': _L0_cond_in['bb'], 'L0_cond_Wqkv': _L0_cond_in['Wqkv'], 'L0_cond_bqkv': _L0_cond_in['bqkv'], 'L0_cond_Wp': _L0_cond_in['Wp'], 'L0_cond_bp': _L0_cond_in['bp'], 'L0_cond_W1': _L0_cond_in['W1'], 'L0_cond_b1': _L0_cond_in['b1'], 'L0_cond_W2': _L0_cond_in['W2'], 'L0_cond_b2': _L0_cond_in['b2'], 'L1_cond_w_adaln1': _L1_cond_in['w_adaln1'], 'L1_cond_b_adaln1': _L1_cond_in['b_adaln1'], 'L1_cond_w_adaln2': _L1_cond_in['w_adaln2'], 'L1_cond_b_adaln2': _L1_cond_in['b_adaln2'], 'L1_cond_wq': _L1_cond_in['wq'], 'L1_cond_bq': _L1_cond_in['bq'], 'L1_cond_wk': _L1_cond_in['wk'], 'L1_cond_bk': _L1_cond_in['bk'], 'L1_cond_wv': _L1_cond_in['wv'], 'L1_cond_bv': _L1_cond_in['bv'], 'L1_cond_wo': _L1_cond_in['wo'], 'L1_cond_bo': _L1_cond_in['bo'], 'L1_cond_w1': _L1_cond_in['w1'], 'L1_cond_b1': _L1_cond_in['b1'], 'L1_cond_w2': _L1_cond_in['w2'], 'L1_cond_b2': _L1_cond_in['b2'], 'L2_cond_W_self': _L2_cond_in['W_self'], 'L2_cond_b_self': _L2_cond_in['b_self'], 'L2_cond_w_bias': _L2_cond_in['w_bias'], 'L2_cond_b_bias': _L2_cond_in['b_bias'], 'L2_cond_Wq': _L2_cond_in['Wq'], 'L2_cond_bq': _L2_cond_in['bq'], 'L2_cond_Wk': _L2_cond_in['Wk'], 'L2_cond_bk': _L2_cond_in['bk'], 'L2_cond_Wout': _L2_cond_in['Wout'], 'L2_cond_bout': _L2_cond_in['bout'], 'L3_cond_W_ada': _L3_cond_in['W_ada'], 'L3_cond_b_ada': _L3_cond_in['b_ada'], 'L3_cond_ln1_g': _L3_cond_in['ln1_g'], 'L3_cond_ln1_b': _L3_cond_in['ln1_b'], 'L3_cond_Wqkv': _L3_cond_in['Wqkv'], 'L3_cond_qn_g': _L3_cond_in['qn_g'], 'L3_cond_qn_b': _L3_cond_in['qn_b'], 'L3_cond_kn_g': _L3_cond_in['kn_g'], 'L3_cond_kn_b': _L3_cond_in['kn_b'], 'L3_cond_Wout': _L3_cond_in['Wout'], 'L3_cond_mlp_g': _L3_cond_in['mlp_g'], 'L3_cond_mlp_b': _L3_cond_in['mlp_b'], 'L3_cond_Wgate': _L3_cond_in['Wgate'], 'L3_cond_fc1s': _L3_cond_in['fc1s'], 'L3_cond_b1s': _L3_cond_in['b1s'], 'L3_cond_fc2s': _L3_cond_in['fc2s'], 'L3_cond_b2s': _L3_cond_in['b2s']}

def reference(x, cond_1024, mask_BxS_bf0, mask_BxSxSx11_ik0, L0_cond_ln_g, L0_cond_ln_b, L0_cond_Wg, L0_cond_bg, L0_cond_Wb, L0_cond_bb, L0_cond_Wqkv, L0_cond_bqkv, L0_cond_Wp, L0_cond_bp, L0_cond_W1, L0_cond_b1, L0_cond_W2, L0_cond_b2, L1_cond_w_adaln1, L1_cond_b_adaln1, L1_cond_w_adaln2, L1_cond_b_adaln2, L1_cond_wq, L1_cond_bq, L1_cond_wk, L1_cond_bk, L1_cond_wv, L1_cond_bv, L1_cond_wo, L1_cond_bo, L1_cond_w1, L1_cond_b1, L1_cond_w2, L1_cond_b2, L2_cond_W_self, L2_cond_b_self, L2_cond_w_bias, L2_cond_b_bias, L2_cond_Wq, L2_cond_bq, L2_cond_Wk, L2_cond_bk, L2_cond_Wout, L2_cond_bout, L3_cond_W_ada, L3_cond_b_ada, L3_cond_ln1_g, L3_cond_ln1_b, L3_cond_Wqkv, L3_cond_qn_g, L3_cond_qn_b, L3_cond_kn_g, L3_cond_kn_b, L3_cond_Wout, L3_cond_mlp_g, L3_cond_mlp_b, L3_cond_Wgate, L3_cond_fc1s, L3_cond_b1s, L3_cond_fc2s, L3_cond_b2s):
    import jax
    import jax.numpy as jnp

    def _L0_cond_ref(hidden, w, ln_g, ln_b, Wg, bg, Wb, bb, Wqkv, bqkv, Wp, bp, W1, b1, W2, b2, num_heads):
        import jax, jax.numpy as jnp
        import numpy as np
        EPS = 1e-05

        def _sln(h, w, ln_g, ln_b, Wg, bg, Wb, bb):
            mu = jnp.mean(h, axis=-1, keepdims=True)
            var = jnp.mean((h - mu) ** 2, axis=-1, keepdims=True)
            ln = (h - mu) / jnp.sqrt(var + EPS) * ln_g + ln_b
            gamma = (w @ Wg.T + bg)[:, None, :]
            beta = (w @ Wb.T + bb)[:, None, :]
            return gamma * ln + beta
        B, N, D = hidden.shape
        hd = D // num_heads
        h = _sln(hidden, w, ln_g, ln_b, Wg, bg, Wb, bb)
        qkv = (h @ Wqkv.T + bqkv).reshape(B, N, num_heads, hd, 3)
        q = jnp.moveaxis(qkv[..., 0], 2, 1)
        k = jnp.moveaxis(qkv[..., 1], 2, 1)
        v = jnp.moveaxis(qkv[..., 2], 2, 1)
        energy = jnp.einsum('bhqd,bhkd->bhqk', q, k)
        att = jax.nn.softmax(energy, axis=-1) / D ** 0.5
        out = jnp.einsum('bhqk,bhkd->bhqd', att, v)
        out = jnp.moveaxis(out, 1, 2).reshape(B, N, D)
        out = out @ Wp.T + bp
        h1 = out + hidden
        h2 = _sln(h1, w, ln_g, ln_b, Wg, bg, Wb, bb)
        return h2 + h1

    def _L1_cond_ref(x, cond, key_padding_mask, w_adaln1, b_adaln1, w_adaln2, b_adaln2, wq, bq, wk, bk, wv, bv, wo, bo, w1, b1, w2, b2):
        import math
        import jax, jax.numpy as jnp
        import numpy as np
        H = 128
        NH = 16
        HD = H // NH
        CD = 128
        MLP = 512
        EPS = 1e-05

        def _layernorm(x):
            mu = jnp.mean(x, axis=-1, keepdims=True)
            var = jnp.var(x, axis=-1, keepdims=True)
            return (x - mu) * jax.lax.rsqrt(var + EPS)

        def _adaln(x, cond, W, b):
            ss = cond @ W.T + b
            scale, shift = jnp.split(ss, 2, axis=-1)
            return _layernorm(x) * (1.0 + scale[:, None, :]) + shift[:, None, :]
        B, L, D = x.shape
        normed = _adaln(x, cond, w_adaln1, b_adaln1)
        q = (normed @ wq.T + bq).reshape(B, L, NH, HD)
        k = (normed @ wk.T + bk).reshape(B, L, NH, HD)
        v = (normed @ wv.T + bv).reshape(B, L, NH, HD)
        scale = math.sqrt(HD)
        scores = jnp.einsum('blhd,bmhd->bhlm', q, k) / scale
        scores = jnp.where(key_padding_mask[:, None, None, :], -jnp.inf, scores)
        attn = jax.nn.softmax(scores, axis=-1)
        attn_out = jnp.einsum('bhlm,bmhd->blhd', attn, v).reshape(B, L, D)
        x = x + attn_out @ wo.T + bo
        normed = _adaln(x, cond, w_adaln2, b_adaln2)
        h = jax.nn.gelu(normed @ w1.T + b1, approximate=False)
        x = x + h @ w2.T + b2
        return x

    def _L2_cond_ref(v, q, adj, W_self, b_self, w_bias, b_bias, Wq, bq, Wk, bk, Wout, bout):
        import jax, jax.numpy as jnp
        import numpy as np
        NONGT = 20
        H = 16
        NEG = -9000000000000000.0

        def _gat_attention(self_feat, cond_adj, label_bias, Wq, bq, Wk, bk, Wout, bout):
            B, N, F = self_feat.shape
            ng = min(NONGT, N)
            dh = F // H
            kv = self_feat[:, :ng]
            qh = (self_feat @ Wq.T + bq).reshape(B, N, H, dh)
            kh = (kv @ Wk.T + bk).reshape(B, ng, H, dh)
            aff = jnp.einsum('bnhd,bmhd->bnhm', qh, kh) * (1.0 / np.sqrt(dh))
            mask = cond_adj[:, :, None, :] > 0
            aff = jnp.where(mask, aff, NEG) + label_bias[:, :, None, :]
            w = jax.nn.softmax(aff, axis=-1)
            out_t = jnp.einsum('bnhm,bmf->bnhf', w, kv)
            out = jnp.einsum('bnhf,hgf->bnhg', out_t, Wout) + bout.reshape(H, F // H)
            return out.reshape(B, N, F)

        def _forward(v, q, adj, W_self, b_self, w_bias, b_bias, Wq, bq, Wk, bk, Wout, bout):
            adj_f = adj.astype(jnp.float32)
            exp_v = v
            row_zero = exp_v.sum(-1) == 0
            q_exp = jnp.where(row_zero[..., None], 0.0, q[:, None, :])
            vcq = jnp.concatenate([exp_v, q_exp], axis=-1)
            self_feat = vcq @ W_self.T + b_self
            output = self_feat
            for d in range(2):
                A = adj_f if d == 0 else jnp.swapaxes(adj_f, 1, 2)
                A = A[:, :, :NONGT, :]
                cond = A.sum(-1)
                vb = A @ w_bias + b_bias
                output = output + _gat_attention(self_feat, cond, vb, Wq[d], bq[d], Wk[d], bk[d], Wout[d], bout[d])
            rel = jax.nn.relu(output)
            return exp_v + rel
        return _forward(v, q, adj, W_self, b_self, w_bias, b_bias, Wq, bq, Wk, bk, Wout, bout)

    def _L3_cond_ref(x, t, W_ada, b_ada, ln1_g, ln1_b, Wqkv, qn_g, qn_b, kn_g, kn_b, Wout, mlp_g, mlp_b, Wgate, fc1s, b1s, fc2s, b2s):
        import jax, jax.numpy as jnp
        import numpy as np
        B, N, D = (2, 256, 128)
        H, HD = (16, 64)
        E, DD = (8, 512)
        EPS = 1e-05

        def _ln(x, g, b):
            m = jnp.mean(x, axis=-1, keepdims=True)
            v = jnp.var(x, axis=-1, keepdims=True)
            return (x - m) * jax.lax.rsqrt(v + EPS) * g + b
        b, n, d = x.shape
        shift = jax.nn.silu(t) @ W_ada.T + b_ada
        h = _ln(x, ln1_g, ln1_b) + shift
        qkv = (h @ Wqkv.T).reshape(b, n, 3, H, HD)
        q = _ln(qkv[:, :, 0].transpose(0, 2, 1, 3), qn_g, qn_b)
        k = _ln(qkv[:, :, 1].transpose(0, 2, 1, 3), kn_g, kn_b)
        v = qkv[:, :, 2].transpose(0, 2, 1, 3)
        scores = jnp.einsum('bhnd,bhmd->bhnm', q, k) / jnp.sqrt(jnp.float32(HD))
        attn = jax.nn.softmax(scores, axis=-1)
        o = jnp.einsum('bhnm,bhmd->bhnd', attn, v)
        o = o.transpose(0, 2, 1, 3).reshape(b, n, H * HD)
        x = x + o @ Wout.T
        tok = x.reshape(-1, d)
        bs = tok.shape[0]
        gate = jax.nn.softmax(tok @ Wgate.T, axis=-1)
        k_cap = bs // E
        vals, idx = jax.lax.top_k(gate.T, k_cap)
        idx_flat = idx.T.reshape(-1)
        w = vals.T
        g = _ln(tok[idx_flat], mlp_g, mlp_b).reshape(k_cap, E, d)
        y = jnp.einsum('ked,ehd->keh', g, fc1s) + b1s
        y = jax.nn.gelu(y, approximate=True)
        y = jnp.einsum('keh,edh->ked', y, fc2s) + b2s
        y = y * w[..., None]
        tok = tok.at[idx_flat].add(y.reshape(-1, d))
        return tok.reshape(x.shape)
    x = _L0_cond_ref(x, cond_1024, L0_cond_ln_g, L0_cond_ln_b, L0_cond_Wg, L0_cond_bg, L0_cond_Wb, L0_cond_bb, L0_cond_Wqkv, L0_cond_bqkv, L0_cond_Wp, L0_cond_bp, L0_cond_W1, L0_cond_b1, L0_cond_W2, L0_cond_b2, 16)
    x = _L1_cond_ref(x, cond_1024, mask_BxS_bf0, L1_cond_w_adaln1, L1_cond_b_adaln1, L1_cond_w_adaln2, L1_cond_b_adaln2, L1_cond_wq, L1_cond_bq, L1_cond_wk, L1_cond_bk, L1_cond_wv, L1_cond_bv, L1_cond_wo, L1_cond_bo, L1_cond_w1, L1_cond_b1, L1_cond_w2, L1_cond_b2)
    x = _L2_cond_ref(x, cond_1024, mask_BxSxSx11_ik0, L2_cond_W_self, L2_cond_b_self, L2_cond_w_bias, L2_cond_b_bias, L2_cond_Wq, L2_cond_bq, L2_cond_Wk, L2_cond_bk, L2_cond_Wout, L2_cond_bout)
    x = _L3_cond_ref(x, cond_1024[:, None, :], L3_cond_W_ada, L3_cond_b_ada, L3_cond_ln1_g, L3_cond_ln1_b, L3_cond_Wqkv, L3_cond_qn_g, L3_cond_qn_b, L3_cond_kn_g, L3_cond_kn_b, L3_cond_Wout, L3_cond_mlp_g, L3_cond_mlp_b, L3_cond_Wgate, L3_cond_fc1s, L3_cond_b1s, L3_cond_fc2s, L3_cond_b2s)
    return x

_drawn_inputs = setup_inputs


def setup_inputs(seed=0):
    import zlib

    import numpy as np

    out = dict(_drawn_inputs(seed))
    spreads = {'L0_cond_ln_g': (1.0, 0.2),
     'L0_cond_ln_b': (0.0, 0.1),
     'L0_cond_bg': (0.0, 0.1),
     'L0_cond_bb': (0.0, 0.1),
     'L0_cond_bqkv': (0.0, 0.8),
     'L0_cond_bp': (0.0, 0.1),
     'L0_cond_b1': (0.0, 0.1),
     'L0_cond_b2': (0.0, 0.1),
     'L1_cond_b_adaln1': (0.0, 0.8),
     'L1_cond_b_adaln2': (0.0, 0.8),
     'L1_cond_bq': (0.0, 0.8),
     'L1_cond_bk': (0.0, 0.8),
     'L1_cond_bv': (0.0, 0.647),
     'L1_cond_bo': (0.0, 0.1),
     'L1_cond_b1': (0.0, 0.573),
     'L1_cond_b2': (0.0, 0.1),
     'L2_cond_b_self': (0.0, 0.1),
     'L2_cond_bq': (0.0, 0.1),
     'L2_cond_bk': (0.0, 0.1),
     'L2_cond_bout': (0.0, 0.1),
     'L3_cond_b_ada': (0.0, 0.8),
     'L3_cond_ln1_g': (1.0, 0.6),
     'L3_cond_ln1_b': (0.0, 0.8),
     'L3_cond_qn_g': (1.0, 0.6),
     'L3_cond_qn_b': (0.0, 0.8),
     'L3_cond_kn_g': (1.0, 0.6),
     'L3_cond_kn_b': (0.0, 0.8),
     'L3_cond_mlp_g': (1.0, 0.6),
     'L3_cond_mlp_b': (0.0, 0.8),
     'L3_cond_b1s': (0.0, 0.8),
     'L3_cond_b2s': (0.0, 0.65)}
    factors = {'L1_cond_w_adaln1': 7.288,
     'L1_cond_w_adaln2': 5.167,
     'L1_cond_wq': 8.0,
     'L1_cond_wk': 8.0,
     'L1_cond_wv': 2.948,
     'L3_cond_W_ada': 4.976,
     'L3_cond_Wgate': 4.189,
     'L3_cond_fc1s': 8.0,
     'L3_cond_fc2s': 7.546}
    for name, (base, spread) in spreads.items():
        noise = np.random.default_rng([zlib.crc32(name.encode()), seed]).standard_normal(out[name].shape)
        drawn = base * np.exp(spread * noise) if base else spread * noise
        out[name] = jnp.asarray(drawn.astype(out[name].dtype))
    for name, factor in factors.items():
        out[name] = (out[name] * factor).astype(out[name].dtype)
    return out
```

```python
from contextlib import ExitStack
from itertools import count

import numpy as np
import concourse.bass as bass
from concourse import mybir

ALU = mybir.AluOpType
ACT = mybir.ActivationFunctionType
AX = mybir.AxisListType.X
F32 = mybir.dt.float32
BF16 = mybir.dt.bfloat16
I32 = mybir.dt.int32
U8 = mybir.dt.uint8

B, S, D, NH = 32, 32, 128, 16
P = 128
TOK = B * S
NT = TOK // P
BPT = P // S
HD = D // NH
NG = 4
NC = NH // NG
HT = TOK // 2
UT = 2 * P
NK2 = 20
NL = 11
HID = 512
NCH = HID // P
HD3 = 64
NE = 8
CAP = TOK // NE
EPS = 1e-5
NEG = -9000000000000000.0
BIG = 3.0e38

W_PARTS = [
    ("condT", B), ("l0_wg", D), ("l0_wb", D), ("l1_ad1", 2 * D), ("l1_ad2", 2 * D), ("l3_ada", D),
    ("l0_wq", D), ("l0_wk", D), ("l0_wv", D), ("l0_wp", D),
    ("l1_wq", D), ("l1_wk", D), ("l1_wv", D), ("l1_wo", D), ("l1_w1", HID), ("l1_w2", HID),
    ("l2_ws1", D), ("l2_ws2", D),
    ("l2_wq0", D), ("l2_wk0", D), ("l2_wv0", D), ("l2_wq1", D), ("l2_wk1", D), ("l2_wv1", D),
    ("l3_wqkv", 3 * NH * HD3), ("l3_wout", NH * HD3), ("l3_gate", NE), ("fc1", NE * HID), ("fc2", NE * HID),
]
C_PARTS = [
    ("ln_g", 1), ("ln_b", 1), ("bg", 1), ("bb", 1), ("bq0", 1), ("bk0", 1), ("bv0", 1),
    ("ad1", 2), ("ad2", 2), ("bq1", 1), ("bk1", 1), ("bv1", 1), ("b1", NCH),
    ("bself", 1), ("bq2", 1), ("bq3", 1), ("bk2", 1), ("bk3", 1), ("bo2", 1), ("bo3", 1),
    ("b_ada", 1), ("ln1_g", 1), ("ln1_b", 1), ("qn_g", 1), ("qn_b", 1), ("kn_g", 1), ("kn_b", 1),
    ("mlp_g", 1), ("mlp_b", 1), ("b1s", NE * NCH),
]
R_PARTS = [("bp", D), ("bo", D), ("b2", D), ("w_bias", NL), ("b_bias", 1), ("b2s", NE * D)]
K_PARTS = [("ident", P), ("head_mask", NC), ("iota_row", P), ("iota_col", 1), ("group16", P), ("mhalf", 32)]
KB_PARTS = [("ident", P), ("before", P), ("ones", P)]


def offsets(parts):
    at, out = 0, {}
    for name, n in parts:
        out[name] = (at, n)
        at += n
    return out, at


W_AT, W_N = offsets(W_PARTS)
C_AT, C_N = offsets(C_PARTS)
R_AT, R_N = offsets(R_PARTS)
K_AT, K_N = offsets(K_PARTS)
KB_AT, KB_N = offsets(KB_PARTS)
SHIFTS = [28, 24, 20, 16, 12, 8, 4, 0]
ROUNDS = len(SHIFTS)

UNITS = [(0, u) for u in range(4)] + [(1, u) for u in range(4)] + [(d, u) for u in range(4) for d in (2, 3)]
UNIT_AT = {cu: i for i, cu in enumerate(UNITS)}
NUNIT = len(UNITS)


def steps():
    out = [("setup",)]

    def add(*names_and_args):
        out.extend(names_and_args)

    def norm(l, h):
        add(("stats", l, h), ("norm", l, h))

    for h in range(2):
        norm(0, h)
    for h in range(2):
        add(("modulate", 0, h), ("project", 0, h))
    add(("tokmod",), ("edges",))

    def unit(U, between=()):
        if U < NUNIT:
            add(("scores", U))
        if U >= 1:
            add(("sum", U - 1), ("turn", U - 1))
        if U >= 2:
            add(("out", U - 2))
        if U >= 1:
            add(("weigh", U - 1))

    for U in range(4):
        unit(U)
        if U == 3:
            norm(1, 0)
            add(("remod", 0))
            norm(2, 0)
    add(("sum", 3), ("turn", 3), ("out", 2), ("modulate", 1, 0), ("weigh", 3), ("project", 1, 0), ("out", 3))
    norm(1, 1)
    add(("scores", 4), ("remod", 1))
    norm(2, 1)
    add(("modulate", 1, 1), ("scores", 5), ("sum", 4), ("turn", 4), ("project", 1, 1), ("weigh", 4))
    for U in (6, 7):
        add(("scores", U), ("sum", U - 1), ("turn", U - 1), ("out", U - 2), ("weigh", U - 1))
    norm(3, 0)
    add(("sum", 7), ("turn", 7), ("out", 6), ("modulate", 2, 0), ("weigh", 7), ("center",), ("up", 0), ("out", 7))
    norm(3, 1)
    add(("down", 0), ("nodes", 0), ("modulate", 2, 1), ("up", 1), ("self", 0), ("down", 1), ("project", 2, 0),
        ("project", 3, 0), ("nodes", 1))
    add(("scores", 8), ("self", 1), ("scores", 9), ("sum", 8), ("turn", 8), ("project", 2, 1), ("weigh", 8),
        ("project", 3, 1))
    for U in range(10, 16):
        add(("scores", U), ("sum", U - 1), ("turn", U - 1), ("weigh", U - 1))
        if U == 12:
            add(("back", 0))
            norm(4, 0)
        if U == 13:
            add(("modulate3", 0))
    add(("sum", 15), ("turn", 15), ("weigh", 15), ("back", 1), ("qkv3", 0))
    norm(4, 1)
    add(("modulate3", 1), ("qkT3", 0))
    for t in range(NT):
        add(("scores3", t), ("sum", NUNIT + t))
        if t + 1 < NT:
            add(("qkv3", t + 1))
        add(("weigh3", t))
        if t + 1 < NT:
            add(("qkT3", t + 1))
        add(("out3", t))
        if t == 4:
            norm(5, 0)
            add(("tokT", 0))
    norm(5, 1)
    add(("tokT", 1), ("split", 0), ("split", 1), ("route",), ("experts",))
    return out


STEPS = steps()


def occurrences():
    seen, out = {}, {}
    for s in STEPS:
        out[s] = seen.get(s[0], 0)
        seen[s[0]] = out[s] + 1
    return out


NTH = occurrences()


def conditional_blocks(nc, x_d, w_d, c_d, r_d, k_d, kb_d, ki_d, mask_d, adj_d, out_d):
    with ExitStack() as ctx:
        def sb(name, shape, dt=F32):
            return ctx.enter_context(nc.sbuf_tensor(name, shape, dt))

        def psum(name, shape, dt=F32):
            return ctx.enter_context(nc.psum_tensor(name, shape, dt))

        class Signal:

            def __init__(self, name, per=1):
                self.sem = ctx.enter_context(nc.semaphore(name))
                self.per = per

            def after(self, item=0, part=None):
                return self.per * item + (self.per if part is None else part)

        W = sb("W", [P, W_N])
        COL = sb("COL", [P, C_N])
        ROW = sb("ROW", [P, R_N])
        K = sb("K", [P, K_N])
        KB = sb("KB", [P, KB_N], BF16)
        KI = sb("KI", [P, ROUNDS], I32)
        PADM = sb("PADM", [P, NT, S], U8)
        X = sb("X", [P, NT, D])
        XB = sb("XB", [P, NT, D])
        XN = sb("XN", [P, NT, D])
        HTb = sb("HTb", [P, TOK])
        QT = sb("QT", [P, 2, TOK])
        REG = sb("REG", [P, 16384])
        PR = sb("PR", [P, 3, NG, 2 * NC, S])
        PTS = sb("PTS", [P, 2, 2, NG, P])
        OT = sb("OT", [P, 2, UT])
        TM = sb("TM", [P, 2, TOK])
        ACC = sb("ACC", [P, TOK])
        PAD = sb("PAD", [P, NT, S])
        EM = sb("EM", [P, 2, NT, S])
        EB = sb("EB", [P, 2, NT, S])
        CM = sb("CM", [P, 7, B])
        CS = sb("CS", [P, 3, B])
        KM = sb("KM", [P, 4, NC])
        SC = sb("SC", [P, 8])
        ST = sb("ST", [P, 2, 4, 6])
        MV = sb("MV", [P, 2, 4, 2])
        RSTD = sb("RSTD", [P, 2, 2, 4])
        MX = sb("MX", [P, 2, 2 * NH])
        SM = sb("SM", [P, 2, 2 * NH])
        RS = sb("RS", [P, 2, 2 * NH])
        NZ = sb("NZ", [P, 2, 2, 4])
        SS3 = sb("SS3", [P, 2, 3, 8])
        WS = sb("WS", [P, 2 * NH])

        Sps = psum("Sps", [P, NG, 512])
        RB = [psum(f"RB{i}", [P, 512]) for i in range(4)]

        KBLK = [REG[:, 4096 * i:4096 * (i + 1)].rearrange("p (c t) -> p c t", c=NC) for i in (0, 2)]
        VBLK = [REG[:, 4096 * i:4096 * (i + 1)].rearrange("p (b g c f) -> p b g c f", g=NG, c=NC, f=HD)
                for i in (1, 3)]
        ADJ = REG[:, 8192:8192 + NT * S * NL].bitcast(I32).rearrange("p (t m l) -> p t m l", m=S, l=NL)
        ADW = REG[:, 8192 + NT * S * NL:8192 + 2 * NT * S * NL].rearrange("p (t m l) -> p t m l", m=S, l=NL)
        HIDb = REG[:, 8192:8192 + NCH * TOK].rearrange("p (c t) -> p c t", c=NCH)
        QK3 = REG[:, 0:4096].rearrange("p (b k c t) -> p b k c t", b=2, k=2, c=8)
        PBD = REG[:, 4096:8192].rearrange("p (b h t) -> p b h t", b=2, h=NH)
        V3 = REG[:, 8192:10240].rearrange("p (b f) -> p b f", b=2)
        OT3 = REG[:, 10240:12288].rearrange("p (b c t) -> p b c t", b=2, c=8)
        QN3 = REG[:, 12288:14336].rearrange("p (i f) -> p i f", i=4)
        SQ3 = REG[:, 14336:15360].rearrange("p (i f) -> p i f", i=2)
        PIC = REG[:, 0:4096].bitcast(BF16).rearrange("p (t s) -> p t s", t=NT)
        PICT = REG[:, 4096:8192].bitcast(BF16).rearrange("p (e t) -> p e t", e=NE)
        XSP = REG[:, 8192:9728].bitcast(BF16).rearrange("p (t k f) -> p t k f", t=NT, k=3)
        YSP = REG[:, 9728:11264].bitcast(BF16).rearrange("p (e k f) -> p e k f", e=NE, k=3)
        GTT = REG[:, 11264:12288]
        HE = REG[:, 12288:13312].rearrange("p (b c s) -> p b c s", b=2, c=NCH)
        GBC = REG[:, 13312:14336]
        JUNK = REG[:, 14336:15360]
        RES = REG[:, 15360:16384].rearrange("p (t f) -> p t f", t=NT)
        TOKT = XB[:, :, :].rearrange("p t f -> p (t f)")

        RG = sb("RG", [P, 12, NT * NE])
        RGB = sb("RGB", [P, 6, NT * NE], BF16)
        RT = sb("RT", [P, 16])
        RTI = sb("RTI", [P, 4], I32)
        YB = sb("YB", [P, 2, 2, D])

        def w(name, a=0, n=None):
            o, size = W_AT[name]
            return W[:, o + a:o + a + (size - a if n is None else n)]

        def col(name, i=0):
            return COL[:, C_AT[name][0] + i:C_AT[name][0] + i + 1]

        def row(name, a=0, n=None):
            o, size = R_AT[name]
            return ROW[:, o + a:o + a + (size - a if n is None else n)]

        def konst(name):
            o, size = K_AT[name]
            return K[:, o:o + size]

        def konst_b(name):
            o, size = KB_AT[name]
            return KB[:, o:o + size]

        def spread(ap, n):
            return ap.unsqueeze(2).broadcast_to([ap.shape[0], ap.shape[1], n])

        def stack(ap, n):
            return ap.unsqueeze(1).broadcast_to([ap.shape[0], n, ap.shape[1]])

        ident = konst("ident")

        def half(h):
            return slice(HT * h, HT * (h + 1))

        def tiles(h):
            return slice(4 * h, 4 * h + 4)

        n_first = 7
        load_first = Signal("load_first", 16 * n_first)
        load_x = Signal("load_x", 16)
        load_l0 = Signal("load_l0", 16)
        load_adj = Signal("load_adj", 16)
        load_l1 = Signal("load_l1", 16)
        load_l2 = Signal("load_l2", 16)
        load_l3 = Signal("load_l3", 16)
        load_fc = Signal("load_fc", 16)
        stored = Signal("stored", 32)
        silu_e = Signal("silu_exp")
        silu = Signal("silu", 3)
        cols_r = Signal("scaled_columns", 10)
        cond_r = Signal("modulation", 8)
        ada_r = Signal("shift3")
        tok_r = Signal("token_modulation")
        stats = Signal("stats", 8)
        rstd = Signal("rstd", 2)
        xb_r = Signal("residual_and_bias")
        normed = Signal("normed", 4)
        modul = Signal("modulated", 2)
        q_r = Signal("q_ready")
        k_r = Signal("kblk_ready", 4)
        v_r = Signal("vblk_ready", 4)
        vz = Signal("vblk_zero")
        prz = Signal("key_padding_zero")
        s_made = Signal("scores_made")
        masked = Signal("scores_masked", 2)
        biased = Signal("scores_biased", 2)
        smax = Signal("score_max")
        ssub = Signal("scores_less_max")
        expd = Signal("exp_done")
        ssum = Signal("exp_sum", 2)
        prob = Signal("probabilities")
        pt_r = Signal("probs_transposed")
        o_r = Signal("attention_out")
        x_r = Signal("residual_attention")
        tg_r = Signal("token_gamma")
        xg_r = Signal("residual_remodulated")
        gelu = Signal("hidden")
        xm_r = Signal("residual_mlp")
        nz_r = Signal("nonzero_rows", 2)
        xT_r = Signal("xT_ready")
        qe_r = Signal("q_masked")
        self_r = Signal("self_feat")
        acc_r = Signal("direction_added")
        rel_r = Signal("relu_added")
        xk_r = Signal("residual_graph")
        edge = Signal("edge_steps")
        edge_w = Signal("edge_weights")
        wsum = Signal("weight_means", 2)
        wc_r = Signal("centered_weights", 2)
        h3_r = Signal("modulated3")
        sq_r = Signal("squares3")
        ss_r = Signal("square_sums3")
        r3_r = Signal("rstd3", 2)
        qn_r = Signal("normed3")
        qk_r = Signal("qkT3_ready")
        v3_r = Signal("v3_ready")
        pbz = Signal("prob_blocks_zero")
        pb_r = Signal("prob_blocks", 4)
        o3_r = Signal("attention_out3")
        x3_r = Signal("residual3")
        tt_r = Signal("tokT_ready")
        rt = Signal("routing_vector")
        rta = Signal("routing_scalar")
        gb_r = Signal("gates_spread")
        cnt = Signal("counts_summed")
        pic_v = Signal("picks_vector")
        pict_r = Signal("picksT")
        xs_a = Signal("split_scalar", 2)
        xs_v = Signal("split_vector", 2)
        gt_r = Signal("gathered")
        he_r = Signal("expert_hidden", NCH)
        y_r = Signal("expert_out", 6)
        res_r = Signal("result")

        RT_LOGIT = 2
        RT_GATE = 5
        RT_ROUND = [RT_GATE + 2 + 5 * k for k in range(ROUNDS + 1)]
        RT_EQ = RT_ROUND[ROUNDS] + 2
        RT_NEED = RT_EQ + 1
        RT_PREFIX = RT_EQ + 6
        RT_POS = RT_EQ + 9
        RT_SPLIT = RT_POS + 4
        RT_WEIGHT = RT_SPLIT + 1

        TAKEN = {
            "cond": (cond_r, lambda i: 7), "ada": (ada_r, lambda i: 1), "tokmod": (tok_r, None),
            "xnT": (modul, lambda i: 2 * i + 1), "xnT3": (h3_r, None), "q": (q_r, None), "k": (k_r, None),
            "v": (v_r, None), "pt": (pt_r, None), "o": (o_r, None), "o2": (acc_r, None), "y": (x_r, None),
            "up": (gelu, None), "down": (xm_r, None), "xT": (xT_r, None), "nz": (qe_r, None), "self": (self_r, None),
            "back": (xk_r, None), "qk3": (qn_r, None), "v3": (v3_r, None), "qkT3": (qk_r, None),
            "o3": (o3_r, None), "y3": (x3_r, None), "tokT": (tt_r, None),
            "logit": (rt, lambda i: RT_LOGIT), "gates": (gb_r, None), "thr": (rt, lambda i: RT_EQ),
            "prefix": (rt, lambda i: RT_PREFIX), "total": (rt, lambda i: RT_NEED), "posT": (pict_r, None),
            "gather": (gt_r, None), "weight": (rt, lambda i: RT_WEIGHT), "fc1": (he_r, None),
            "fc2": (y_r, lambda i: 6 * i + 1), "scatter": (res_r, None),
        }
        made = Signal("bank_made")

        PRODUCTS = {
            "setup": ["cond", "ada"], "modulate": ["xnT"], "modulate3": ["xnT3"], "project": ["q", "k", "v"],
            "tokmod": ["tokmod"] * 4, "turn": ["pt"] * 2, "up": ["up"] * NCH, "down": ["down"],
            "nodes": ["xT", "nz"], "self": ["self"], "back": ["back"], "qkv3": ["qk3"] * 4 + ["v3"] * 2,
            "qkT3": ["qkT3"] * 4, "weigh3": ["o3"] * 2, "out": ["y"], "out3": ["y3"], "tokT": ["tokT"],
            "route": ["logit", "gates", "gates", "thr", "prefix", "total"],
        }
        RING_ORDER = []
        for s in STEPS:
            if s[0] == "weigh":
                kinds = ["o" if UNITS[s[1]][0] < 2 else "o2"]
            elif s[0] == "experts":
                kinds = ["posT"] * 4 + ["gather"] * 2 + ["weight"]
                for e in range(NE + 1):
                    kinds += ["fc1"] * (e < NE) + ["posT"] * (3 * (e % 2)) + ["fc2"] * (e > 0)
                kinds += ["scatter"] * 2
            else:
                kinds = PRODUCTS.get(s[0], [])
            for kind in kinds:
                RING_ORDER.append((kind, sum(k == kind for k, _ in RING_ORDER)))
        RING_AT = {key: n for n, key in enumerate(RING_ORDER)}

        def bank(kind, item=0):
            return RB[RING_AT[kind, item] % len(RB)]

        def count_made(kind, item=0):
            return RING_AT[kind, item] + 1

        def used_before(kind, item=0):
            return RING_AT[kind, item] >= len(RB)

        def last_read(kind, item=0):
            before, i = RING_ORDER[RING_AT[kind, item] - len(RB)]
            signal, value = TAKEN[before]
            return signal.sem, value(i) if value else signal.after(i)

        block = ctx.enter_context(nc.Block())

        @block.sync
        def _(sp):
            def load_w(first, last, signal):
                a, b = W_AT[first][0], W_AT[last][0] + W_AT[last][1]
                sp.dma_start(W[:, a:b], w_d[:, a:b]).then_inc(signal.sem, 16)

            xv = x_d.rearrange("b s d -> (b s) d").rearrange("(t p) d -> p t d", p=P)
            sp.dma_start(X[:, :, :], xv).then_inc(load_x.sem, 16)
            load_w("condT", "l3_ada", load_first)
            sp.dma_start(COL[:, :], c_d).then_inc(load_first.sem, 16)
            sp.dma_start(K[:, :], k_d).then_inc(load_first.sem, 16)
            load_w("l0_wq", "l0_wp", load_l0)
            sp.dma_start(ADJ, adj_d.rearrange("b n m l -> (b n) m l").rearrange("(t p) m l -> p t m l", p=P))\
              .then_inc(load_adj.sem, 16)
            load_w("l1_wq", "l1_w2", load_l1)
            load_w("l2_ws1", "l2_wv1", load_l2)
            load_w("l3_wqkv", "l3_gate", load_l3)
            load_w("fc1", "fc2", load_fc)
            ov = out_d.rearrange("b s d -> (b s) d").rearrange("(t p) d -> p t d", p=P)
            for h in range(2):
                sp.wait_ge(res_r.sem, res_r.after(h))
                sp.dma_start(ov[:, tiles(h), :], RES[:, tiles(h), :]).then_inc(stored.sem, 16)
            sp.wait_ge(stored.sem, stored.after())

        @block.gpsimd
        def _(gp):
            gp.memset(VBLK[0], 0.0).then_inc(vz.sem, 1)
            XB_ADD = {0: "bp", 2: "bo", 3: "b2"}
            n_xb = 0
            for s in STEPS:
                k = s[0]
                if k == "stats":
                    l, h = s[1:]
                    n = NTH[s]
                    if n == 0:
                        gp.wait_ge(load_first.sem, load_first.after())
                    gp.wait_ge(stats.sem, stats.after(n))
                    gp.tensor_scalar(RSTD[:, h, 0, :], MV[:, h, :, 1], EPS, None, ALU.add).then_inc(rstd.sem, 1)
                    gp.wait_ge(rstd.sem, rstd.after(n, 1))
                    gp.tensor_tensor(RSTD[:, h, 1, :], RSTD[:, h, 0, :], konst("mhalf")[:, 0:4], ALU.pow)\
                      .then_inc(rstd.sem, 1)
                    if l == 1:
                        gp.wait_ge(tok_r.sem, tok_r.after(2 + h))
                        add = TM[:, 1, half(h)].rearrange("p (t f) -> p t f", t=4)
                    elif l in XB_ADD:
                        add = stack(row(XB_ADD[l]), 4)
                    if l < 4:
                        gp.tensor_tensor(XB[:, tiles(h), :], X[:, tiles(h), :], add, ALU.add).then_inc(xb_r.sem, 1)
                        n_xb += 1
                elif k == "turn":
                    U = s[1]
                    n = S if UNITS[U][0] < 2 else NK2
                    pr = PR[:, U % 3].rearrange("p g x m -> p (g x) m")[:, :, 0:n]
                    gp.wait_ge(ssum.sem, ssum.after(U))
                    gp.tensor_tensor(pr, pr, spread(RS[:, U % 2, :], n), ALU.mult).then_inc(prob.sem, 1)
                    if U == 3:
                        gp.wait_ge(edge.sem, edge.after(2 * NT))
                        gp.memset(VBLK[1], 0.0).then_inc(vz.sem, 1)
                elif k == "center":
                    gp.wait_ge(wsum.sem, wsum.after())
                    for i in range(2):
                        v = w("l3_wqkv", 1024 * i, 1024).rearrange("p (h f) -> p h f", f=HD3)
                        gp.tensor_tensor(v, v, spread(WS[:, NH * i:NH * (i + 1)], HD3), ALU.add).then_inc(wc_r.sem, 1)
                elif k == "nodes":
                    for i in range(3) if s[1] == 0 else ():
                        gp.wait_ge(made.sem, count_made("pt", 2 * max(U for U in range(8) if U % 3 == i) + 1))
                        gp.memset(PR[:, i].rearrange("p g x m -> p (g x) m")[:, :, NK2:S], 0.0).then_inc(prz.sem, 1)
                elif k == "qkv3":
                    t = s[1]
                    if t == 0:
                        gp.wait_ge(made.sem, count_made("o2", 7))
                        gp.memset(PBD, 0.0).then_inc(pbz.sem, 1)
                    for i in range(4):
                        n = 4 * t + i
                        gp.wait_ge(ss_r.sem, ss_r.after(n))
                        b = SS3[:, n % 2]
                        gp.tensor_scalar(b[:, 1, :], b[:, 0, :], 1.0 / HD3, EPS, ALU.mult, ALU.add)\
                          .then_inc(r3_r.sem, 1)
                        gp.wait_ge(r3_r.sem, r3_r.after(n, 1))
                        gp.tensor_tensor(b[:, 2, :], b[:, 1, :], konst("mhalf")[:, 0:8], ALU.pow)\
                          .then_inc(r3_r.sem, 1)
                elif k == "sum" and s[1] >= NUNIT:
                    U = s[1]
                    pr = PR[:, U % 3, 0:2].rearrange("p g x m -> p (g x) m")
                    gp.wait_ge(ssum.sem, ssum.after(U))
                    gp.tensor_tensor(pr, pr, spread(RS[:, U % 2, 0:NH], S), ALU.mult).then_inc(prob.sem, 1)

        @block.scalar
        def _(act):
            act.dma_start(ROW[:, :], r_d.broadcast_to([P, R_N])).then_inc(load_first.sem, 16)
            act.dma_start(KB[:, :], kb_d).then_inc(load_first.sem, 16)
            act.dma_start(KI[:, :], ki_d).then_inc(load_first.sem, 16)
            act.dma_start(PADM[:, :, :], mask_d).then_inc(load_first.sem, 16)
            q_scale = [1.0] + [HD ** -0.5] * 3
            q_bias = [col("bq0"), SC[:, 1:2], SC[:, 2:3], SC[:, 3:4]]
            for s in STEPS:
                k = s[0]
                if k == "setup":
                    act.wait_ge(load_first.sem, load_first.after())
                    act.activation(CS[:, 0, :], w("condT"), ACT.Exp, scale=-1.0).then_inc(silu_e.sem, 1)
                elif k == "tokmod":
                    for i in range(4):
                        act.wait_ge(made.sem, count_made("tokmod", i))
                        act.activation(TM[:, i // 2, half(i % 2)], bank("tokmod", i)[:, :], ACT.Copy)\
                           .then_inc(tok_r.sem, 1)
                elif k == "project":
                    call, h = s[1:]
                    n, par = NTH[s], call // 3
                    if n == 0:
                        act.wait_ge(cols_r.sem, cols_r.after())
                    act.wait_ge(made.sem, count_made("q", n))
                    act.activation(QT[:, par, half(h)], bank("q", n)[:, :], ACT.Identity, bias=q_bias[call],
                                   scale=q_scale[call]).then_inc(q_r.sem, 1)
                    act.wait_ge(made.sem, count_made("k", n))
                    for c in range(NC):
                        act.activation(KBLK[par][:, c, half(h)], bank("k", n)[:, :], ACT.Identity,
                                       bias=KM[:, call, c:c + 1], scale=konst("head_mask")[:, c:c + 1])\
                           .then_inc(k_r.sem, 1)
                    act.wait_ge(made.sem, count_made("v", n))
                    act.wait_ge(vz.sem, vz.after(par))
                    for c in range(NC):
                        rows = slice(S * c, S * c + S)
                        act.activation(VBLK[par][rows, 16 * h:16 * h + 16, :, c, :],
                                       bank("v", n)[rows, :].rearrange("p (b g f) -> p b g f", g=NG, f=HD), ACT.Copy)\
                           .then_inc(v_r.sem, 1)
                elif k == "scores":
                    U = s[1]
                    n = S if UNITS[U][0] < 2 else NK2
                    pr = PR[:, U % 3].rearrange("p g x m -> p (g x) m")[:, :, 0:n]
                    act.wait_ge(ssub.sem, ssub.after(U))
                    act.activation(pr, pr, ACT.Exp).then_inc(expd.sem, 1)
                elif k == "turn":
                    U = s[1]
                    for tt in range(2):
                        if U >= 2 and tt == 0:
                            act.wait_ge(made.sem, count_made(*(("o", U - 2) if U - 2 < 8 else ("o2", U - 10))))
                        act.wait_ge(made.sem, count_made("pt", 2 * U + tt))
                        act.activation(PTS[:, U % 2, tt].rearrange("p g t -> p (g t)"), bank("pt", 2 * U + tt)[:, :],
                                       ACT.Copy).then_inc(pt_r.sem, 1)
                elif k == "weigh":
                    U = s[1]
                    call = UNITS[U][0]
                    if call < 2:
                        if U >= 2:
                            act.wait_ge(made.sem, count_made("y", U - 2))
                        act.wait_ge(made.sem, count_made("o", U))
                        act.activation(OT[:, U % 2, :], bank("o", U)[:, 0:UT], ACT.Identity,
                                       bias=SC[:, 0:1] if call == 0 else col("bv1"),
                                       scale=D ** -0.5 if call == 0 else 1.0).then_inc(o_r.sem, 1)
                elif k == "up":
                    h = s[1]
                    for c in range(NCH):
                        act.wait_ge(made.sem, count_made("up", NCH * h + c))
                        act.activation(HIDb[:, c, half(h)], bank("up", NCH * h + c)[:, :], ACT.Gelu,
                                       bias=col("b1", c)).then_inc(gelu.sem, 1)
                elif k == "nodes":
                    h = s[1]
                    act.wait_ge(made.sem, count_made("xT", h))
                    act.activation(TM[:, 0, half(h)], bank("xT", h)[:, :], ACT.Copy).then_inc(xT_r.sem, 1)
                elif k == "self":
                    h = s[1]
                    act.wait_ge(made.sem, count_made("self", h))
                    act.activation(TM[:, 1, half(h)], bank("self", h)[:, :], ACT.Identity, bias=col("bself"))\
                       .then_inc(self_r.sem, 1)
                elif k == "back":
                    h = s[1]
                    act.wait_ge(made.sem, count_made("back", h))
                    act.activation(X[:, tiles(h), :].rearrange("p t f -> p (t f)"), bank("back", h)[:, :], ACT.Copy)\
                       .then_inc(xk_r.sem, 1)
                elif k == "qkv3":
                    t = s[1]
                    for i in range(4):
                        n = 4 * t + i
                        if n >= 2:
                            act.wait_ge(ss_r.sem, ss_r.after(n - 2))
                        act.wait_ge(made.sem, count_made("qk3", n))
                        act.activation(SQ3[:, n % 2, :], bank("qk3", n)[:, :], ACT.Square).then_inc(sq_r.sem, 1)
                    for i in range(2):
                        n = 2 * t + i
                        if t >= 2:
                            act.wait_ge(made.sem, count_made("o3", 2 * (t - 2) + 1))
                        act.wait_ge(made.sem, count_made("v3", n))
                        act.activation(V3[:, t % 2, 512 * i:512 * i + 512], bank("v3", n)[:, :], ACT.Copy)\
                           .then_inc(v3_r.sem, 1)
                elif k == "qkT3":
                    t = s[1]
                    for i in range(4):
                        n = 4 * t + i
                        if t >= 2:
                            act.wait_ge(s_made.sem, s_made.after(NUNIT + t - 2))
                        act.wait_ge(made.sem, count_made("qkT3", n))
                        act.activation(QK3[:, t % 2, i // 2, 4 * (i % 2):4 * (i % 2) + 4, :]
                                       .rearrange("p c t -> p (c t)"), bank("qkT3", n)[:, :], ACT.Identity,
                                       bias=SC[:, 5:6] if i < 2 else col("kn_b"),
                                       scale=SC[:, 4:5] if i < 2 else col("kn_g")).then_inc(qk_r.sem, 1)
                elif k == "scores3":
                    U = NUNIT + s[1]
                    pr = PR[:, U % 3, 0:2].rearrange("p g x m -> p (g x) m")
                    act.wait_ge(ssub.sem, ssub.after(U))
                    act.activation(pr, pr, ACT.Exp).then_inc(expd.sem, 1)
                elif k == "weigh3":
                    t = s[1]
                    for i in range(2):
                        n = 2 * t + i
                        if t >= 2:
                            act.wait_ge(made.sem, count_made("y3", t - 2))
                        act.wait_ge(made.sem, count_made("o3", n))
                        act.activation(OT3[:, t % 2, 4 * i:4 * i + 4, :].rearrange("p c t -> p (c t)"),
                                       bank("o3", n)[:, :], ACT.Copy).then_inc(o3_r.sem, 1)
                elif k == "split":
                    h = s[1]
                    xn = XN[:, tiles(h), :]
                    act.wait_ge(made.sem, count_made("y3", NT - 1))
                    act.wait_ge(normed.sem, normed.after(NTH["norm", 5, h]))
                    act.activation(XSP[:, tiles(h), 0, :], xn, ACT.Copy).then_inc(xs_a.sem, 1)
                    act.wait_ge(xs_v.sem, xs_v.after(h, 1))
                    act.activation(XSP[:, tiles(h), 1, :], xn, ACT.Copy).then_inc(xs_a.sem, 1)
                elif k == "tokT":
                    h = s[1]
                    act.wait_ge(made.sem, count_made("tokT", h))
                    act.activation(TOKT[:, half(h)], bank("tokT", h)[:, :], ACT.Copy).then_inc(tt_r.sem, 1)
                elif k == "route":
                    act.wait_ge(rt.sem, RT_LOGIT)
                    act.activation(RG[:, 1, :], RG[:, 0, :], ACT.Exp).then_inc(rta.sem, 1)
                    for i in range(2):
                        act.wait_ge(made.sem, count_made("gates", i))
                        act.activation(GBC[:, half(i)], bank("gates", i)[:, :], ACT.Copy).then_inc(gb_r.sem, 1)
                elif k == "experts":
                    for i in range(2):
                        act.wait_ge(made.sem, count_made("gather", i))
                        act.activation(GTT[:, 512 * i:512 * i + 512], bank("gather", i)[:, :], ACT.Identity,
                                       bias=col("mlp_b"), scale=col("mlp_g")).then_inc(gt_r.sem, 1)
                    for e in range(NE):
                        if e >= 2:
                            act.wait_ge(made.sem, count_made("fc2", e - 2))
                        act.wait_ge(made.sem, count_made("fc1", e))
                        for c in range(NCH):
                            act.activation(HE[:, e % 2, c, :], bank("fc1", e)[:, P * c:P * c + P],
                                           ACT.Gelu_apprx_tanh, bias=col("b1s", NCH * e + c)).then_inc(he_r.sem, 1)

        @block.vector
        def _(dve):
            COPY = dict(scalar2=None)

            edge_steps, rt_steps = count(1), count(1)

            def edge_step():
                return next(edge_steps)

            def rt_step():
                return next(rt_steps)

            for s in STEPS:
                k = s[0]
                if k == "setup":
                    dve.wait_ge(load_first.sem, load_first.after())
                    for call in range(4):
                        dve.tensor_scalar(KM[:, call, :], konst("head_mask"), col(f"bk{call}"), None, ALU.mult)\
                           .then_inc(cols_r.sem, 1)
                    for i, (c, scale) in enumerate([(col("bv0"), D ** -0.5), (col("bq1"), HD ** -0.5),
                                                    (col("bq2"), HD ** -0.5), (col("bq3"), HD ** -0.5),
                                                    (col("qn_g"), HD3 ** -0.5), (col("qn_b"), HD3 ** -0.5)]):
                        dve.tensor_scalar(SC[:, i:i + 1], c, scale, None, ALU.mult).then_inc(cols_r.sem, 1)
                    dve.tensor_scalar(PAD[:, :, :], PADM[:, :, :], -BIG, BIG, ALU.mult, ALU.mult).then_inc(edge.sem, 1)
                    dve.wait_ge(edge.sem, edge_step())
                    dve.wait_ge(silu_e.sem, silu_e.after())
                    dve.tensor_scalar(CS[:, 0, :], CS[:, 0, :], 1.0, None, ALU.add).then_inc(silu.sem, 1)
                    dve.wait_ge(silu.sem, silu.after(0, 1))
                    dve.reciprocal(CS[:, 0, :], CS[:, 0, :]).then_inc(silu.sem, 1)
                    dve.wait_ge(silu.sem, silu.after(0, 2))
                    dve.tensor_tensor(CS[:, 0, :], CS[:, 0, :], w("condT"), ALU.mult).then_inc(silu.sem, 1)
                    dve.wait_ge(made.sem, count_made("cond"))
                    m = bank("cond")[:, 0:6 * B].rearrange("p (i b) -> p i b", i=6)
                    dve.tensor_scalar(CM[:, 0, :], m[:, 0], col("bg"), col("ln_g"), ALU.add, ALU.mult)\
                       .then_inc(cond_r.sem, 1)
                    dve.tensor_scalar(CS[:, 1, :], m[:, 0], col("bg"), col("ln_b"), ALU.add, ALU.mult)\
                       .then_inc(cond_r.sem, 1)
                    dve.tensor_scalar(CS[:, 2, :], m[:, 1], col("bb"), None, ALU.add).then_inc(cond_r.sem, 1)
                    for i, name in ((2, "ad1"), (4, "ad2")):
                        dve.tensor_scalar(CM[:, i, :], m[:, i], col(name, 0), 1.0, ALU.add, ALU.add)\
                           .then_inc(cond_r.sem, 1)
                        dve.tensor_scalar(CM[:, i + 1, :], m[:, i + 1], col(name, 1), None, ALU.add)\
                           .then_inc(cond_r.sem, 1)
                    dve.wait_ge(cond_r.sem, cond_r.after(0, 7))
                    dve.tensor_tensor(CM[:, 1, :], CS[:, 1, :], CS[:, 2, :], ALU.add).then_inc(cond_r.sem, 1)
                    dve.wait_ge(made.sem, count_made("ada"))
                    dve.tensor_scalar(CM[:, 6, :], bank("ada")[:, 0:B], col("b_ada"), col("ln1_b"), ALU.add, ALU.add)\
                       .then_inc(ada_r.sem, 1)
                elif k == "stats":
                    l, h = s[1:]
                    n = NTH[s]
                    if l == 0:
                        dve.wait_ge(load_x.sem, load_x.after())
                    elif l == 1:
                        dve.wait_ge(x_r.sem, x_r.after(2 * h + 1))
                    elif l == 2:
                        dve.wait_ge(xg_r.sem, xg_r.after(h))
                    elif l == 3:
                        dve.wait_ge(x_r.sem, x_r.after(4 + 2 * h + 1))
                    elif l == 4:
                        dve.wait_ge(xk_r.sem, xk_r.after(h))
                    else:
                        dve.wait_ge(x3_r.sem, x3_r.after(4 * h + 3))
                    for t in range(4):
                        dve.bn_stats(ST[:, h, t, :], X[:, 4 * h + t, :]).then_inc(stats.sem, 1)
                    for t in range(4):
                        dve.wait_ge(stats.sem, stats.after(n, 1 + t))
                        dve.bn_aggr(MV[:, h, t, :], ST[:, h, t, :]).then_inc(stats.sem, 1)
                elif k == "norm":
                    l, h = s[1:]
                    n = NTH[s]
                    dve.wait_ge(rstd.sem, rstd.after(NTH["stats", l, h]))
                    for t in range(4):
                        dve.tensor_scalar(XN[:, 4 * h + t, :], X[:, 4 * h + t, :], MV[:, h, t, 0:1],
                                          RSTD[:, h, 1, t:t + 1], ALU.subtract, ALU.mult).then_inc(normed.sem, 1)
                elif k == "modulate":
                    m, h = s[1:]
                    n = NTH[s]
                    o = HTb[:, half(h)].rearrange("p (b q) -> p b q", q=S)
                    bs = slice(16 * h, 16 * h + 16)
                    dve.wait_ge(cond_r.sem, cond_r.after())
                    dve.wait_ge(made.sem, count_made("xnT", n))
                    dve.tensor_tensor(o, bank("xnT", n)[:, :].rearrange("p (b q) -> p b q", q=S),
                                      spread(CM[:, 2 * m, bs], S), ALU.mult).then_inc(modul.sem, 1)
                    dve.wait_ge(modul.sem, modul.after(n, 1))
                    dve.tensor_tensor(o, o, spread(CM[:, 2 * m + 1, bs], S), ALU.add).then_inc(modul.sem, 1)
                elif k == "modulate3":
                    h = s[1]
                    dve.wait_ge(made.sem, count_made("xnT3", h))
                    dve.scalar_tensor_tensor(HTb[:, half(h)].rearrange("p (b q) -> p b q", q=S),
                                             bank("xnT3", h)[:, :].rearrange("p (b q) -> p b q", q=S), col("ln1_g"),
                                             spread(CM[:, 6, 16 * h:16 * h + 16], S), ALU.mult, ALU.add)\
                       .then_inc(h3_r.sem, 1)
                elif k == "remod":
                    h = s[1]
                    dve.wait_ge(tok_r.sem, tok_r.after(h))
                    dve.wait_ge(normed.sem, normed.after(NTH["norm", 1, h]))
                    xn = XN[:, tiles(h), :]
                    dve.tensor_tensor(xn, xn, TM[:, 0, half(h)].rearrange("p (t f) -> p t f", t=4), ALU.mult)\
                       .then_inc(tg_r.sem, 1)
                    dve.wait_ge(tg_r.sem, tg_r.after(h))
                    dve.wait_ge(xb_r.sem, xb_r.after(NTH["stats", 1, h]))
                    dve.tensor_tensor(X[:, tiles(h), :], xn, XB[:, tiles(h), :], ALU.add).then_inc(xg_r.sem, 1)
                elif k == "edges":
                    dve.wait_ge(load_adj.sem, load_adj.after())
                    cond = EM[:, 0].rearrange("p t m -> p (t m)")
                    bias = EB[:, 0].rearrange("p t m -> p (t m)")
                    for t in range(NT):
                        dve.tensor_tensor(ADW[:, t], ADJ[:, t], stack(row("w_bias"), S), ALU.mult)\
                           .then_inc(edge_w.sem, 1)
                    for t in range(NT):
                        dve.tensor_reduce(EM[:, 0, t, :], ADJ[:, t], AX, ALU.add).then_inc(edge.sem, 1)
                        dve.wait_ge(edge.sem, edge_step())
                    for t in range(NT):
                        dve.wait_ge(edge_w.sem, edge_w.after(t))
                        dve.tensor_reduce(EB[:, 0, t, :], ADW[:, t], AX, ALU.add).then_inc(edge.sem, 1)
                        dve.wait_ge(edge.sem, edge_step())
                    dve.tensor_scalar(EM[:, 0], EM[:, 0], 0.0, None, ALU.is_gt).then_inc(edge.sem, 1)
                    dve.wait_ge(edge.sem, edge_step())
                    dve.tensor_scalar(EB[:, 0], EB[:, 0], row("b_bias"), None, ALU.add).then_inc(edge.sem, 1)
                    dve.wait_ge(edge.sem, edge_step())
                    dve.tensor_scalar(EM[:, 1], EM[:, 0], -NEG, NEG, ALU.mult, ALU.add).then_inc(edge.sem, 1)
                    dve.wait_ge(edge.sem, edge_step())
                    dve.tensor_tensor(EB[:, 0], EB[:, 0], EM[:, 1], ALU.add).then_inc(edge.sem, 1)
                    dve.wait_ge(edge.sem, edge_step())
                    dve.transpose(EM[:, 1].rearrange("p t m -> p (t m)"), cond).then_inc(edge.sem, 1)
                    dve.wait_ge(edge.sem, edge_step())
                    dve.transpose(EB[:, 1].rearrange("p t m -> p (t m)"), bias).then_inc(edge.sem, 1)
                    dve.wait_ge(edge.sem, edge_step())
                elif k == "scores":
                    U = s[1]
                    call, u = UNITS[U]
                    n = S if call < 2 else NK2
                    sc = Sps[:, :, 0:UT].rearrange("p g (x m) -> p g x m", m=S)[:, :, :, 0:n]
                    pr = PR[:, U % 3, :, :, 0:n]
                    if U >= 3:
                        dve.wait_ge(made.sem, count_made("pt", 2 * (U - 3) + 1))
                    if call >= 2:
                        dve.wait_ge(prz.sem, prz.after(2))
                    dve.wait_ge(s_made.sem, s_made.after(U))
                    if call == 1:
                        for tt in range(2):
                            pad = PAD[:, 2 * u + tt, :].unsqueeze(1).unsqueeze(1).broadcast_to([P, NG, NC, S])
                            dve.tensor_tensor(pr[:, :, NC * tt:NC * tt + NC], sc[:, :, NC * tt:NC * tt + NC], pad,
                                              ALU.add).then_inc(masked.sem, 1)
                        dve.wait_ge(masked.sem, masked.after(U - 4))
                    elif call >= 2:
                        for tt in range(2):
                            em, eb = (a[:, call - 2, 2 * u + tt, 0:n].unsqueeze(1).unsqueeze(1)
                                      .broadcast_to([P, NG, NC, n]) for a in (EM, EB))
                            part = pr[:, :, NC * tt:NC * tt + NC]
                            dve.tensor_tensor(part, sc[:, :, NC * tt:NC * tt + NC], em, ALU.mult)\
                               .then_inc(masked.sem, 1)
                        for tt in range(2):
                            eb = EB[:, call - 2, 2 * u + tt, 0:n].unsqueeze(1).unsqueeze(1)\
                                .broadcast_to([P, NG, NC, n])
                            part = pr[:, :, NC * tt:NC * tt + NC]
                            dve.wait_ge(masked.sem, masked.after(U - 4, 1 + tt))
                            dve.tensor_tensor(part, part, eb, ALU.add).then_inc(biased.sem, 1)
                        dve.wait_ge(biased.sem, biased.after(U - 8))
                    src = sc if call == 0 else pr
                    mx = MX[:, U % 2, :].rearrange("p (g x) -> p g x", g=NG)
                    dve.tensor_reduce(mx, src, AX, ALU.max).then_inc(smax.sem, 1)
                    dve.wait_ge(smax.sem, smax.after(U))
                    dve.tensor_tensor(pr, src, mx.unsqueeze(3).broadcast_to([P, NG, 2 * NC, n]), ALU.subtract)\
                       .then_inc(ssub.sem, 1)
                elif k == "sum":
                    U = s[1]
                    if U < NUNIT:
                        n = S if UNITS[U][0] < 2 else NK2
                        heads = 2 * NH
                        pr = PR[:, U % 3].rearrange("p g x m -> p (g x) m")[:, :, 0:n]
                    else:
                        heads = NH
                        pr = PR[:, U % 3, 0:2].rearrange("p g x m -> p (g x) m")
                    if U >= 2:
                        dve.wait_ge(prob.sem, prob.after(U - 2))
                    dve.wait_ge(expd.sem, expd.after(U))
                    dve.tensor_reduce(SM[:, U % 2, 0:heads], pr, AX, ALU.add).then_inc(ssum.sem, 1)
                    dve.wait_ge(ssum.sem, ssum.after(U, 1))
                    dve.reciprocal(RS[:, U % 2, 0:heads], SM[:, U % 2, 0:heads]).then_inc(ssum.sem, 1)
                elif k == "weigh" and UNITS[s[1]][0] >= 2:
                    U = s[1]
                    call, u = UNITS[U]
                    a = ACC[:, UT * u:UT * u + UT]
                    dve.wait_ge(made.sem, count_made("o2", U - 8))
                    base = TM[:, 1, UT * u:UT * u + UT] if call == 2 else a
                    if call == 2:
                        dve.wait_ge(self_r.sem, self_r.after(u // 2))
                    else:
                        dve.wait_ge(acc_r.sem, acc_r.after(U - 9))
                        dve.wait_ge(xT_r.sem, xT_r.after(u // 2))
                    dve.scalar_tensor_tensor(a, bank("o2", U - 8)[:, 0:UT], col(f"bo{call}"), base, ALU.add, ALU.add)\
                       .then_inc(acc_r.sem, 1)
                    if call == 3:
                        dve.wait_ge(acc_r.sem, acc_r.after(U - 8))
                        dve.scalar_tensor_tensor(a, a, 0.0, TM[:, 0, UT * u:UT * u + UT], ALU.max, ALU.add)\
                           .then_inc(rel_r.sem, 1)
                elif k == "out":
                    U = s[1]
                    u = UNITS[U][1]
                    dve.wait_ge(made.sem, count_made("y", U))
                    call = UNITS[U][0]
                    dve.wait_ge(xb_r.sem, xb_r.after(NTH["stats", 2 * call, u // 2]))
                    xt = slice(2 * u, 2 * u + 2)
                    dve.tensor_tensor(X[:, xt, :], bank("y", U)[:, 0:UT].rearrange("p (t f) -> p t f", t=2),
                                      XB[:, xt, :], ALU.add).then_inc(x_r.sem, 1)
                elif k == "down":
                    h = s[1]
                    dve.wait_ge(made.sem, count_made("down", h))
                    dve.wait_ge(xb_r.sem, xb_r.after(NTH["stats", 3, h]))
                    dve.tensor_tensor(X[:, tiles(h), :], bank("down", h)[:, :].rearrange("p (t f) -> p t f", t=4),
                                      XB[:, tiles(h), :], ALU.add).then_inc(xm_r.sem, 1)
                elif k == "nodes":
                    h = s[1]
                    dve.wait_ge(xm_r.sem, xm_r.after(h))
                    dve.tensor_reduce(NZ[:, h, 0, :], X[:, tiles(h), :], AX, ALU.add).then_inc(nz_r.sem, 1)
                    dve.wait_ge(nz_r.sem, nz_r.after(h, 1))
                    dve.tensor_scalar(NZ[:, h, 1, :], NZ[:, h, 0, :], 0.0, None, ALU.not_equal).then_inc(nz_r.sem, 1)
                    dve.wait_ge(made.sem, count_made("nz", h))
                    dve.tensor_tensor(HTb[:, half(h)].rearrange("p (b q) -> p b q", q=S),
                                      bank("nz", h)[:, :].rearrange("p (b q) -> p b q", q=S),
                                      spread(w("condT")[:, 16 * h:16 * h + 16], S), ALU.mult).then_inc(qe_r.sem, 1)
                elif k == "center":
                    dve.wait_ge(load_l3.sem, load_l3.after())
                    dve.tensor_reduce(WS[:, :], w("l3_wqkv", 0, 2048).rearrange("p (h f) -> p h f", f=HD3), AX,
                                      ALU.add).then_inc(wsum.sem, 1)
                    dve.wait_ge(wsum.sem, wsum.after(0, 1))
                    dve.tensor_scalar(WS[:, :], WS[:, :], -1.0 / HD3, None, ALU.mult).then_inc(wsum.sem, 1)
                elif k == "qkv3":
                    t = s[1]
                    for i in range(4):
                        n = 4 * t + i
                        if n >= 2:
                            dve.wait_ge(qn_r.sem, qn_r.after(n - 2)) if n - 2 < 4 * t else None
                        dve.wait_ge(sq_r.sem, sq_r.after(n))
                        dve.tensor_reduce(SS3[:, n % 2, 0, :], SQ3[:, n % 2, :].rearrange("p (h f) -> p h f", f=HD3),
                                          AX, ALU.add).then_inc(ss_r.sem, 1)
                        if i % 2:
                            for m in (n - 1, n):
                                if m >= 4:
                                    dve.wait_ge(made.sem, count_made("qkT3", m - 4))
                                dve.wait_ge(r3_r.sem, r3_r.after(m))
                                dve.tensor_tensor(QN3[:, m % 4, :].rearrange("p (h f) -> p h f", f=HD3),
                                                  bank("qk3", m)[:, :].rearrange("p (h f) -> p h f", f=HD3),
                                                  spread(SS3[:, m % 2, 2, :], HD3), ALU.mult).then_inc(qn_r.sem, 1)
                elif k == "scores3":
                    U = NUNIT + s[1]
                    sc = Sps[:, 0:2, 0:UT].rearrange("p r (c m) -> p r c m", m=S)
                    pr = PR[:, U % 3, 0:2]
                    mx = MX[:, U % 2, 0:NH].rearrange("p (g x) -> p g x", g=2)
                    if U - 3 >= NUNIT:
                        dve.wait_ge(pb_r.sem, pb_r.after(U - 3 - NUNIT))
                    else:
                        dve.wait_ge(made.sem, count_made("pt", 2 * (U - 3) + 1))
                    dve.wait_ge(s_made.sem, s_made.after(U))
                    dve.tensor_reduce(mx, sc, AX, ALU.max).then_inc(smax.sem, 1)
                    dve.wait_ge(smax.sem, smax.after(U))
                    dve.tensor_tensor(pr, sc, mx.unsqueeze(3).broadcast_to([P, 2, 8, S]), ALU.subtract)\
                       .then_inc(ssub.sem, 1)
                elif k == "weigh3":
                    t = s[1]
                    U = NUNIT + t
                    if t == 0:
                        dve.wait_ge(pbz.sem, pbz.after())
                    if t >= 2:
                        dve.wait_ge(made.sem, count_made("o3", 2 * (t - 2) + 1))
                    dve.wait_ge(prob.sem, prob.after(U))
                    for j in range(BPT):
                        rows = slice(S * j, S * j + S)
                        dve.transpose(PBD[rows, t % 2, :, S * j:S * j + S],
                                      PR[rows, U % 3, 0:2].rearrange("p g x m -> p (g x) m")).then_inc(pb_r.sem, 1)
                elif k == "out3":
                    t = s[1]
                    dve.wait_ge(made.sem, count_made("y3", t))
                    dve.wait_ge(xk_r.sem, xk_r.after(t // 4))
                    dve.tensor_tensor(X[:, t, :], bank("y3", t)[:, 0:D], X[:, t, :], ALU.add).then_inc(x3_r.sem, 1)
                elif k == "split":
                    h = s[1]
                    xn = XN[:, tiles(h), :]
                    dve.wait_ge(xs_a.sem, xs_a.after(h, 1))
                    dve.tensor_tensor(xn, xn, XSP[:, tiles(h), 0, :], ALU.subtract).then_inc(xs_v.sem, 1)
                    dve.wait_ge(xs_a.sem, xs_a.after(h, 2))
                    dve.tensor_tensor(XSP[:, tiles(h), 2, :], xn, XSP[:, tiles(h), 1, :], ALU.subtract)\
                       .then_inc(xs_v.sem, 1)
                elif k == "route":
                    te = lambda a: a.rearrange("p (t e) -> p t e", e=NE)
                    gate = RG[:, 2, :]
                    dve.wait_ge(made.sem, count_made("logit"))
                    lg = te(bank("logit")[:, 0:NT * NE])
                    dve.tensor_reduce(RT[:, 0:8], lg, AX, ALU.max).then_inc(rt.sem, 1)
                    dve.wait_ge(rt.sem, rt_step())
                    dve.tensor_tensor(te(RG[:, 0, :]), lg, spread(RT[:, 0:8], NE), ALU.subtract).then_inc(rt.sem, 1)
                    dve.wait_ge(rt.sem, rt_step())
                    dve.wait_ge(rta.sem, rta.after())
                    dve.tensor_reduce(RT[:, 8:16], te(RG[:, 1, :]), AX, ALU.add).then_inc(rt.sem, 1)
                    dve.wait_ge(rt.sem, rt_step())
                    dve.reciprocal(RT[:, 8:16], RT[:, 8:16]).then_inc(rt.sem, 1)
                    dve.wait_ge(rt.sem, rt_step())
                    dve.tensor_tensor(te(gate), te(RG[:, 1, :]), spread(RT[:, 8:16], NE), ALU.mult).then_inc(rt.sem, 1)
                    at = rt_step()
                    dve.wait_ge(rt.sem, at)
                    assert at == RT_GATE
                    dve.tensor_copy(JUNK.rearrange("p (x r) -> p x r", r=16), spread(gate, 16)).then_inc(rt.sem, 1)
                    dve.wait_ge(rt.sem, rt_step())
                    dve.memset(RTI[:, 0:1], 0).then_inc(rt.sem, 1)
                    dve.wait_ge(rt.sem, rt_step())
                    dve.wait_ge(gb_r.sem, gb_r.after(1))
                    for i, shift in enumerate(SHIFTS):
                        dve.tensor_tensor(RTI[:, 1:2], RTI[:, 0:1], KI[:, i:i + 1], ALU.bitwise_or).then_inc(rt.sem, 1)
                        dve.wait_ge(rt.sem, rt_step())
                        dve.tensor_scalar(JUNK, GBC, RTI[:, 1:2].bitcast(F32), 0.0, ALU.is_ge, ALU.add,
                                          accum_out=RT[:, 0:1]).then_inc(rt.sem, 1)
                        dve.wait_ge(rt.sem, rt_step())
                        dve.tensor_scalar(RT[:, 1:2], RT[:, 0:1], float(CAP), None, ALU.is_ge).then_inc(rt.sem, 1)
                        at = rt_step()
                        dve.wait_ge(rt.sem, at)
                        assert at == RT_ROUND[i] + 3
                        dve.wait_ge(cnt.sem, cnt.after(i))
                        dve.tensor_scalar(RTI[:, 2:3], Sps[:, 0, 0:1], -1.0, float(1 << shift), ALU.add,
                                          ALU.mult).then_inc(rt.sem, 1)
                        dve.wait_ge(rt.sem, rt_step())
                        dve.tensor_tensor(RTI[:, 0:1], RTI[:, 0:1], RTI[:, 2:3], ALU.bitwise_or).then_inc(rt.sem, 1)
                        dve.wait_ge(rt.sem, rt_step())
                    dve.wait_ge(made.sem, count_made("thr"))
                    thr = stack(bank("thr")[:, 0:P:16], NT)
                    above, at_thr = (RGB[:, i, :] for i in range(2))
                    dve.tensor_tensor(te(above), te(gate), thr, ALU.is_gt).then_inc(rt.sem, 1)
                    dve.wait_ge(rt.sem, rt_step())
                    dve.tensor_tensor(te(at_thr), te(gate), thr, ALU.is_equal).then_inc(rt.sem, 1)
                    at = rt_step()
                    dve.wait_ge(rt.sem, at)
                    assert at == RT_EQ
                    dve.wait_ge(made.sem, count_made("total"))
                    need = RT[:, 2:10]
                    dve.tensor_scalar(need, bank("total")[:, 0:NE], -1.0, float(CAP), ALU.mult, ALU.add).then_inc(rt.sem, 1)
                    dve.wait_ge(rt.sem, rt_step())
                    dve.wait_ge(made.sem, count_made("prefix"))
                    pre = bank("prefix")[:, 0:2 * NT * NE].rearrange("p (i t e) -> p i t e", i=2, e=NE)
                    a, b, c, pos = (RG[:, i, :] for i in (4, 5, 6, 7))
                    dve.tensor_tensor(te(a), pre[:, 1], stack(need, NT), ALU.is_lt).then_inc(rt.sem, 1)
                    dve.wait_ge(rt.sem, rt_step())
                    dve.tensor_tensor(a, a, at_thr, ALU.mult).then_inc(rt.sem, 1)
                    dve.wait_ge(rt.sem, rt_step())
                    dve.tensor_tensor(a, a, above, ALU.add).then_inc(rt.sem, 1)
                    dve.wait_ge(rt.sem, rt_step())
                    dve.tensor_tensor(te(b), pre[:, 1], stack(need, NT), ALU.min).then_inc(rt.sem, 1)
                    dve.wait_ge(rt.sem, rt_step())
                    dve.tensor_tensor(te(b), te(b), pre[:, 0], ALU.add).then_inc(rt.sem, 1)
                    at = rt_step()
                    dve.wait_ge(rt.sem, at)
                    assert at == RT_PREFIX
                    dve.tensor_scalar(c, a, -512.0, 512.0, ALU.mult, ALU.add).then_inc(rt.sem, 1)
                    dve.wait_ge(rt.sem, rt_step())
                    dve.tensor_tensor(pos, b, c, ALU.add).then_inc(rt.sem, 1)
                    dve.wait_ge(rt.sem, rt_step())
                    dve.tensor_copy(RGB[:, 2, :], pos).then_inc(rt.sem, 1)
                    at = rt_step()
                    dve.wait_ge(rt.sem, at)
                    assert at == RT_POS
                    parts = RGB[:, 3:6, :]
                    dve.tensor_copy(parts[:, 0, :], gate).then_inc(rt.sem, 1)
                    dve.wait_ge(rt.sem, rt_step())
                    dve.tensor_tensor(RG[:, 3, :], gate, parts[:, 0, :], ALU.subtract).then_inc(rt.sem, 1)
                    dve.wait_ge(rt.sem, rt_step())
                    dve.tensor_copy(parts[:, 1, :], RG[:, 3, :]).then_inc(rt.sem, 1)
                    dve.wait_ge(rt.sem, rt_step())
                    dve.tensor_tensor(parts[:, 2, :], RG[:, 3, :], parts[:, 1, :], ALU.subtract).then_inc(rt.sem, 1)
                    at = rt_step()
                    dve.wait_ge(rt.sem, at)
                    assert at == RT_SPLIT
                elif k == "experts":
                    def pick_T(i):
                        dve.wait_ge(made.sem, count_made("posT", i))
                        dve.tensor_scalar(PICT[:, i // 2, half(i % 2)], bank("posT", i)[:, :], konst("iota_col"), None,
                                          ALU.is_equal).then_inc(pict_r.sem, 1)

                    for t in range(NT):
                        dve.tensor_tensor(PIC[:, t].rearrange("p (e s) -> p e s", e=NE), stack(konst("iota_row"), NE),
                                          spread(RG[:, 7, NE * t:NE * t + NE], CAP), ALU.is_equal).then_inc(pic_v.sem, 1)
                    n_posT = 0
                    for _ in range(4):
                        pick_T(n_posT)
                        n_posT += 1
                    dve.wait_ge(made.sem, count_made("weight"))
                    dve.tensor_reduce(RT[:, 0:NE], bank("weight")[:, 0:3 * NE]
                                           .rearrange("p (e k) -> p e k", k=3), AX, ALU.add).then_inc(rt.sem, 1)
                    at = rt_step()
                    dve.wait_ge(rt.sem, at)
                    assert at == RT_WEIGHT
                    for e in range(NE + 1):
                        for _ in range(3 * (e % 2)):
                            pick_T(n_posT)
                            n_posT += 1
                        if e:
                            f = e - 1
                            y, r = YB[:, f % 2, 0, :], YB[:, f % 2, 1, :]
                            dve.wait_ge(made.sem, count_made("fc2", f))
                            dve.tensor_tensor(y, bank("fc2", f)[:, 0:D], row("b2s", D * f, D), ALU.add)\
                               .then_inc(y_r.sem, 1)
                            dve.wait_ge(y_r.sem, y_r.after(f, 1))
                            dve.tensor_scalar(y, y, RT[:, f:f + 1], None, ALU.mult).then_inc(y_r.sem, 1)
                            dve.wait_ge(y_r.sem, y_r.after(f, 2))
                            dve.tensor_copy(YSP[:, f, 0, :], y).then_inc(y_r.sem, 1)
                            dve.wait_ge(y_r.sem, y_r.after(f, 3))
                            dve.tensor_tensor(r, y, YSP[:, f, 0, :], ALU.subtract).then_inc(y_r.sem, 1)
                            dve.wait_ge(y_r.sem, y_r.after(f, 4))
                            dve.tensor_copy(YSP[:, f, 1, :], r).then_inc(y_r.sem, 1)
                            dve.wait_ge(y_r.sem, y_r.after(f, 5))
                            dve.tensor_tensor(YSP[:, f, 2, :], r, YSP[:, f, 1, :], ALU.subtract).then_inc(y_r.sem, 1)
                    for h in range(2):
                        dve.wait_ge(made.sem, count_made("scatter", h))
                        dve.tensor_tensor(RES[:, tiles(h), :], bank("scatter", h)[:, :]
                                          .rearrange("p (t f) -> p t f", t=4), X[:, tiles(h), :], ALU.add)\
                           .then_inc(res_r.sem, 1)

        @block.tensor
        def _(pe):
            def mm(out, lhsT, rhs, start=True, stop=True):
                return pe.matmul(out, lhsT, rhs, start=start, stop=stop)

            def turn4(out, src):
                for i in range(4):
                    last = pe.transpose(out[:, P * i:P * i + P], src(i), ident)
                return last

            for s in STEPS:
                k = s[0]
                if k == "setup":
                    pe.wait_ge(load_first.sem, load_first.after())
                    b = bank("cond")
                    for i, lhsT in enumerate([w("l0_wg"), w("l0_wb"), w("l1_ad1", 0, D), w("l1_ad1", D, D),
                                              w("l1_ad2", 0, D), w("l1_ad2", D, D)]):
                        last = mm(b[:, B * i:B * i + B], lhsT, w("condT"))
                    last.then_inc(made.sem, 1)
                    b = bank("ada")
                    pe.wait_ge(silu.sem, silu.after())
                    mm(b[:, 0:B], w("l3_ada"), CS[:, 0, :]).then_inc(made.sem, 1)
                elif k == "tokmod":
                    pe.wait_ge(cond_r.sem, cond_r.after())
                    for i in range(4):
                        pe.wait_ge(*last_read("tokmod", i))
                        b = bank("tokmod", i)
                        for t in range(4):
                            for j in range(BPT):
                                at = 16 * (i % 2) + 4 * t + j
                                last = mm(b[S * j:S * j + S, P * t:P * t + P],
                                          CM[:, i // 2, at:at + 1].broadcast_to([P, S]), ident)
                        last.then_inc(made.sem, 1)
                elif k == "modulate":
                    m, h = s[1:]
                    if used_before("xnT", NTH[s]):
                        pe.wait_ge(*last_read("xnT", NTH[s]))
                    b = bank("xnT", NTH[s])
                    pe.wait_ge(normed.sem, normed.after(NTH["norm", (0, 2, 3)[m], h]))
                    turn4(b, lambda i: XN[:, 4 * h + i, :]).then_inc(made.sem, 1)
                elif k == "modulate3":
                    h = s[1]
                    pe.wait_ge(*last_read("xnT3", h))
                    b = bank("xnT3", h)
                    pe.wait_ge(normed.sem, normed.after(NTH["norm", 4, h]))
                    turn4(b, lambda i: XN[:, 4 * h + i, :]).then_inc(made.sem, 1)
                elif k == "project":
                    call, h = s[1:]
                    n = NTH[s]
                    names = [("l0_wq", "l0_wk", "l0_wv"), ("l1_wq", "l1_wk", "l1_wv"),
                             ("l2_wq0", "l2_wk0", "l2_wv0"), ("l2_wq1", "l2_wk1", "l2_wv1")][call]
                    if h == 0 and call < 2:
                        loaded = load_l1 if call else load_l0
                        pe.wait_ge(loaded.sem, loaded.after())
                    if call < 2:
                        pe.wait_ge(modul.sem, modul.after(NTH["modulate", call, h]))
                        src = HTb[:, half(h)]
                    else:
                        pe.wait_ge(self_r.sem, self_r.after(h))
                        src = TM[:, 1, half(h)]
                    for kind, name in zip("qk", names):
                        if used_before(kind, n):
                            pe.wait_ge(*last_read(kind, n))
                        b = bank(kind, n)
                        mm(b[:, :], w(name), src).then_inc(made.sem, 1)
                    pe.wait_ge(*last_read("v", n))
                    b = bank("v", n)
                    for i in range(16):
                        for c in range(NC):
                            last = mm(b[S * c:S * c + S, S * i:S * i + S], src[:, S * i:S * i + S],
                                      w(names[2], S * c, S))
                    last.then_inc(made.sem, 1)
                elif k == "scores":
                    U = s[1]
                    call, u = UNITS[U]
                    par, n = call // 3, S if call < 2 else NK2
                    if U:
                        pc = UNITS[U - 1][0]
                        if pc == 0:
                            pe.wait_ge(ssub.sem, ssub.after(U - 1))
                        else:
                            pe.wait_ge(masked.sem, masked.after(U - 5))
                    nth = NTH["project", call, u // 2]
                    pe.wait_ge(q_r.sem, q_r.after(nth))
                    pe.wait_ge(k_r.sem, k_r.after(nth))
                    for tt in range(2):
                        for j in range(BPT):
                            t0 = UT * u + P * tt + S * j
                            for g in range(NG):
                                rows = slice(S * g, S * g + S)
                                o = Sps[S * j:S * j + S, g, P * tt:P * tt + P].rearrange("p (c m) -> p c m", m=S)
                                last = mm(o[:, :, 0:n], QT[rows, par, t0:t0 + S], KBLK[par][rows, :, t0:t0 + n])
                    last.then_inc(s_made.sem, 1)
                elif k == "turn":
                    U = s[1]
                    for tt in range(2):
                        pe.wait_ge(*last_read("pt", 2 * U + tt))
                        b = bank("pt", 2 * U + tt)
                        pe.wait_ge(prob.sem, prob.after(U))
                        turn4(b, lambda g: PR[:, U % 3, g, NC * tt:NC * tt + NC, :].rearrange("p c m -> p (c m)")).then_inc(made.sem, 1)
                elif k == "weigh":
                    U = s[1]
                    call, u = UNITS[U]
                    par = call // 3
                    kind, item = ("o", U) if call < 2 else ("o2", U - 8)
                    pe.wait_ge(*last_read(kind, item))
                    b = bank(kind, item)
                    pe.wait_ge(pt_r.sem, pt_r.after(2 * U + 1))
                    pe.wait_ge(v_r.sem, v_r.after(NTH["project", call, u // 2]))
                    for tt in range(2):
                        for j in range(BPT):
                            bb = 8 * u + 4 * tt + j
                            for g in range(NG):
                                last = mm(b[S * g:S * g + S, P * tt + S * j:P * tt + S * j + S],
                                          VBLK[par][:, bb, g].rearrange("p c f -> p (c f)"), PTS[:, U % 2, tt, g, S * j:S * j + S])
                    last.then_inc(made.sem, 1)
                elif k == "out":
                    U = s[1]
                    pe.wait_ge(*last_read("y", U))
                    b = bank("y", U)
                    pe.wait_ge(o_r.sem, o_r.after(U))
                    for tt in range(2):
                        last = mm(b[:, P * tt:P * tt + P], OT[:, U % 2, P * tt:P * tt + P],
                                  w("l0_wp" if UNITS[U][0] == 0 else "l1_wo"))
                    last.then_inc(made.sem, 1)
                elif k == "up":
                    h = s[1]
                    if h == 0:
                        pe.wait_ge(vz.sem, vz.after(1))
                    pe.wait_ge(modul.sem, modul.after(NTH["modulate", 2, h]))
                    for c in range(NCH):
                        pe.wait_ge(*last_read("up", NCH * h + c))
                        b = bank("up", NCH * h + c)
                        mm(b[:, :], w("l1_w1", P * c, P), HTb[:, half(h)]).then_inc(made.sem, 1)
                elif k == "down":
                    h = s[1]
                    pe.wait_ge(*last_read("down", h))
                    b = bank("down", h)
                    pe.wait_ge(gelu.sem, gelu.after(NCH * h + NCH - 1))
                    for t in range(4):
                        for c in range(NCH):
                            t0 = HT * h + P * t
                            last = mm(b[:, P * t:P * t + P], HIDb[:, c, t0:t0 + P], w("l1_w2", P * c, P),
                                      c == 0, c == NCH - 1)
                    last.then_inc(made.sem, 1)
                elif k == "nodes":
                    h = s[1]
                    pe.wait_ge(*last_read("xT", h))
                    b = bank("xT", h)
                    pe.wait_ge(xm_r.sem, xm_r.after(h))
                    turn4(b, lambda i: X[:, 4 * h + i, :]).then_inc(made.sem, 1)
                    pe.wait_ge(*last_read("nz", h))
                    b = bank("nz", h)
                    pe.wait_ge(nz_r.sem, nz_r.after(h))
                    for t in range(4):
                        last = mm(b[:, P * t:P * t + P], NZ[:, h, 1, t:t + 1].broadcast_to([P, P]), ident)
                    last.then_inc(made.sem, 1)
                elif k == "self":
                    h = s[1]
                    if h == 0:
                        pe.wait_ge(load_l2.sem, load_l2.after())
                    pe.wait_ge(*last_read("self", h))
                    b = bank("self", h)
                    pe.wait_ge(xT_r.sem, xT_r.after(h))
                    mm(b[:, :], w("l2_ws1"), TM[:, 0, half(h)], True, False)
                    pe.wait_ge(qe_r.sem, qe_r.after(h))
                    mm(b[:, :], w("l2_ws2"), HTb[:, half(h)], False, True).then_inc(made.sem, 1)
                elif k == "back":
                    h = s[1]
                    pe.wait_ge(*last_read("back", h))
                    b = bank("back", h)
                    pe.wait_ge(rel_r.sem, rel_r.after(2 * h + 1))
                    turn4(b, lambda i: ACC[:, HT * h + P * i:HT * h + P * i + P]).then_inc(made.sem, 1)
                elif k == "qkv3":
                    t = s[1]
                    if t % 4 == 0:
                        pe.wait_ge(h3_r.sem, h3_r.after(t // 4))
                    if t == 0:
                        pe.wait_ge(wc_r.sem, wc_r.after())
                    src = HTb[:, P * t:P * t + P]
                    for i in range(4):
                        pe.wait_ge(*last_read("qk3", 4 * t + i))
                        b = bank("qk3", 4 * t + i)
                        mm(b[:, :], src, w("l3_wqkv", 512 * i, 512)).then_inc(made.sem, 1)
                    for i in range(2):
                        pe.wait_ge(*last_read("v3", 2 * t + i))
                        b = bank("v3", 2 * t + i)
                        mm(b[:, :], src, w("l3_wqkv", 2048 + 512 * i, 512)).then_inc(made.sem, 1)
                elif k == "qkT3":
                    t = s[1]
                    for i in range(4):
                        n = 4 * t + i
                        pe.wait_ge(*last_read("qkT3", n))
                        b = bank("qkT3", n)
                        pe.wait_ge(qn_r.sem, qn_r.after(n))
                        turn4(b, lambda c: QN3[:, n % 4, P * c:P * c + P]).then_inc(made.sem, 1)
                elif k == "scores3":
                    t = s[1]
                    U = NUNIT + t
                    if t == 0:
                        pe.wait_ge(masked.sem, masked.after(NUNIT - 5))
                    else:
                        pe.wait_ge(ssub.sem, ssub.after(U - 1))
                    pe.wait_ge(qk_r.sem, qk_r.after(4 * t + 3))
                    for c in range(8):
                        for j in range(BPT):
                            for r in range(2):
                                rows = slice(HD3 * r, HD3 * r + HD3)
                                last = mm(Sps[S * j:S * j + S, r, S * c:S * c + S],
                                          QK3[rows, t % 2, 0, c, S * j:S * j + S],
                                          QK3[rows, t % 2, 1, c, S * j:S * j + S])
                    last.then_inc(s_made.sem, 1)
                elif k == "weigh3":
                    t = s[1]
                    pe.wait_ge(v3_r.sem, v3_r.after(2 * t + 1))
                    pe.wait_ge(pb_r.sem, pb_r.after(t))
                    for i in range(2):
                        pe.wait_ge(*last_read("o3", 2 * t + i))
                        b = bank("o3", 2 * t + i)
                        for c in range(4 * i, 4 * i + 4):
                            for r in range(2):
                                last = mm(b[HD3 * r:HD3 * r + HD3, P * (c % 4):P * (c % 4) + P],
                                          V3[:, t % 2, HD3 * (2 * c + r):HD3 * (2 * c + r) + HD3],
                                          PBD[:, t % 2, 8 * r + c, :])
                        last.then_inc(made.sem, 1)
                elif k == "out3":
                    t = s[1]
                    pe.wait_ge(*last_read("y3", t))
                    b = bank("y3", t)
                    pe.wait_ge(o3_r.sem, o3_r.after(2 * t + 1))
                    for c in range(8):
                        last = mm(b[:, 0:D], OT3[:, t % 2, c, :], w("l3_wout", P * c, P), c == 0, c == 7)
                    last.then_inc(made.sem, 1)
                elif k == "tokT":
                    h = s[1]
                    pe.wait_ge(*last_read("tokT", h))
                    b = bank("tokT", h)
                    pe.wait_ge(x3_r.sem, x3_r.after(4 * h + 3))
                    turn4(b, lambda i: X[:, 4 * h + i, :]).then_inc(made.sem, 1)
                elif k == "route":
                    pe.wait_ge(*last_read("logit"))
                    b = bank("logit")
                    pe.wait_ge(tt_r.sem, tt_r.after(1))
                    for t in range(NT):
                        last = mm(b[:, NE * t:NE * t + NE], TOKT[:, P * t:P * t + P], w("l3_gate"))
                    last.then_inc(made.sem, 1)
                    for i in range(2):
                        pe.wait_ge(*last_read("gates", i))
                        b = bank("gates", i)
                        pe.wait_ge(rt.sem, RT_GATE + 1)
                        turn4(b, lambda t: JUNK[:, P * (4 * i + t):P * (4 * i + t) + P]).then_inc(made.sem, 1)
                    for i in range(ROUNDS):
                        pe.wait_ge(rt.sem, RT_ROUND[i] + 3)
                        mm(Sps[:, 0, 0:1], konst("group16"), RT[:, 1:2]).then_inc(cnt.sem, 1)
                    pe.wait_ge(*last_read("thr"))
                    b = bank("thr")
                    pe.wait_ge(rt.sem, RT_ROUND[ROUNDS])
                    pe.transpose(b[:, 0:P], RTI[:, 0:1].bitcast(F32).broadcast_to([P, P]), ident).then_inc(made.sem, 1)
                    pe.wait_ge(*last_read("prefix"))
                    b = bank("prefix")
                    pe.wait_ge(rt.sem, RT_EQ)
                    flags = RGB[:, 0:2, :].rearrange("p i (t e) -> p i t e", e=NE)
                    o = b[:, 0:2 * NT * NE].rearrange("p (i t e) -> p i t e", i=2, e=NE)
                    mm(b[:, 0:2 * NT * NE], konst_b("before"), RGB[:, 0:2, :], True, False)
                    for t in range(NT - 1):
                        for i in range(2):
                            last = mm(o[:, i, t + 1:NT, :], konst_b("ones"), stack(flags[:, i, t, :], NT - 1 - t),
                                      False, t == NT - 2 and i == 1)
                    last.then_inc(made.sem, 1)
                    pe.wait_ge(*last_read("total"))
                    b = bank("total")
                    for t in range(NT):
                        last = mm(b[:, 0:NE], konst_b("ones"), flags[:, 0, t, :], t == 0, t == NT - 1)
                    last.then_inc(made.sem, 1)
                elif k == "experts":
                    def pos_T(i):
                        pe.wait_ge(*last_read("posT", i))
                        b = bank("posT", i)
                        for t in range(4):
                            at = NE * (4 * (i % 2) + t) + i // 2
                            last = mm(b[:, P * t:P * t + P], RGB[:, 2, at:at + 1].broadcast_to([P, P]),
                                      konst_b("ident"))
                        last.then_inc(made.sem, 1)

                    pe.wait_ge(rt.sem, RT_POS)
                    n_posT = 0
                    for _ in range(4):
                        pos_T(n_posT)
                        n_posT += 1
                    pe.wait_ge(xs_v.sem, xs_v.after(1))
                    pe.wait_ge(xs_a.sem, xs_a.after(1))
                    for i in range(2):
                        pe.wait_ge(*last_read("gather", i))
                        b = bank("gather", i)
                        for t in range(NT):
                            if i == 0:
                                pe.wait_ge(pic_v.sem, pic_v.after(t))
                            for c in range(3):
                                last = mm(b[:, :], XSP[:, t, c, :], PIC[:, t, 512 * i:512 * i + 512],
                                          t == 0 and c == 0, t == NT - 1 and c == 2)
                        last.then_inc(made.sem, 1)
                    pe.wait_ge(*last_read("weight"))
                    b = bank("weight")
                    pe.wait_ge(rt.sem, RT_SPLIT)
                    for e in range(NE):
                        for t in range(NT):
                            last = mm(b[:, 3 * e:3 * e + 3], PIC[:, t, CAP * e:CAP * e + CAP],
                                      RGB[:, 3:6, NE * t + e], t == 0, t == NT - 1)
                    last.then_inc(made.sem, 1)
                    pe.wait_ge(load_fc.sem, load_fc.after())
                    for e in range(NE + 1):
                        if e < NE:
                            pe.wait_ge(*last_read("fc1", e))
                            b = bank("fc1", e)
                            pe.wait_ge(gt_r.sem, gt_r.after(e // 4))
                            for c in range(NCH):
                                last = mm(b[:, P * c:P * c + P], w("fc1", HID * e + P * c, P),
                                          GTT[:, CAP * e:CAP * e + CAP])
                            last.then_inc(made.sem, 1)
                        for _ in range(3 * (e % 2)):
                            pos_T(n_posT)
                            n_posT += 1
                        if e:
                            f = e - 1
                            pe.wait_ge(*last_read("fc2", f))
                            b = bank("fc2", f)
                            pe.wait_ge(he_r.sem, he_r.after(f))
                            for c in range(NCH):
                                last = mm(b[:, 0:D], HE[:, f % 2, c, :], w("fc2", HID * f + P * c, P),
                                          c == 0, c == NCH - 1)
                            last.then_inc(made.sem, 1)
                    for h in range(2):
                        pe.wait_ge(*last_read("scatter", h))
                        b = bank("scatter", h)
                        pe.wait_ge(pict_r.sem, pict_r.after(15))
                        pe.wait_ge(y_r.sem, y_r.after(NE - 1))
                        for t in range(4):
                            for e in range(NE):
                                for c in range(3):
                                    t0 = HT * h + P * t
                                    last = mm(b[:, P * t:P * t + P], PICT[:, e, t0:t0 + P], YSP[:, e, c, :],
                                              e == 0 and c == 0, e == NE - 1 and c == 2)
                        last.then_inc(made.sem, 1)


def heads_cgf(a):
    return np.ascontiguousarray(a.reshape(NG, NC, HD, -1).transpose(1, 0, 2, 3)).reshape(D, -1)


def pack(parts, pieces):
    for name, n in parts:
        assert pieces[name].shape[1] == n, (name, pieces[name].shape)
    return np.ascontiguousarray(np.concatenate([pieces[name] for name, _ in parts], axis=1))


def packed_inputs(v):
    def T(a):
        return a.T

    def chunks(a):
        return a.reshape(-1, P, a.shape[1]).transpose(1, 0, 2).reshape(P, -1)

    def column(a):
        return a.reshape(-1, P).T

    qkv0 = v["L0_cond_Wqkv"].reshape(D, 3, D)
    bqkv0 = v["L0_cond_bqkv"].reshape(D, 3)
    weights = {
        "condT": T(v["cond_1024"]), "l0_wg": T(v["L0_cond_Wg"]), "l0_wb": T(v["L0_cond_Wb"]),
        "l1_ad1": T(v["L1_cond_w_adaln1"]), "l1_ad2": T(v["L1_cond_w_adaln2"]), "l3_ada": T(v["L3_cond_W_ada"]),
        "l0_wq": T(qkv0[:, 0]), "l0_wk": T(qkv0[:, 1]), "l0_wv": T(heads_cgf(qkv0[:, 2])), "l0_wp": T(v["L0_cond_Wp"]),
        "l1_wq": T(v["L1_cond_wq"]), "l1_wk": T(v["L1_cond_wk"]), "l1_wv": T(heads_cgf(v["L1_cond_wv"])),
        "l1_wo": T(v["L1_cond_wo"]), "l1_w1": T(v["L1_cond_w1"]), "l1_w2": chunks(T(v["L1_cond_w2"])),
        "l2_ws1": T(v["L2_cond_W_self"][:, :D]), "l2_ws2": T(v["L2_cond_W_self"][:, D:]),
        "l3_wqkv": T(v["L3_cond_Wqkv"]), "l3_wout": chunks(T(v["L3_cond_Wout"])), "l3_gate": T(v["L3_cond_Wgate"]),
        "fc1": v["L3_cond_fc1s"].transpose(2, 0, 1).reshape(D, -1),
        "fc2": v["L3_cond_fc2s"].reshape(NE, D, NCH, P).transpose(3, 0, 2, 1).reshape(P, -1),
    }
    for d in range(2):
        weights[f"l2_wq{d}"] = T(v["L2_cond_Wq"][d])
        weights[f"l2_wk{d}"] = T(v["L2_cond_Wk"][d])
        weights[f"l2_wv{d}"] = T(heads_cgf(v["L2_cond_Wout"][d].reshape(D, D)))
    twice = lambda a: np.concatenate([a, a])
    columns = {
        "ln_g": v["L0_cond_ln_g"], "ln_b": v["L0_cond_ln_b"], "bg": v["L0_cond_bg"], "bb": v["L0_cond_bb"],
        "bq0": bqkv0[:, 0], "bk0": bqkv0[:, 1], "bv0": bqkv0[:, 2],
        "ad1": v["L1_cond_b_adaln1"], "ad2": v["L1_cond_b_adaln2"], "bq1": v["L1_cond_bq"], "bk1": v["L1_cond_bk"],
        "bv1": v["L1_cond_bv"], "b1": v["L1_cond_b1"], "bself": v["L2_cond_b_self"],
        "bq2": v["L2_cond_bq"][0], "bq3": v["L2_cond_bq"][1], "bk2": v["L2_cond_bk"][0], "bk3": v["L2_cond_bk"][1],
        "bo2": v["L2_cond_bout"][0], "bo3": v["L2_cond_bout"][1],
        "b_ada": v["L3_cond_b_ada"], "ln1_g": v["L3_cond_ln1_g"], "ln1_b": v["L3_cond_ln1_b"],
        "qn_g": twice(v["L3_cond_qn_g"]), "qn_b": twice(v["L3_cond_qn_b"]),
        "kn_g": twice(v["L3_cond_kn_g"]), "kn_b": twice(v["L3_cond_kn_b"]),
        "mlp_g": v["L3_cond_mlp_g"], "mlp_b": v["L3_cond_mlp_b"], "b1s": v["L3_cond_b1s"].reshape(-1),
    }
    rows = {
        "bp": v["L0_cond_bp"], "bo": v["L1_cond_bo"], "b2": v["L1_cond_b2"], "w_bias": v["L2_cond_w_bias"],
        "b_bias": v["L2_cond_b_bias"].reshape(1), "b2s": v["L3_cond_b2s"].reshape(-1),
    }
    return (pack(W_PARTS, weights), pack(C_PARTS, {n: column(a) for n, a in columns.items()}),
            pack(R_PARTS, {n: a.reshape(1, -1) for n, a in rows.items()}))


def constants():
    p = np.arange(P)
    eye = np.eye(P, dtype=np.float32)
    k = {
        "ident": eye, "head_mask": (p[:, None] // HD % NC == np.arange(NC)).astype(np.float32),
        "iota_row": np.broadcast_to(p, (P, P)).astype(np.float32), "iota_col": p[:, None].astype(np.float32),
        "group16": (p[:, None] // 16 == p // 16).astype(np.float32), "mhalf": np.full((P, 32), -0.5, np.float32),
    }
    kb = {"ident": eye, "before": (p[:, None] < p).astype(np.float32), "ones": np.ones((P, P), np.float32)}
    ki = np.stack([(p % 16) << s if s < 28 else np.where(p % 16 < 4, (p % 16) << s, 0x7F000000) for s in SHIFTS], 1)
    return pack(K_PARTS, k), pack(KB_PARTS, kb), ki.astype(np.int32)


def kernel(**inputs):
    import ml_dtypes
    import concourse.bacc as bacc
    from concourse.bass_utils import run_bass_kernel_spmd

    v = {n: np.asarray(a) for n, a in inputs.items()}
    w, c, r = packed_inputs(v)
    k, kb, ki = constants()
    pad = v["mask_BxS_bf0"].reshape(NT, BPT, 1, S)
    pad = np.ascontiguousarray(np.broadcast_to(pad, (NT, BPT, S, S)).reshape(NT, P, S).transpose(1, 0, 2))
    arrays = {
        "x": np.ascontiguousarray(v["x"]), "weights": w, "columns": c, "rows": r, "constants": k,
        "constants_bf16": kb.astype(ml_dtypes.bfloat16), "candidates": ki, "padding": pad,
        "adjacency": np.ascontiguousarray(v["mask_BxSxSx11_ik0"]),
    }
    nc = bacc.Bacc("TRN2", target_bir_lowering=False, num_devices=1)
    aps = [nc.dram_tensor(f"{n}_in", a.shape, U8 if a.dtype == bool else mybir.dt.from_np(a.dtype),
                          kind="ExternalInput").ap()
           for n, a in arrays.items()]
    out = nc.dram_tensor("result", (B, S, D), F32, kind="ExternalOutput").ap()
    conditional_blocks(nc, *aps, out)
    r = run_bass_kernel_spmd(nc, [{f"{n}_in": a for n, a in arrays.items()}], core_ids=[0])
    return r.results[0]["result"]
```

```python
from contextlib import ExitStack
from itertools import count

import numpy as np
import concourse.bass as bass
from concourse import mybir

ALU = mybir.AluOpType
ACT = mybir.ActivationFunctionType
AX = mybir.AxisListType.X
F32 = mybir.dt.float32
BF16 = mybir.dt.bfloat16
I32 = mybir.dt.int32
U8 = mybir.dt.uint8

B, S, D, NH = 32, 32, 128, 16
P = 128
TOK = B * S
NT = TOK // P
BPT = P // S
HD = D // NH
NG = 4
NC = NH // NG
HT = TOK // 2
UT = 2 * P
NK2 = 20
NL = 11
HID = 512
NCH = HID // P
HD3 = 64
NE = 8
CAP = TOK // NE
EPS = 1e-5
NEG = -9000000000000000.0
BIG = 3.0e38

W_PARTS = [
    ("condT", B), ("l0_wg", D), ("l0_wb", D), ("l1_ad1", 2 * D), ("l1_ad2", 2 * D), ("l3_ada", D),
    ("l0_wq", D), ("l0_wk", D), ("l0_wv", D), ("l0_wp", D),
    ("l1_wq", D), ("l1_wk", D), ("l1_wv", D), ("l1_wo", D), ("l1_w1", HID), ("l1_w2", HID),
    ("l2_ws1", D), ("l2_ws2", D),
    ("l2_wq0", D), ("l2_wk0", D), ("l2_wv0", D), ("l2_wq1", D), ("l2_wk1", D), ("l2_wv1", D),
    ("l3_wqkv", 3 * NH * HD3), ("l3_wout", NH * HD3), ("l3_gate", NE), ("fc1", NE * HID), ("fc2", NE * HID),
]
C_PARTS = [
    ("ln_g", 1), ("ln_b", 1), ("bg", 1), ("bb", 1), ("bq0", 1), ("bk0", 1), ("bv0", 1),
    ("ad1", 2), ("ad2", 2), ("bq1", 1), ("bk1", 1), ("bv1", 1), ("b1", NCH),
    ("bself", 1), ("bq2", 1), ("bq3", 1), ("bk2", 1), ("bk3", 1), ("bo2", 1), ("bo3", 1),
    ("b_ada", 1), ("ln1_g", 1), ("ln1_b", 1), ("qn_g", 1), ("qn_b", 1), ("kn_g", 1), ("kn_b", 1),
    ("mlp_g", 1), ("mlp_b", 1), ("b1s", NE * NCH),
]
R_PARTS = [("bp", D), ("bo", D), ("b2", D), ("w_bias", NL), ("b_bias", 1), ("b2s", NE * D)]
K_PARTS = [("ident", P), ("head_mask", NC), ("group16", P), ("mhalf", 32)]
KB_PARTS = [("ident", P), ("before", P), ("ones", P), ("iota_row", P)]


def offsets(parts):
    at, out = 0, {}
    for name, n in parts:
        out[name] = (at, n)
        at += n
    return out, at


W_AT, W_N = offsets(W_PARTS)
C_AT, C_N = offsets(C_PARTS)
R_AT, R_N = offsets(R_PARTS)
K_AT, K_N = offsets(K_PARTS)
KB_AT, KB_N = offsets(KB_PARTS)
SHIFTS = [28, 24, 20, 16, 12, 8, 4, 0]
ROUNDS = len(SHIFTS)

UNITS = [(0, u) for u in range(4)] + [(1, u) for u in range(4)] + [(d, u) for u in range(4) for d in (2, 3)]
UNIT_AT = {cu: i for i, cu in enumerate(UNITS)}
NUNIT = len(UNITS)


NORMS = [(0, 0), (0, 1), (1, 0), (2, 0), (1, 1), (2, 1), (3, 0), (3, 1), (4, 0), (4, 1), (5, 0), (5, 1)]
NORM_AT = {lh: i for i, lh in enumerate(NORMS)}
PROJECTS = [(0, 0), (0, 1), (1, 0), (1, 1), (2, 0), (3, 0), (2, 1), (3, 1)]
PROJECT_AT = {ch: i for i, ch in enumerate(PROJECTS)}

def steps(text):
    out = []
    for word in text.split():
        kind, _, items = word.partition(":")
        first, _, last = (items or "0").partition("-")
        out += [(kind, i) for i in range(int(first), int(last or first) + 1)]
    return out


PE_STEPS = steps("""
    cond xnT:0 tokmod:0 k:0 q:0 v:0 xnT:1 scores:0 tokmod:1-2 q:1 scores:1 k:1 v:1 pt:0-1 scores:2 o:0 tokmod:3 y:0
    ada pt:2-3 scores:3 o:1 pt:4 y:1 pt:5 o:2 y:2 pt:6-7 o:3 xnT:2 y:3 q:2 k:2 v:2 scores:4 xnT:3 scores:5 k:3 q:3
    v:3 scores:6 pt:8-9 scores:7 o:4 pt:10-11 y:4 o:5 pt:12-13 y:5 o:6 pt:14-15 y:6 o:7 xnT:4 y:7 up:0-3 xnT:5
    down:0 up:4 xT:0 up:5-7 nz:0 down:1 self:0 xT:1 nz:1 k:4-5 q:4 v:4 scores:8 q:5 v:5 self:1 scores:9 k:6-7
    scores:10 q:6 pt:16-17 scores:11 v:6 o2:0 q:7 scores:12 pt:18-20 v:7 o2:1 pt:21-22 scores:13 pt:23 o2:2-3
    scores:14 pt:24-25 scores:15 o2:4 pt:26 back:0 pt:27-28 o2:5 pt:29 o2:6 pt:30-31 xnT3:0 o2:7 qk3:0 v3:0 qk3:1-3
    back:1 v3:1 qkT3:0 qk3:4 qkT3:1 qk3:5 qkT3:2 qk3:6 qkT3:3 qk3:7 qkT3:4 scores3:0 qk3:8 qkT3:5-6 xnT3:1 qk3:9
    qkT3:7 qk3:10 qkT3:8 qk3:11 scores3:1 qkT3:9 qk3:12-13 qkT3:10 qk3:14 qkT3:11 qk3:15 qkT3:12 scores3:2 qk3:16
    qkT3:13 qk3:17 qkT3:14 qk3:18 qkT3:15 qk3:19 qkT3:16 scores3:3 qkT3:17 qk3:20 qkT3:18 qk3:21-22 qkT3:19 qk3:23
    scores3:4 qkT3:20 qk3:24 qkT3:21 qk3:25 o3:0 qkT3:22-23 qk3:26-27 o3:1 v3:2 qkT3:24 qk3:28 scores3:5 qkT3:25
    o3:2 qk3:29 qkT3:26 qk3:30 qkT3:27 qk3:31 scores3:6 v3:3-5 o3:3 qkT3:28-29 v3:6-7 qkT3:30 y3:0 o3:4 y3:1 o3:5-6
    v3:8-9 o3:7 qkT3:31 y3:2 o3:8-9 v3:10 scores3:7 v3:11 y3:3-4 o3:10-11 v3:12-14 o3:12-13 y3:5 v3:15 o3:14-15
    tokT:0 y3:6-7 tokT:1 logit gates:0-1 counts:0-7 thr total prefix gather:0-5 pickT:0 gather:6-14 weight fc1:0
    gather:15 fc1:1 fc2:0 fc1:2 fc2:1 fc1:3 pickT:1-2 fc2:2 fc1:4 pickT:3-4 fc2:3 pickT:5 fc1:5 pickT:6-7 fc2:4
    scatter:0 fc1:6 pickT:8 fc2:5 pickT:9 fc1:7 pickT:10-12 fc2:6-7 pickT:13-15 scatter:1-3
""")
ACT_STEPS = steps("""
    silu tokmod:0 k:0 q:0 v:0 tokmod:1-2 exp:0 q:1 k:1 exp:1 pt:0-1 v:1 o:0 tokmod:3 exp:2 pt:2-3 o:1 exp:3 pt:4-5
    o:2 pt:6-7 o:3 q:2 k:2 v:2 exp:4 k:3 q:3 exp:5 v:3 pt:8-9 exp:6 o:4 pt:10-11 exp:7 o:5 pt:12-13 o:6 pt:14-15 o:7
    up:0-4 xT:0 up:5-7 self:0 xT:1 k:4 q:4 k:5 v:4 q:5 exp:8 v:5 self:1 k:6-7 exp:9 q:6 pt:16-17 exp:10 v:6 q:7
    exp:11 pt:18-20 v:7 pt:21 exp:12 pt:22-23 exp:13 pt:24-25 exp:14 pt:26 back:0 pt:27 exp:15 pt:28-31 square:0
    v3:0 square:1-3 back:1 v3:1 qkT3:0 square:4 qkT3:1 square:5 qkT3:2 square:6 qkT3:3 square:7 qkT3:4 square:8
    qkT3:5 exp:16 qkT3:6 square:9 qkT3:7 square:10 qkT3:8 square:11 qkT3:9 square:12-13 qkT3:10 square:14 exp:17
    qkT3:11 square:15 qkT3:12 square:16 qkT3:13 square:17 qkT3:14 exp:18 square:18 qkT3:15 square:19 qkT3:16-17
    square:20 qkT3:18 square:21 exp:19 square:22 qkT3:19 square:23 qkT3:20 square:24 qkT3:21 exp:20 square:25 o3:0
    qkT3:22-23 square:26-27 o3:1 v3:2 qkT3:24 square:28 qkT3:25 exp:21 o3:2 square:29 qkT3:26 square:30 qkT3:27
    square:31 v3:3-5 o3:3 qkT3:28-29 v3:6-7 qkT3:30 exp:22 o3:4-6 v3:8-9 o3:7 qkT3:31 o3:8-9 v3:10-11 exp:23
    o3:10-11 v3:12-14 o3:12-13 v3:15 o3:14-15 tokT:0 split:0 tokT:1 split:1-2 gexp split:3 gates:0-1 pickT:0
    gather:0 fc1:0 gather:1 fc1:1-3 pickT:1-2 fc1:4 pickT:3-6 fc1:5 pickT:7 fc1:6 pickT:8-9 fc1:7 pickT:10-15
""")
DVE_STEPS = steps("""
    stats:0-1 padding norm:0 cond columns modul:0 norm:1 edge:0-5 modul:1 less_max:0 edge:6 sum:0 edge:7 less_max:1
    edges center sum:1 silu less_max:2 y:0 ada sum:2 less_max:3 y:1 stats:2 sum:3 norm:2 remod:0 stats:3 y:2 norm:3
    modul:2 y:3 stats:4 norm:4 remod:1 stats:5 norm:5 mask:4 modul:3 less_max:4 mask:5 less_max:5 sum:4-5 mask:6
    less_max:6 sum:6 mask:7 less_max:7 y:4 sum:7 y:5 stats:6 y:6 norm:6 modul:4 y:7 stats:7 norm:7 modul:5 down:0
    nonzero:0 nz:0 down:1 nonzero:1 nz:1 mask:8 less_max:8 sum:8 mask:9 less_max:9 mask:10 less_max:10 mask:11
    sum:9-10 less_max:11 o2:0 sum:11 mask:12 less_max:12 o2:1 sum:12 mask:13 less_max:13 o2:2-3 mask:14 less_max:14
    sum:13-14 mask:15 less_max:15 o2:4 stats:8 sum:15 o2:5 norm:8 o2:6 modul3:0 o2:7 ss3:0-2 qk3:0 stats:9 qk3:1
    ss3:3 qk3:2 ss3:4 qk3:3 norm:9 qk3:4 ss3:5-7 qk3:5 less_max:16 qk3:6 ss3:8 qk3:7 sum:16 modul3:1 qk3:8 ss3:9
    blocks:0 ss3:10 qk3:9 ss3:11 less_max:17 qk3:10 ss3:12 qk3:11 ss3:13 qk3:12 ss3:14 sum:17 qk3:13 ss3:15 qk3:14
    less_max:18 ss3:16 blocks:1 qk3:15 ss3:17 qk3:16 sum:18 ss3:18 qk3:17 ss3:19 qk3:18 less_max:19 qk3:19 ss3:20-21
    sum:19 qk3:20 ss3:22-23 qk3:21 less_max:20 qk3:22 ss3:24 sum:20 qk3:23 ss3:25 qk3:24-25 ss3:26-27 blocks:2
    qk3:26 ss3:28 qk3:27 less_max:21 qk3:28 sum:21 ss3:29-31 qk3:29-31 blocks:3 less_max:22 y3:0 sum:22 y3:1
    blocks:4-5 y3:2 blocks:6 less_max:23 y3:3 stats:10 y3:4 sum:23 norm:10 blocks:7 y3:5-7 stats:11 split:0 norm:11
    split:1 logit split:2 softmax split_gates split:3 round:0 bits:0 round:1 bits:1 round:2 bits:2 round:3 bits:3
    round:4 bits:4 round:5 bits:5 round:6 bits:6 round:7 bits:7 flags slots pick:0-7 weight fc2:0-4 scatter:0
    fc2:5-7 scatter:1-3
""")
GP_STEPS = steps("""
    rstd:0-1 xb:0-1 divide:0 vzero center:0 divide:1 center:1 divide:2 rstd:2 xb:2 divide:3 rstd:3 xb:3 rstd:4 xb:4
    rstd:5 xb:5 divide:4-7 pzero:0 rstd:6 xb:6 pzero:1-2 rstd:7 xb:7 divide:8-14 rstd:8 divide:15 bzero rstd3:0-3
    rstd:9 rstd3:4-8 divide:16 rstd3:9-15 divide:17 rstd3:16-19 divide:18 rstd3:20-23 divide:19 rstd3:24-25
    divide:20 rstd3:26-28 divide:21 rstd3:29-31 divide:22 rstd:10 divide:23 rstd:11
""")


def conditional_blocks(nc, x_d, w_d, c_d, r_d, k_d, kb_d, ki_d, mask_d, adj_d, out_d):
    with ExitStack() as ctx:
        def sb(name, shape, dt=F32):
            return ctx.enter_context(nc.sbuf_tensor(name, shape, dt))

        def psum(name, shape, dt=F32):
            return ctx.enter_context(nc.psum_tensor(name, shape, dt))

        class Signal:

            def __init__(self, name, per=1):
                self.sem = ctx.enter_context(nc.semaphore(name))
                self.per = per

            def after(self, item=0, part=None):
                return self.per * item + (self.per if part is None else part)

        W = sb("W", [P, W_N])
        COL = sb("COL", [P, C_N])
        ROW = sb("ROW", [P, R_N])
        K = sb("K", [P, K_N])
        KB = sb("KB", [P, KB_N], BF16)
        KI = sb("KI", [P, ROUNDS], I32)
        PADM = sb("PADM", [P, NT, S], U8)
        X = sb("X", [P, NT, D])
        XB = sb("XB", [P, NT, D])
        XN = sb("XN", [P, NT, D])
        HTb = sb("HTb", [P, TOK])
        QT = sb("QT", [P, 2, TOK])
        REG = sb("REG", [P, 16384])
        PR = sb("PR", [P, 3, NG, 2 * NC, S])
        PTS = sb("PTS", [P, 2, 2, NG, P])
        OT = sb("OT", [P, 2, UT])
        TM = sb("TM", [P, 2, TOK])
        ACC = sb("ACC", [P, TOK])
        PAD = sb("PAD", [P, NT, S])
        PA = sb("PA", [P, NT])
        EM = sb("EM", [P, 2, NT, S])
        EB = sb("EB", [P, 2, NT, S])
        CM = sb("CM", [P, 7, B])
        CS = sb("CS", [P, 3, B])
        KM = sb("KM", [P, 4, NC])
        SC = sb("SC", [P, 8])
        ST = sb("ST", [P, 2, 4, 6])
        MV = sb("MV", [P, 2, 4, 2])
        RSTD = sb("RSTD", [P, 2, 2, 4])
        MX = sb("MX", [P, 2, 2 * NH])
        SM = sb("SM", [P, 2, 2 * NH])
        RS = sb("RS", [P, 2, 2 * NH])
        NZ = sb("NZ", [P, 2, 2, 4])
        SS3 = sb("SS3", [P, 4, 3, 8])
        WS = sb("WS", [P, 2 * NH])

        Sps = psum("Sps", [P, NG, 512])
        RB = [psum(f"RB{i}", [P, 512]) for i in range(4)]

        KBLK = [REG[:, 4096 * i:4096 * (i + 1)].rearrange("p (c t) -> p c t", c=NC) for i in (0, 2)]
        VBLK = [REG[:, 4096 * i:4096 * (i + 1)].rearrange("p (b g c f) -> p b g c f", g=NG, c=NC, f=HD)
                for i in (1, 3)]
        ADJ = REG[:, 8192:8192 + NT * S * NL].bitcast(I32).rearrange("p (t m l) -> p t m l", m=S, l=NL)
        ADW = REG[:, 8192 + NT * S * NL:8192 + 2 * NT * S * NL].rearrange("p (t m l) -> p t m l", m=S, l=NL)
        HIDb = REG[:, 8192:8192 + NCH * TOK].rearrange("p (c t) -> p c t", c=NCH)
        QK3 = REG[:, 0:4096].rearrange("p (b k c t) -> p b k c t", b=2, k=2, c=8)
        PBD = REG[:, 4096:8192].rearrange("p (b h t) -> p b h t", b=2, h=NH)
        V3 = REG[:, 8192:10240].rearrange("p (b f) -> p b f", b=2)
        OT3 = REG[:, 10240:12288].rearrange("p (b c t) -> p b c t", b=2, c=8)
        QN3 = REG[:, 12288:14336].rearrange("p (i f) -> p i f", i=4)
        SQ3 = REG[:, 14336:15360].rearrange("p (i f) -> p i f", i=2)
        PIC = REG[:, 0:4096].bitcast(BF16).rearrange("p (t s) -> p t s", t=NT)
        PICT = REG[:, 4096:8192].bitcast(BF16).rearrange("p (e t) -> p e t", e=NE)
        XSP = REG[:, 8192:9728].bitcast(BF16).rearrange("p (t k f) -> p t k f", t=NT, k=3)
        YSP = REG[:, 9728:11264].bitcast(BF16).rearrange("p (e k f) -> p e k f", e=NE, k=3)
        GTT = REG[:, 11264:12288]
        HE = REG[:, 12288:13312].rearrange("p (b c s) -> p b c s", b=2, c=NCH)
        GBC = REG[:, 13312:14336]
        JUNK = REG[:, 14336:15360]
        RES = REG[:, 15360:16384].rearrange("p (t f) -> p t f", t=NT)
        TOKT = XB[:, :, :].rearrange("p t f -> p (t f)")

        RG = sb("RG", [P, 12, NT * NE])
        RGB = sb("RGB", [P, 6, NT * NE], BF16)
        RT = sb("RT", [P, 16])
        RTI = sb("RTI", [P, 4], I32)
        YB = TM[:, 0, 0:4 * D].rearrange("p (b i f) -> p b i f", b=2, i=2)

        def w(name, a=0, n=None):
            o, size = W_AT[name]
            return W[:, o + a:o + a + (size - a if n is None else n)]

        def col(name, i=0):
            return COL[:, C_AT[name][0] + i:C_AT[name][0] + i + 1]

        def row(name, a=0, n=None):
            o, size = R_AT[name]
            return ROW[:, o + a:o + a + (size - a if n is None else n)]

        def konst(name):
            o, size = K_AT[name]
            return K[:, o:o + size]

        def konst_b(name):
            o, size = KB_AT[name]
            return KB[:, o:o + size]

        def spread(ap, n):
            return ap.unsqueeze(2).broadcast_to([ap.shape[0], ap.shape[1], n])

        def stack(ap, n):
            return ap.unsqueeze(1).broadcast_to([ap.shape[0], n, ap.shape[1]])

        ident = konst("ident")

        def last_norm(n):
            return max(m for m in range(n) if NORMS[m][1] == NORMS[n][1])

        def half(h):
            return slice(HT * h, HT * (h + 1))

        def tiles(h):
            return slice(4 * h, 4 * h + 4)

        n_first = 7
        load_first = Signal("load_first", 16 * n_first)
        load_x = Signal("load_x", 16)
        load_l0 = Signal("load_l0", 16)
        load_adj = Signal("load_adj", 16)
        load_l1 = Signal("load_l1", 16)
        load_l2 = Signal("load_l2", 16)
        load_l3 = Signal("load_l3", 16)
        load_fc = Signal("load_fc", 16)
        stored = Signal("stored", 32)
        silu_e = Signal("silu_exp")
        silu = Signal("silu", 3)
        cols_r = Signal("scaled_columns", 10)
        cond_r = Signal("modulation", 8)
        ada_r = Signal("shift3")
        tok_r = Signal("token_modulation")
        stats = Signal("stats", 8)
        rstd = Signal("rstd", 2)
        xb_r = Signal("residual_and_bias")
        normed = Signal("normed", 4)
        modul = Signal("modulated", 2)
        q_r = Signal("q_ready")
        k_r = Signal("kblk_ready", 4)
        v_r = Signal("vblk_ready", 4)
        vz = Signal("vblk_zero")
        prz = Signal("key_padding_zero")
        s_made = Signal("scores_made")
        masked = Signal("scores_masked", 2)
        biased = Signal("scores_biased", 2)
        smax = Signal("score_max")
        ssub = Signal("scores_less_max")
        expd = Signal("exp_done")
        ssum = Signal("exp_sum", 2)
        prob = Signal("probabilities")
        pt_r = Signal("probs_transposed")
        o_r = Signal("attention_out")
        x_r = Signal("residual_attention")
        tg_r = Signal("token_gamma")
        xg_r = Signal("residual_remodulated")
        gelu = Signal("hidden")
        xm_r = Signal("residual_mlp")
        nz_r = Signal("nonzero_rows", 2)
        xT_r = Signal("xT_ready")
        qe_r = Signal("q_masked")
        self_r = Signal("self_feat")
        acc_r = Signal("direction_added")
        rel_r = Signal("relu_added")
        xk_r = Signal("residual_graph")
        edge = Signal("edge_steps")
        edge_w = Signal("edge_weights")
        wsum = Signal("weight_means", 2)
        wc_r = Signal("centered_weights", 2)
        h3_r = Signal("modulated3")
        sq_r = Signal("squares3")
        ss_r = Signal("square_sums3")
        r3_r = Signal("rstd3", 2)
        qn_r = Signal("normed3")
        qk_r = Signal("qkT3_ready")
        v3_r = Signal("v3_ready")
        pbz = Signal("prob_blocks_zero")
        pb_r = Signal("prob_blocks", 4)
        o3_r = Signal("attention_out3")
        x3_r = Signal("residual3")
        tt_r = Signal("tokT_ready")
        rt = Signal("routing_vector")
        rta = Signal("routing_scalar")
        gb_r = Signal("gates_spread")
        cnt = Signal("counts_summed")
        pic_v = Signal("picks_vector")
        pict_r = Signal("picksT")
        sg_r = Signal("gates_split", 5)
        wt_r = Signal("slot_weights")
        xs_a = Signal("split_scalar", 2)
        xs_v = Signal("split_vector", 2)
        g_made = Signal("gather_made")
        gt_r = Signal("gathered")
        he_r = Signal("expert_hidden", NCH)
        y_r = Signal("expert_out", 6)
        res_r = Signal("result")

        RT_LOGIT = 2
        RT_GATE = 5
        RT_ROUND = [RT_GATE + 2 + 5 * k for k in range(ROUNDS + 1)]
        RT_EQ = RT_ROUND[ROUNDS] + 2
        RT_NEED = RT_EQ + 1
        RT_PREFIX = RT_EQ + 6
        RT_POS = RT_EQ + 9

        TAKEN = {
            "cond": (cond_r, lambda i: 7), "ada": (ada_r, lambda i: 1), "tokmod": (tok_r, None),
            "xnT": (modul, lambda i: 2 * i + 1), "xnT3": (h3_r, None), "q": (q_r, None), "k": (k_r, None),
            "v": (v_r, None), "pt": (pt_r, None), "o": (o_r, None), "o2": (acc_r, None), "y": (x_r, None),
            "up": (gelu, None), "down": (xm_r, None), "xT": (xT_r, None), "nz": (qe_r, None), "self": (self_r, None),
            "back": (xk_r, None), "qk3": (qn_r, None), "v3": (v3_r, None), "qkT3": (qk_r, None),
            "o3": (o3_r, None), "y3": (x3_r, None), "tokT": (tt_r, None),
            "logit": (rt, lambda i: RT_LOGIT), "gates": (gb_r, None), "thr": (rt, lambda i: RT_EQ),
            "prefix": (rt, lambda i: RT_PREFIX), "total": (rt, lambda i: RT_NEED), "pickT": (pict_r, None),
            "weight": (wt_r, None), "fc1": (he_r, None),
            "fc2": (y_r, lambda i: 6 * i + 1), "scatter": (res_r, None),
        }
        made = Signal("bank_made")

        RING_ORDER = [(kind, i) for kind, i in PE_STEPS if kind in TAKEN]
        RING_AT = {key: n for n, key in enumerate(RING_ORDER)}
        n_small = RING_AT["qk3", 0]
        small = [n % len(RB) for n in range(n_small)]
        cycle = [4, 5] + [(n_small + i) % len(RB) for i in range(len(RB))]
        BANK_OF = small + [cycle[n % len(cycle)] for n in range(len(RING_ORDER) - n_small)]
        BANKS = [RB[i][:, :] for i in range(len(RB))] + [Sps[:, 2, :], Sps[:, 3, :]]

        def bank(kind, item=0):
            return BANKS[BANK_OF[RING_AT[kind, item]]]

        def count_made(kind, item=0):
            return RING_AT[kind, item] + 1

        def used_before(kind, item=0):
            n = RING_AT[kind, item]
            return BANK_OF[n] in BANK_OF[:n] or BANK_OF[n] >= len(RB)

        def last_read(kind, item=0):
            n = RING_AT[kind, item]
            before = [m for m in range(n) if BANK_OF[m] == BANK_OF[n]]
            if not before:
                return masked.sem, masked.after(NUNIT - 5)
            kind, i = RING_ORDER[before[-1]]
            signal, value = TAKEN[kind]
            return signal.sem, value(i) if value else signal.after(i)

        block = ctx.enter_context(nc.Block())

        @block.sync
        def _(sp):
            def load_w(first, last, signal):
                a, b = W_AT[first][0], W_AT[last][0] + W_AT[last][1]
                sp.dma_start(W[:, a:b], w_d[:, a:b]).then_inc(signal.sem, 16)

            xv = x_d.rearrange("b s d -> (b s) d").rearrange("(t p) d -> p t d", p=P)
            sp.dma_start(X[:, :, :], xv).then_inc(load_x.sem, 16)
            load_w("condT", "l3_ada", load_first)
            sp.dma_start(COL[:, :], c_d).then_inc(load_first.sem, 16)
            sp.dma_start(K[:, :], k_d).then_inc(load_first.sem, 16)
            load_w("l0_wq", "l0_wp", load_l0)
            sp.dma_start(ADJ, adj_d.rearrange("b n m l -> (b n) m l").rearrange("(t p) m l -> p t m l", p=P))\
              .then_inc(load_adj.sem, 16)
            load_w("l1_wq", "l1_w2", load_l1)
            load_w("l2_ws1", "l2_wv1", load_l2)
            load_w("l3_wqkv", "l3_gate", load_l3)
            load_w("fc1", "fc2", load_fc)
            ov = out_d.rearrange("b s d -> (b s) d").rearrange("(t p) d -> p t d", p=P)
            for h in range(2):
                sp.wait_ge(res_r.sem, res_r.after(2 + h))
                sp.dma_start(ov[:, tiles(h), :], RES[:, tiles(h), :]).then_inc(stored.sem, 16)
            sp.wait_ge(stored.sem, stored.after())

        @block.gpsimd
        def _(gp):
            gp.memset(VBLK[0], 0.0).then_inc(vz.sem, 1)
            XB_ADD = {0: "bp", 2: "bo", 3: "b2"}
            for k, n in GP_STEPS:
                if k == "rstd":
                    l, h = NORMS[n]
                    if n == 0:
                        gp.wait_ge(load_first.sem, load_first.after())
                    if n >= 2:
                        gp.wait_ge(normed.sem, normed.after(last_norm(n)))
                    gp.wait_ge(stats.sem, stats.after(n))
                    gp.tensor_scalar(RSTD[:, h, 0, :], MV[:, h, :, 1], EPS, None, ALU.add).then_inc(rstd.sem, 1)
                    gp.wait_ge(rstd.sem, rstd.after(n, 1))
                    gp.tensor_tensor(RSTD[:, h, 1, :], RSTD[:, h, 0, :], konst("mhalf")[:, 0:4], ALU.pow)\
                      .then_inc(rstd.sem, 1)
                elif k == "xb":
                    l, h = NORMS[n]
                    if n == 0:
                        gp.wait_ge(load_first.sem, load_first.after())
                    if l == 1:
                        gp.wait_ge(tok_r.sem, tok_r.after(2 + h))
                    add = TM[:, 1, half(h)].rearrange("p (t f) -> p t f", t=4) if l == 1 else stack(row(XB_ADD[l]), 4)
                    gp.wait_ge(stats.sem, stats.after(n))
                    gp.tensor_tensor(XB[:, tiles(h), :], X[:, tiles(h), :], add, ALU.add).then_inc(xb_r.sem, 1)
                elif k == "divide":
                    U = n
                    gp.wait_ge(ssum.sem, ssum.after(U))
                    if U < NUNIT:
                        m = S if UNITS[U][0] < 2 else NK2
                        pr = PR[:, U % 3].rearrange("p g x m -> p (g x) m")[:, :, 0:m]
                        gp.tensor_tensor(pr, pr, spread(RS[:, U % 2, :], m), ALU.mult).then_inc(prob.sem, 1)
                    else:
                        pr = PR[:, U % 3, 0:2].rearrange("p g x m -> p (g x) m")
                        gp.tensor_tensor(pr, pr, spread(RS[:, U % 2, 0:NH], S), ALU.mult).then_inc(prob.sem, 1)
                elif k == "vzero":
                    gp.wait_ge(edge.sem, edge.after(2 * NT + 2))
                    gp.memset(VBLK[1], 0.0).then_inc(vz.sem, 1)
                elif k == "center":
                    gp.wait_ge(wsum.sem, wsum.after())
                    v = w("l3_wqkv", 1024 * n, 1024).rearrange("p (h f) -> p h f", f=HD3)
                    gp.tensor_tensor(v, v, spread(WS[:, NH * n:NH * (n + 1)], HD3), ALU.add).then_inc(wc_r.sem, 1)
                elif k == "pzero":
                    gp.wait_ge(made.sem, count_made("pt", 2 * max(U for U in range(8) if U % 3 == n) + 1))
                    gp.memset(PR[:, n].rearrange("p g x m -> p (g x) m")[:, :, NK2:S], 0.0).then_inc(prz.sem, 1)
                elif k == "bzero":
                    gp.wait_ge(made.sem, count_made("o2", 6))
                    gp.memset(PBD, 0.0).then_inc(pbz.sem, 1)
                elif k == "rstd3":
                    gp.wait_ge(ss_r.sem, ss_r.after(n))
                    b = SS3[:, n % 4]
                    gp.tensor_scalar(b[:, 1, :], b[:, 0, :], 1.0 / HD3, EPS, ALU.mult, ALU.add)\
                      .then_inc(r3_r.sem, 1)
                    gp.wait_ge(r3_r.sem, r3_r.after(n, 1))
                    gp.tensor_tensor(b[:, 2, :], b[:, 1, :], konst("mhalf")[:, 0:8], ALU.pow)\
                      .then_inc(r3_r.sem, 1)
                else:
                    raise ValueError(k)

        @block.scalar
        def _(act):
            act.dma_start(ROW[:, :], r_d.broadcast_to([P, R_N])).then_inc(load_first.sem, 16)
            act.dma_start(KB[:, :], kb_d).then_inc(load_first.sem, 16)
            act.dma_start(KI[:, :], ki_d).then_inc(load_first.sem, 16)
            act.dma_start(PADM[:, :, :], mask_d).then_inc(load_first.sem, 16)
            q_scale = [1.0] + [HD ** -0.5] * 3
            q_bias = [col("bq0"), SC[:, 1:2], SC[:, 2:3], SC[:, 3:4]]
            for k, n in ACT_STEPS:
                if k == "silu":
                    act.wait_ge(load_first.sem, load_first.after())
                    act.activation(CS[:, 0, :], w("condT"), ACT.Exp, scale=-1.0).then_inc(silu_e.sem, 1)
                elif k == "tokmod":
                    act.wait_ge(made.sem, count_made("tokmod", n))
                    act.activation(TM[:, n // 2, half(n % 2)], bank("tokmod", n)[:, :], ACT.Copy)\
                       .then_inc(tok_r.sem, 1)
                elif k == "q":
                    call, h = PROJECTS[n]
                    if n == 0:
                        act.wait_ge(cols_r.sem, cols_r.after())
                    if n in (2, 3):
                        act.wait_ge(s_made.sem, s_made.after(2 * h + 1))
                    elif n in (4, 6):
                        act.wait_ge(s_made.sem, s_made.after(4 + 2 * h + 1))
                    act.wait_ge(made.sem, count_made("q", n))
                    act.activation(QT[:, call // 3, half(h)], bank("q", n)[:, :], ACT.Identity, bias=q_bias[call],
                                   scale=q_scale[call]).then_inc(q_r.sem, 1)
                elif k == "k":
                    call, h = PROJECTS[n]
                    if n == 5:
                        act.wait_ge(made.sem, count_made("down", 1))
                    elif n in (2, 3, 4, 6):
                        act.wait_ge(s_made.sem, s_made.after(4 * (call - 1) + 2 * h + 1))
                    act.wait_ge(made.sem, count_made("k", n))
                    for c in range(NC):
                        act.activation(KBLK[call // 3][:, c, half(h)], bank("k", n)[:, :], ACT.Identity,
                                       bias=KM[:, call, c:c + 1], scale=konst("head_mask")[:, c:c + 1])\
                           .then_inc(k_r.sem, 1)
                elif k == "v":
                    call, h = PROJECTS[n]
                    act.wait_ge(vz.sem, vz.after(call // 3))
                    if n in (2, 3, 4, 6):
                        act.wait_ge(made.sem, count_made("o", 4 * (call - 1) + 2 * h + 1))
                    act.wait_ge(made.sem, count_made("v", n))
                    for c in range(NC):
                        rows = slice(S * c, S * c + S)
                        act.activation(VBLK[call // 3][rows, 16 * h:16 * h + 16, :, c, :],
                                       bank("v", n)[rows, :].rearrange("p (b g f) -> p b g f", g=NG, f=HD), ACT.Copy)\
                           .then_inc(v_r.sem, 1)
                elif k == "exp":
                    U = n
                    m = NK2 if 8 <= U < NUNIT else S
                    pr = PR[:, U % 3, 0:4 if U < NUNIT else 2].rearrange("p g x m -> p (g x) m")[:, :, 0:m]
                    act.wait_ge(ssub.sem, ssub.after(U))
                    act.activation(pr, pr, ACT.Exp).then_inc(expd.sem, 1)
                elif k == "pt":
                    U, tt = n // 2, n % 2
                    if U >= 2 and tt == 0:
                        act.wait_ge(made.sem, count_made(*(("o", U - 2) if U - 2 < 8 else ("o2", U - 10))))
                    act.wait_ge(made.sem, count_made("pt", n))
                    act.activation(PTS[:, U % 2, tt].rearrange("p g t -> p (g t)"), bank("pt", n)[:, :],
                                   ACT.Copy).then_inc(pt_r.sem, 1)
                elif k == "o":
                    U = n
                    if U >= 2:
                        act.wait_ge(made.sem, count_made("y", U - 2))
                    act.wait_ge(made.sem, count_made("o", U))
                    act.activation(OT[:, U % 2, :], bank("o", U)[:, 0:UT], ACT.Identity,
                                   bias=SC[:, 0:1] if U < 4 else col("bv1"),
                                   scale=D ** -0.5 if U < 4 else 1.0).then_inc(o_r.sem, 1)
                elif k == "up":
                    h, c = n // NCH, n % NCH
                    act.wait_ge(made.sem, count_made("up", n))
                    act.activation(HIDb[:, c, half(h)], bank("up", n)[:, :], ACT.Gelu,
                                   bias=col("b1", c)).then_inc(gelu.sem, 1)
                elif k == "xT":
                    act.wait_ge(made.sem, count_made("xT", n))
                    act.activation(TM[:, 0, half(n)], bank("xT", n)[:, :], ACT.Copy).then_inc(xT_r.sem, 1)
                elif k == "self":
                    act.wait_ge(made.sem, count_made("self", n))
                    act.activation(TM[:, 1, half(n)], bank("self", n)[:, :], ACT.Identity, bias=col("bself"))\
                       .then_inc(self_r.sem, 1)
                elif k == "back":
                    act.wait_ge(made.sem, count_made("back", n))
                    act.activation(X[:, tiles(n), :].rearrange("p t f -> p (t f)"), bank("back", n)[:, :], ACT.Copy)\
                       .then_inc(xk_r.sem, 1)
                elif k == "square":
                    if n == 0:
                        act.wait_ge(made.sem, count_made("o2", 7))
                    if n >= 2:
                        act.wait_ge(ss_r.sem, ss_r.after(n - 2))
                    act.wait_ge(made.sem, count_made("qk3", n))
                    act.activation(SQ3[:, n % 2, :], bank("qk3", n)[:, :], ACT.Square).then_inc(sq_r.sem, 1)
                elif k == "v3":
                    t, i = n // 2, n % 2
                    if n == 0:
                        act.wait_ge(s_made.sem, s_made.after(NUNIT - 1))
                    if t >= 2:
                        act.wait_ge(made.sem, count_made("o3", 2 * (t - 2) + 1))
                    act.wait_ge(made.sem, count_made("v3", n))
                    act.activation(V3[:, t % 2, 512 * i:512 * i + 512], bank("v3", n)[:, :], ACT.Copy)\
                       .then_inc(v3_r.sem, 1)
                elif k == "qkT3":
                    t, i = n // 4, n % 4
                    if n == 0:
                        act.wait_ge(s_made.sem, s_made.after(NUNIT - 2))
                    if t >= 2:
                        act.wait_ge(s_made.sem, s_made.after(NUNIT + t - 2))
                    act.wait_ge(made.sem, count_made("qkT3", n))
                    act.activation(QK3[:, t % 2, i // 2, 4 * (i % 2):4 * (i % 2) + 4, :]
                                   .rearrange("p c t -> p (c t)"), bank("qkT3", n)[:, :], ACT.Identity,
                                   bias=SC[:, 5:6] if i < 2 else col("kn_b"),
                                   scale=SC[:, 4:5] if i < 2 else col("kn_g")).then_inc(qk_r.sem, 1)
                elif k == "o3":
                    t, i = n // 2, n % 2
                    if t >= 2:
                        act.wait_ge(made.sem, count_made("y3", t - 2))
                    act.wait_ge(made.sem, count_made("o3", n))
                    act.activation(OT3[:, t % 2, 4 * i:4 * i + 4, :].rearrange("p c t -> p (c t)"),
                                   bank("o3", n)[:, :], ACT.Copy).then_inc(o3_r.sem, 1)
                elif k == "split":
                    h, i = n // 2, n % 2
                    if i:
                        act.wait_ge(xs_v.sem, xs_v.after(h, 1))
                    else:
                        act.wait_ge(made.sem, count_made("y3", NT - 1))
                        act.wait_ge(normed.sem, normed.after(NORM_AT[5, h]))
                    act.activation(XSP[:, tiles(h), i, :], XN[:, tiles(h), :], ACT.Copy).then_inc(xs_a.sem, 1)
                elif k == "tokT":
                    act.wait_ge(made.sem, count_made("tokT", n))
                    act.activation(TOKT[:, half(n)], bank("tokT", n)[:, :], ACT.Copy).then_inc(tt_r.sem, 1)
                elif k == "gexp":
                    act.wait_ge(rt.sem, RT_LOGIT)
                    act.activation(RG[:, 1, :], RG[:, 0, :], ACT.Exp).then_inc(rta.sem, 1)
                elif k == "gates":
                    act.wait_ge(made.sem, count_made("gates", n))
                    act.activation(GBC[:, half(n)], bank("gates", n)[:, :], ACT.Copy).then_inc(gb_r.sem, 1)
                elif k == "pickT":
                    act.wait_ge(made.sem, count_made("pickT", n))
                    act.activation(PICT[:, n // 2, half(n % 2)], bank("pickT", n)[:, :], ACT.Copy)\
                       .then_inc(pict_r.sem, 1)
                elif k == "gather":
                    act.wait_ge(g_made.sem, g_made.after(n))
                    act.activation(GTT[:, 512 * n:512 * n + 512], Sps[:, n, :], ACT.Identity,
                                   bias=col("mlp_b"), scale=col("mlp_g")).then_inc(gt_r.sem, 1)
                elif k == "fc1":
                    e = n
                    if e >= 2:
                        act.wait_ge(made.sem, count_made("fc2", e - 2))
                    act.wait_ge(made.sem, count_made("fc1", e))
                    for c in range(NCH):
                        act.activation(HE[:, e % 2, c, :], bank("fc1", e)[:, P * c:P * c + P],
                                       ACT.Gelu_apprx_tanh, bias=col("b1s", NCH * e + c)).then_inc(he_r.sem, 1)
                else:
                    raise ValueError(k)

        @block.vector
        def _(dve):
            edge_steps, rt_steps = count(1), count(1)

            def edge_step():
                return next(edge_steps)

            def rt_step():
                return next(rt_steps)

            def te(a):
                return a.rearrange("p (t e) -> p t e", e=NE)

            gate = RG[:, 2, :]
            above, at_thr = (RGB[:, i, :] for i in range(2))
            for k, n in DVE_STEPS:
                if k == "columns":
                    dve.wait_ge(load_first.sem, load_first.after())
                    for call in range(4):
                        dve.tensor_scalar(KM[:, call, :], konst("head_mask"), col(f"bk{call}"), None, ALU.mult)\
                           .then_inc(cols_r.sem, 1)
                    for i, (c, scale) in enumerate([(col("bv0"), D ** -0.5), (col("bq1"), HD ** -0.5),
                                                    (col("bq2"), HD ** -0.5), (col("bq3"), HD ** -0.5),
                                                    (col("qn_g"), HD3 ** -0.5), (col("qn_b"), HD3 ** -0.5)]):
                        dve.tensor_scalar(SC[:, i:i + 1], c, scale, None, ALU.mult).then_inc(cols_r.sem, 1)
                elif k == "silu":
                    dve.wait_ge(silu_e.sem, silu_e.after())
                    dve.tensor_scalar(CS[:, 0, :], CS[:, 0, :], 1.0, None, ALU.add).then_inc(silu.sem, 1)
                    dve.wait_ge(silu.sem, silu.after(0, 1))
                    dve.reciprocal(CS[:, 0, :], CS[:, 0, :]).then_inc(silu.sem, 1)
                    dve.wait_ge(silu.sem, silu.after(0, 2))
                    dve.tensor_tensor(CS[:, 0, :], CS[:, 0, :], w("condT"), ALU.mult).then_inc(silu.sem, 1)
                elif k == "cond":
                    dve.wait_ge(made.sem, count_made("cond"))
                    m = bank("cond")[:, 0:6 * B].rearrange("p (i b) -> p i b", i=6)
                    dve.tensor_scalar(CM[:, 0, :], m[:, 0], col("bg"), col("ln_g"), ALU.add, ALU.mult)\
                       .then_inc(cond_r.sem, 1)
                    dve.tensor_scalar(CS[:, 1, :], m[:, 0], col("bg"), col("ln_b"), ALU.add, ALU.mult)\
                       .then_inc(cond_r.sem, 1)
                    dve.tensor_scalar(CS[:, 2, :], m[:, 1], col("bb"), None, ALU.add).then_inc(cond_r.sem, 1)
                    for i, name in ((2, "ad1"), (4, "ad2")):
                        dve.tensor_scalar(CM[:, i, :], m[:, i], col(name, 0), 1.0, ALU.add, ALU.add)\
                           .then_inc(cond_r.sem, 1)
                        dve.tensor_scalar(CM[:, i + 1, :], m[:, i + 1], col(name, 1), None, ALU.add)\
                           .then_inc(cond_r.sem, 1)
                    dve.wait_ge(cond_r.sem, cond_r.after(0, 7))
                    dve.tensor_tensor(CM[:, 1, :], CS[:, 1, :], CS[:, 2, :], ALU.add).then_inc(cond_r.sem, 1)
                elif k == "ada":
                    dve.wait_ge(made.sem, count_made("ada"))
                    dve.tensor_scalar(CM[:, 6, :], bank("ada")[:, 0:B], col("b_ada"), col("ln1_b"), ALU.add, ALU.add)\
                       .then_inc(ada_r.sem, 1)
                elif k == "stats":
                    l, h = NORMS[n]
                    if l == 0:
                        dve.wait_ge(load_x.sem, load_x.after())
                    elif l == 1:
                        dve.wait_ge(x_r.sem, x_r.after(2 * h + 1))
                    elif l == 2:
                        dve.wait_ge(xg_r.sem, xg_r.after(h))
                    elif l == 3:
                        dve.wait_ge(x_r.sem, x_r.after(4 + 2 * h + 1))
                    elif l == 4:
                        dve.wait_ge(xk_r.sem, xk_r.after(h))
                    else:
                        dve.wait_ge(x3_r.sem, x3_r.after(4 * h + 3))
                    for t in range(4):
                        dve.bn_stats(ST[:, h, t, :], X[:, 4 * h + t, :]).then_inc(stats.sem, 1)
                    for t in range(4):
                        dve.wait_ge(stats.sem, stats.after(n, 1 + t))
                        dve.bn_aggr(MV[:, h, t, :], ST[:, h, t, :]).then_inc(stats.sem, 1)
                elif k == "norm":
                    l, h = NORMS[n]
                    if l == 3:
                        dve.wait_ge(modul.sem, modul.after(2 + h))
                    elif l == 4:
                        dve.wait_ge(modul.sem, modul.after(4 + h))
                    elif l == 5:
                        dve.wait_ge(h3_r.sem, h3_r.after(h))
                    elif l:
                        dve.wait_ge(modul.sem, modul.after(h))
                    dve.wait_ge(rstd.sem, rstd.after(n))
                    for t in range(4):
                        dve.tensor_scalar(XN[:, 4 * h + t, :], X[:, 4 * h + t, :], MV[:, h, t, 0:1],
                                          RSTD[:, h, 1, t:t + 1], ALU.subtract, ALU.mult).then_inc(normed.sem, 1)
                elif k == "modul":
                    m, h = n // 2, n % 2
                    if m == 1:
                        dve.wait_ge(made.sem, count_made("v", h))
                    elif m == 2:
                        dve.wait_ge(made.sem, count_made("v", 2 + h))
                    o = HTb[:, half(h)].rearrange("p (b q) -> p b q", q=S)
                    bs = slice(16 * h, 16 * h + 16)
                    dve.wait_ge(cond_r.sem, cond_r.after())
                    dve.wait_ge(made.sem, count_made("xnT", n))
                    dve.tensor_tensor(o, bank("xnT", n)[:, :].rearrange("p (b q) -> p b q", q=S),
                                      spread(CM[:, 2 * m, bs], S), ALU.mult).then_inc(modul.sem, 1)
                    dve.wait_ge(modul.sem, modul.after(n, 1))
                    dve.tensor_tensor(o, o, spread(CM[:, 2 * m + 1, bs], S), ALU.add).then_inc(modul.sem, 1)
                elif k == "modul3":
                    h = n
                    dve.wait_ge(made.sem, count_made("self", h))
                    dve.wait_ge(made.sem, count_made("xnT3", h))
                    dve.scalar_tensor_tensor(HTb[:, half(h)].rearrange("p (b q) -> p b q", q=S),
                                             bank("xnT3", h)[:, :].rearrange("p (b q) -> p b q", q=S), col("ln1_g"),
                                             spread(CM[:, 6, 16 * h:16 * h + 16], S), ALU.mult, ALU.add)\
                       .then_inc(h3_r.sem, 1)
                elif k == "remod":
                    h = n
                    dve.wait_ge(tok_r.sem, tok_r.after(h))
                    dve.wait_ge(normed.sem, normed.after(NORM_AT[1, h]))
                    xn = XN[:, tiles(h), :]
                    dve.tensor_tensor(xn, xn, TM[:, 0, half(h)].rearrange("p (t f) -> p t f", t=4), ALU.mult)\
                       .then_inc(tg_r.sem, 1)
                    dve.wait_ge(tg_r.sem, tg_r.after(h))
                    dve.wait_ge(xb_r.sem, xb_r.after(NORM_AT[1, h]))
                    dve.tensor_tensor(X[:, tiles(h), :], xn, XB[:, tiles(h), :], ALU.add).then_inc(xg_r.sem, 1)
                elif k == "padding":
                    dve.wait_ge(load_first.sem, load_first.after())
                    dve.tensor_reduce(PA[:, :], PADM[:, :, :], AX, ALU.min).then_inc(edge.sem, 1)
                    dve.wait_ge(edge.sem, edge_step())
                    dve.tensor_scalar(PA[:, :], PA[:, :], 1.0, -BIG, ALU.add, ALU.mult).then_inc(edge.sem, 1)
                    dve.wait_ge(edge.sem, edge_step())
                    dve.tensor_tensor(PAD[:, :, :], PADM[:, :, :], spread(PA[:, :], S), ALU.mult).then_inc(edge.sem, 1)
                    dve.wait_ge(edge.sem, edge_step())
                elif k == "edge":
                    dve.wait_ge(load_adj.sem, load_adj.after())
                    dve.tensor_tensor(ADW[:, n], ADJ[:, n], stack(row("w_bias"), S), ALU.mult).then_inc(edge_w.sem, 1)
                    dve.tensor_reduce(EM[:, 0, n, :], ADJ[:, n], AX, ALU.add).then_inc(edge.sem, 1)
                    edge_step()
                    dve.wait_ge(edge_w.sem, edge_w.after(n))
                    dve.tensor_reduce(EB[:, 0, n, :], ADW[:, n], AX, ALU.add).then_inc(edge.sem, 1)
                    edge_step()
                elif k == "edges":
                    dve.wait_ge(edge.sem, edge.after(2 * NT + 2))
                    cond = EM[:, 0].rearrange("p t m -> p (t m)")
                    bias = EB[:, 0].rearrange("p t m -> p (t m)")
                    dve.tensor_scalar(EM[:, 0], EM[:, 0], 0.0, None, ALU.is_gt).then_inc(edge.sem, 1)
                    dve.wait_ge(edge.sem, edge_step())
                    dve.tensor_scalar(EB[:, 0], EB[:, 0], row("b_bias"), None, ALU.add).then_inc(edge.sem, 1)
                    dve.wait_ge(edge.sem, edge_step())
                    dve.tensor_scalar(EM[:, 1], EM[:, 0], -NEG, NEG, ALU.mult, ALU.add).then_inc(edge.sem, 1)
                    dve.wait_ge(edge.sem, edge_step())
                    dve.tensor_tensor(EB[:, 0], EB[:, 0], EM[:, 1], ALU.add).then_inc(edge.sem, 1)
                    dve.wait_ge(edge.sem, edge_step())
                    dve.transpose(EM[:, 1].rearrange("p t m -> p (t m)"), cond).then_inc(edge.sem, 1)
                    dve.wait_ge(edge.sem, edge_step())
                    dve.transpose(EB[:, 1].rearrange("p t m -> p (t m)"), bias).then_inc(edge.sem, 1)
                    dve.wait_ge(edge.sem, edge_step())
                elif k == "mask" and n < 8:
                    U, u = n, n - 4
                    dve.wait_ge(made.sem, count_made("pt", 2 * (U - 3) + 1))
                    dve.wait_ge(edge.sem, edge.after(2))
                    dve.wait_ge(s_made.sem, s_made.after(U))
                    for tt in range(2):
                        pad = PAD[:, 2 * u + tt, :].unsqueeze(1).unsqueeze(1).broadcast_to([P, NG, NC, S])
                        xs = slice(NC * tt, NC * tt + NC)
                        sc = Sps[:, :, P * tt:P * tt + P].rearrange("p g (x m) -> p g x m", m=S)
                        dve.tensor_tensor(PR[:, U % 3, :, xs, :], sc, pad, ALU.add).then_inc(masked.sem, 1)
                elif k == "mask":
                    U = n
                    call, u = UNITS[U]
                    dve.wait_ge(made.sem, count_made("pt", 2 * (U - 3) + 1))
                    dve.wait_ge(prz.sem, prz.after(2))
                    dve.wait_ge(s_made.sem, s_made.after(U))
                    dve.wait_ge(edge.sem, edge.after(2 * NT + 8))
                    for tt in range(2):
                        em = EM[:, call - 2, 2 * u + tt, 0:NK2].unsqueeze(1).unsqueeze(1)\
                            .broadcast_to([P, NG, NC, NK2])
                        sc = Sps[:, :, P * tt:P * tt + P].rearrange("p g (x m) -> p g x m", m=S)[:, :, :, 0:NK2]
                        dve.tensor_tensor(PR[:, U % 3, :, NC * tt:NC * tt + NC, 0:NK2], sc, em, ALU.mult)\
                           .then_inc(masked.sem, 1)
                    for tt in range(2):
                        eb = EB[:, call - 2, 2 * u + tt, 0:NK2].unsqueeze(1).unsqueeze(1)\
                            .broadcast_to([P, NG, NC, NK2])
                        part = PR[:, U % 3, :, NC * tt:NC * tt + NC, 0:NK2]
                        dve.wait_ge(masked.sem, masked.after(U - 4, 1 + tt))
                        dve.tensor_tensor(part, part, eb, ALU.add).then_inc(biased.sem, 1)
                elif k == "less_max" and n < NUNIT:
                    U = n
                    call, u = UNITS[U]
                    n = S if call < 2 else NK2
                    sc = Sps[:, :, 0:UT].rearrange("p g (x m) -> p g x m", m=S)[:, :, :, 0:n]
                    pr = PR[:, U % 3, :, :, 0:n]
                    if call == 0:
                        if U == 3:
                            dve.wait_ge(made.sem, count_made("pt", 1))
                        dve.wait_ge(s_made.sem, s_made.after(U))
                    elif call == 1:
                        dve.wait_ge(masked.sem, masked.after(U - 4))
                    else:
                        dve.wait_ge(biased.sem, biased.after(U - 8))
                    src = sc if call == 0 else pr
                    mx = MX[:, U % 2, :].rearrange("p (g x) -> p g x", g=NG)
                    dve.tensor_reduce(mx, src, AX, ALU.max).then_inc(smax.sem, 1)
                    dve.wait_ge(smax.sem, smax.after(U))
                    dve.tensor_tensor(pr, src, mx.unsqueeze(3).broadcast_to([P, NG, 2 * NC, n]), ALU.subtract)\
                       .then_inc(ssub.sem, 1)
                elif k == "sum":
                    U = n
                    if U < NUNIT:
                        n = S if UNITS[U][0] < 2 else NK2
                        heads = 2 * NH
                        pr = PR[:, U % 3].rearrange("p g x m -> p (g x) m")[:, :, 0:n]
                    else:
                        heads = NH
                        pr = PR[:, U % 3, 0:2].rearrange("p g x m -> p (g x) m")
                    if U >= 2:
                        dve.wait_ge(prob.sem, prob.after(U - 2))
                    dve.wait_ge(expd.sem, expd.after(U))
                    dve.tensor_reduce(SM[:, U % 2, 0:heads], pr, AX, ALU.add).then_inc(ssum.sem, 1)
                    dve.wait_ge(ssum.sem, ssum.after(U, 1))
                    dve.reciprocal(RS[:, U % 2, 0:heads], SM[:, U % 2, 0:heads]).then_inc(ssum.sem, 1)
                elif k == "o2":
                    U = n + 8
                    call, u = UNITS[U]
                    a = ACC[:, UT * u:UT * u + UT]
                    dve.wait_ge(made.sem, count_made("o2", U - 8))
                    base = TM[:, 1, UT * u:UT * u + UT] if call == 2 else a
                    if call == 2:
                        dve.wait_ge(self_r.sem, self_r.after(u // 2))
                    else:
                        dve.wait_ge(acc_r.sem, acc_r.after(U - 9))
                        dve.wait_ge(xT_r.sem, xT_r.after(u // 2))
                    dve.scalar_tensor_tensor(a, bank("o2", U - 8)[:, 0:UT], col(f"bo{call}"), base, ALU.add, ALU.add)\
                       .then_inc(acc_r.sem, 1)
                    if call == 3:
                        dve.wait_ge(acc_r.sem, acc_r.after(U - 8))
                        dve.scalar_tensor_tensor(a, a, 0.0, TM[:, 0, UT * u:UT * u + UT], ALU.max, ALU.add)\
                           .then_inc(rel_r.sem, 1)
                elif k == "y":
                    U = n
                    u = UNITS[U][1]
                    dve.wait_ge(made.sem, count_made("y", U))
                    call = UNITS[U][0]
                    dve.wait_ge(xb_r.sem, xb_r.after(NORM_AT[2 * call, u // 2]))
                    xt = slice(2 * u, 2 * u + 2)
                    dve.tensor_tensor(X[:, xt, :], bank("y", U)[:, 0:UT].rearrange("p (t f) -> p t f", t=2),
                                      XB[:, xt, :], ALU.add).then_inc(x_r.sem, 1)
                elif k == "down":
                    h = n
                    dve.wait_ge(made.sem, count_made("down", h))
                    dve.wait_ge(xb_r.sem, xb_r.after(NORM_AT[3, h]))
                    dve.tensor_tensor(X[:, tiles(h), :], bank("down", h)[:, :].rearrange("p (t f) -> p t f", t=4),
                                      XB[:, tiles(h), :], ALU.add).then_inc(xm_r.sem, 1)
                elif k == "nonzero":
                    h = n
                    dve.wait_ge(xm_r.sem, xm_r.after(h))
                    dve.tensor_reduce(NZ[:, h, 0, :], X[:, tiles(h), :], AX, ALU.add).then_inc(nz_r.sem, 1)
                    dve.wait_ge(nz_r.sem, nz_r.after(h, 1))
                    dve.tensor_scalar(NZ[:, h, 1, :], NZ[:, h, 0, :], 0.0, None, ALU.not_equal).then_inc(nz_r.sem, 1)
                elif k == "nz":
                    h = n
                    dve.wait_ge(made.sem, count_made("up", NCH * h + NCH - 1))
                    dve.wait_ge(made.sem, count_made("nz", h))
                    dve.tensor_tensor(HTb[:, half(h)].rearrange("p (b q) -> p b q", q=S),
                                      bank("nz", h)[:, :].rearrange("p (b q) -> p b q", q=S),
                                      spread(w("condT")[:, 16 * h:16 * h + 16], S), ALU.mult).then_inc(qe_r.sem, 1)
                elif k == "center":
                    dve.wait_ge(load_l3.sem, load_l3.after())
                    dve.tensor_reduce(WS[:, :], w("l3_wqkv", 0, 2048).rearrange("p (h f) -> p h f", f=HD3), AX,
                                      ALU.add).then_inc(wsum.sem, 1)
                    dve.wait_ge(wsum.sem, wsum.after(0, 1))
                    dve.tensor_scalar(WS[:, :], WS[:, :], -1.0 / HD3, None, ALU.mult).then_inc(wsum.sem, 1)
                elif k == "ss3":
                    if n >= 4:
                        dve.wait_ge(qn_r.sem, qn_r.after(n - 4))
                    dve.wait_ge(sq_r.sem, sq_r.after(n))
                    dve.tensor_reduce(SS3[:, n % 4, 0, :], SQ3[:, n % 2, :].rearrange("p (h f) -> p h f", f=HD3),
                                      AX, ALU.add).then_inc(ss_r.sem, 1)
                elif k == "qk3":
                    if n >= 4:
                        dve.wait_ge(made.sem, count_made("qkT3", n - 4))
                    dve.wait_ge(r3_r.sem, r3_r.after(n))
                    dve.tensor_tensor(QN3[:, n % 4, :].rearrange("p (h f) -> p h f", f=HD3),
                                      bank("qk3", n)[:, :].rearrange("p (h f) -> p h f", f=HD3),
                                      spread(SS3[:, n % 4, 2, :], HD3), ALU.mult).then_inc(qn_r.sem, 1)
                elif k == "less_max":
                    U = n
                    sc = Sps[:, 0:2, 0:UT].rearrange("p r (c m) -> p r c m", m=S)
                    pr = PR[:, U % 3, 0:2]
                    mx = MX[:, U % 2, 0:NH].rearrange("p (g x) -> p g x", g=2)
                    if U - 3 >= NUNIT:
                        dve.wait_ge(pb_r.sem, pb_r.after(U - 3 - NUNIT))
                    else:
                        dve.wait_ge(made.sem, count_made("pt", 2 * (U - 3) + 1))
                    dve.wait_ge(s_made.sem, s_made.after(U))
                    dve.tensor_reduce(mx, sc, AX, ALU.max).then_inc(smax.sem, 1)
                    dve.wait_ge(smax.sem, smax.after(U))
                    dve.tensor_tensor(pr, sc, mx.unsqueeze(3).broadcast_to([P, 2, 8, S]), ALU.subtract)\
                       .then_inc(ssub.sem, 1)
                elif k == "blocks":
                    t = n
                    U = NUNIT + t
                    if t == 0:
                        dve.wait_ge(pbz.sem, pbz.after())
                    if t >= 2:
                        dve.wait_ge(made.sem, count_made("o3", 2 * (t - 2) + 1))
                    dve.wait_ge(prob.sem, prob.after(U))
                    for j in range(BPT):
                        rows = slice(S * j, S * j + S)
                        dve.transpose(PBD[rows, t % 2, :, S * j:S * j + S],
                                      PR[rows, U % 3, 0:2].rearrange("p g x m -> p (g x) m")).then_inc(pb_r.sem, 1)
                elif k == "y3":
                    t = n
                    dve.wait_ge(made.sem, count_made("y3", t))
                    dve.wait_ge(xk_r.sem, xk_r.after(t // 4))
                    dve.tensor_tensor(X[:, t, :], bank("y3", t)[:, 0:D], X[:, t, :], ALU.add).then_inc(x3_r.sem, 1)
                elif k == "split":
                    h, i = n // 2, n % 2
                    xn = XN[:, tiles(h), :]
                    dve.wait_ge(xs_a.sem, xs_a.after(h, 1 + i))
                    dve.tensor_tensor(XSP[:, tiles(h), 2, :] if i else xn, xn, XSP[:, tiles(h), i, :], ALU.subtract)\
                       .then_inc(xs_v.sem, 1)
                elif k == "logit":
                    dve.wait_ge(made.sem, count_made("logit"))
                    lg = te(bank("logit")[:, 0:NT * NE])
                    dve.tensor_reduce(RT[:, 0:8], lg, AX, ALU.max).then_inc(rt.sem, 1)
                    dve.wait_ge(rt.sem, rt_step())
                    dve.tensor_tensor(te(RG[:, 0, :]), lg, spread(RT[:, 0:8], NE), ALU.subtract).then_inc(rt.sem, 1)
                    dve.wait_ge(rt.sem, rt_step())
                elif k == "softmax":
                    dve.wait_ge(rta.sem, rta.after())
                    dve.tensor_reduce(RT[:, 8:16], te(RG[:, 1, :]), AX, ALU.add).then_inc(rt.sem, 1)
                    dve.wait_ge(rt.sem, rt_step())
                    dve.reciprocal(RT[:, 8:16], RT[:, 8:16]).then_inc(rt.sem, 1)
                    dve.wait_ge(rt.sem, rt_step())
                    dve.tensor_tensor(te(gate), te(RG[:, 1, :]), spread(RT[:, 8:16], NE), ALU.mult).then_inc(rt.sem, 1)
                    at = rt_step()
                    dve.wait_ge(rt.sem, at)
                    assert at == RT_GATE
                    dve.tensor_copy(JUNK.rearrange("p (x r) -> p x r", r=16), spread(gate, 16)).then_inc(rt.sem, 1)
                    dve.wait_ge(rt.sem, rt_step())
                    dve.memset(RTI[:, 0:1], 0).then_inc(rt.sem, 1)
                    dve.wait_ge(rt.sem, rt_step())
                elif k == "round":
                    if n == 0:
                        dve.wait_ge(gb_r.sem, gb_r.after(1))
                    i, shift = n, SHIFTS[n]
                    dve.tensor_tensor(RTI[:, 1:2], RTI[:, 0:1], KI[:, i:i + 1], ALU.bitwise_or).then_inc(rt.sem, 1)
                    dve.wait_ge(rt.sem, rt_step())
                    dve.tensor_scalar(JUNK.bitcast(BF16)[:, 0:TOK], GBC, RTI[:, 1:2].bitcast(F32), 0.0, ALU.is_ge, ALU.add,
                                      accum_out=RT[:, 0:1]).then_inc(rt.sem, 1)
                    dve.wait_ge(rt.sem, rt_step())
                    dve.tensor_scalar(RT[:, 1:2], RT[:, 0:1], float(CAP), None, ALU.is_ge).then_inc(rt.sem, 1)
                    at = rt_step()
                    dve.wait_ge(rt.sem, at)
                    assert at == RT_ROUND[i] + 3
                elif k == "bits":
                    i, shift = n, SHIFTS[n]
                    dve.wait_ge(cnt.sem, cnt.after(i))
                    dve.tensor_scalar(RTI[:, 2:3], Sps[:, 0, 0:1], -1.0, float(1 << shift), ALU.add,
                                      ALU.mult).then_inc(rt.sem, 1)
                    dve.wait_ge(rt.sem, rt_step())
                    dve.tensor_tensor(RTI[:, 0:1], RTI[:, 0:1], RTI[:, 2:3], ALU.bitwise_or).then_inc(rt.sem, 1)
                    dve.wait_ge(rt.sem, rt_step())
                elif k == "flags":
                    dve.wait_ge(made.sem, count_made("thr"))
                    thr = stack(bank("thr")[:, 0:P:16], NT)
                    dve.tensor_tensor(te(above), te(gate), thr, ALU.is_gt).then_inc(rt.sem, 1)
                    dve.wait_ge(rt.sem, rt_step())
                    dve.tensor_tensor(te(at_thr), te(gate), thr, ALU.is_equal).then_inc(rt.sem, 1)
                    at = rt_step()
                    dve.wait_ge(rt.sem, at)
                    assert at == RT_EQ
                elif k == "slots":
                    dve.wait_ge(made.sem, count_made("total"))
                    need = RT[:, 2:10]
                    dve.tensor_scalar(need, bank("total")[:, 0:NE], -1.0, float(CAP), ALU.mult, ALU.add).then_inc(rt.sem, 1)
                    dve.wait_ge(rt.sem, rt_step())
                    dve.wait_ge(made.sem, count_made("prefix"))
                    pre = bank("prefix")[:, 0:2 * NT * NE].rearrange("p (i t e) -> p i t e", i=2, e=NE)
                    a, b, c, pos = (RG[:, i, :] for i in (4, 5, 6, 7))
                    dve.tensor_tensor(te(a), pre[:, 1], stack(need, NT), ALU.is_lt).then_inc(rt.sem, 1)
                    dve.wait_ge(rt.sem, rt_step())
                    dve.tensor_tensor(a, a, at_thr, ALU.mult).then_inc(rt.sem, 1)
                    dve.wait_ge(rt.sem, rt_step())
                    dve.tensor_tensor(a, a, above, ALU.add).then_inc(rt.sem, 1)
                    dve.wait_ge(rt.sem, rt_step())
                    dve.tensor_tensor(te(b), pre[:, 1], stack(need, NT), ALU.min).then_inc(rt.sem, 1)
                    dve.wait_ge(rt.sem, rt_step())
                    dve.tensor_tensor(te(b), te(b), pre[:, 0], ALU.add).then_inc(rt.sem, 1)
                    at = rt_step()
                    dve.wait_ge(rt.sem, at)
                    assert at == RT_PREFIX
                    dve.tensor_scalar(c, a, -512.0, 512.0, ALU.mult, ALU.add).then_inc(rt.sem, 1)
                    dve.wait_ge(rt.sem, rt_step())
                    dve.tensor_tensor(pos, b, c, ALU.add).then_inc(rt.sem, 1)
                    dve.wait_ge(rt.sem, rt_step())
                    dve.tensor_copy(RGB[:, 2, :], pos).then_inc(rt.sem, 1)
                    at = rt_step()
                    dve.wait_ge(rt.sem, at)
                    assert at == RT_POS
                elif k == "split_gates":
                    parts = RGB[:, 3:6, :]
                    dve.wait_ge(rt.sem, RT_GATE)
                    for i in range(3):
                        if i:
                            dve.wait_ge(sg_r.sem, sg_r.after(0, 2 * i))
                        if i < 2:
                            dve.tensor_copy(parts[:, i, :], gate if i == 0 else RG[:, 3, :]).then_inc(sg_r.sem, 1)
                            dve.wait_ge(sg_r.sem, sg_r.after(0, 2 * i + 1))
                            dve.tensor_tensor(RG[:, 3, :], gate if i == 0 else RG[:, 3, :], parts[:, i, :],
                                              ALU.subtract).then_inc(sg_r.sem, 1)
                        else:
                            dve.tensor_copy(parts[:, 2, :], RG[:, 3, :]).then_inc(sg_r.sem, 1)
                elif k == "pick":
                    if n == 0:
                        dve.wait_ge(rt.sem, RT_POS)
                    dve.tensor_tensor(PIC[:, n].rearrange("p (e s) -> p e s", e=NE), stack(konst_b("iota_row"), NE),
                                      spread(RGB[:, 2, NE * n:NE * n + NE], CAP), ALU.is_equal).then_inc(pic_v.sem, 1)
                elif k == "weight":
                    dve.wait_ge(made.sem, count_made("weight"))
                    dve.tensor_reduce(RT[:, 0:NE], bank("weight")[:, 0:3 * NE].rearrange("p (e k) -> p e k", k=3), AX,
                                      ALU.add).then_inc(wt_r.sem, 1)
                elif k == "fc2":
                    y, r = YB[:, n % 2, 0, :], YB[:, n % 2, 1, :]
                    dve.wait_ge(made.sem, count_made("fc2", n))
                    dve.tensor_tensor(y, bank("fc2", n)[:, 0:D], row("b2s", D * n, D), ALU.add).then_inc(y_r.sem, 1)
                    dve.wait_ge(wt_r.sem, wt_r.after())
                    dve.wait_ge(y_r.sem, y_r.after(n, 1))
                    dve.tensor_scalar(y, y, RT[:, n:n + 1], None, ALU.mult).then_inc(y_r.sem, 1)
                    dve.wait_ge(y_r.sem, y_r.after(n, 2))
                    dve.tensor_copy(YSP[:, n, 0, :], y).then_inc(y_r.sem, 1)
                    dve.wait_ge(y_r.sem, y_r.after(n, 3))
                    dve.tensor_tensor(r, y, YSP[:, n, 0, :], ALU.subtract).then_inc(y_r.sem, 1)
                    dve.wait_ge(y_r.sem, y_r.after(n, 4))
                    dve.tensor_copy(YSP[:, n, 1, :], r).then_inc(y_r.sem, 1)
                    dve.wait_ge(y_r.sem, y_r.after(n, 5))
                    dve.tensor_tensor(YSP[:, n, 2, :], r, YSP[:, n, 1, :], ALU.subtract).then_inc(y_r.sem, 1)
                elif k == "scatter":
                    h = n % 2
                    rows = RES[:, tiles(h), :]
                    if n >= 2:
                        dve.wait_ge(res_r.sem, res_r.after(n - 2))
                    dve.wait_ge(made.sem, count_made("scatter", n))
                    dve.tensor_tensor(rows, bank("scatter", n)[:, :].rearrange("p (t f) -> p t f", t=4),
                                      X[:, tiles(h), :] if n < 2 else rows, ALU.add).then_inc(res_r.sem, 1)
                else:
                    raise ValueError(k)

        @block.tensor
        def _(pe):
            def mm(out, lhsT, rhs, start=True, stop=True):
                return pe.matmul(out, lhsT, rhs, start=start, stop=stop)

            def turn4(out, src):
                for i in range(4):
                    last = pe.transpose(out[:, P * i:P * i + P], src(i), ident)
                return last

            for k, n in PE_STEPS:
                if k in TAKEN:
                    b = bank(k, n)
                    if used_before(k, n):
                        pe.wait_ge(*last_read(k, n))
                if k == "cond":
                    pe.wait_ge(load_first.sem, load_first.after())
                    for i, lhsT in enumerate([w("l0_wg"), w("l0_wb"), w("l1_ad1", 0, D), w("l1_ad1", D, D),
                                              w("l1_ad2", 0, D), w("l1_ad2", D, D)]):
                        last = mm(b[:, B * i:B * i + B], lhsT, w("condT"))
                    last.then_inc(made.sem, 1)
                elif k == "ada":
                    pe.wait_ge(silu.sem, silu.after())
                    mm(b[:, 0:B], w("l3_ada"), CS[:, 0, :]).then_inc(made.sem, 1)
                elif k == "tokmod":
                    pe.wait_ge(cond_r.sem, cond_r.after())
                    for t in range(4):
                        for j in range(BPT):
                            at = 16 * (n % 2) + 4 * t + j
                            last = mm(b[S * j:S * j + S, P * t:P * t + P],
                                      CM[:, n // 2, at:at + 1].broadcast_to([P, S]), ident)
                    last.then_inc(made.sem, 1)
                elif k == "xnT":
                    h = n % 2
                    pe.wait_ge(normed.sem, normed.after(NORM_AT[(0, 2, 3)[n // 2], h]))
                    turn4(b, lambda i: XN[:, 4 * h + i, :]).then_inc(made.sem, 1)
                elif k == "xnT3":
                    pe.wait_ge(normed.sem, normed.after(NORM_AT[4, n]))
                    turn4(b, lambda i: XN[:, 4 * n + i, :]).then_inc(made.sem, 1)
                elif k in ("q", "k", "v"):
                    call, h = PROJECTS[n]
                    name = ("l0_w{}", "l1_w{}", "l2_w{}0", "l2_w{}1")[call].format(k)
                    if call < 2:
                        loaded = load_l1 if call else load_l0
                        pe.wait_ge(loaded.sem, loaded.after())
                        pe.wait_ge(modul.sem, modul.after(2 * call + h))
                        src = HTb[:, half(h)]
                    else:
                        pe.wait_ge(self_r.sem, self_r.after(h))
                        src = TM[:, 1, half(h)]
                    if k == "v":
                        for i in range(16):
                            for c in range(NC):
                                last = mm(b[S * c:S * c + S, S * i:S * i + S], src[:, S * i:S * i + S],
                                          w(name, S * c, S))
                        last.then_inc(made.sem, 1)
                    else:
                        mm(b[:, :], w(name), src).then_inc(made.sem, 1)
                elif k == "scores":
                    U = n
                    call, u = UNITS[U]
                    par, m = call // 3, S if call < 2 else NK2
                    if 1 <= U <= 4:
                        pe.wait_ge(ssub.sem, ssub.after(U - 1))
                    elif U > 4:
                        pe.wait_ge(masked.sem, masked.after(U - 5))
                    nth = PROJECT_AT[call, u // 2]
                    pe.wait_ge(q_r.sem, q_r.after(nth))
                    pe.wait_ge(k_r.sem, k_r.after(nth))
                    for tt in range(2):
                        for j in range(BPT):
                            t0 = UT * u + P * tt + S * j
                            for g in range(NG):
                                rows = slice(S * g, S * g + S)
                                o = Sps[S * j:S * j + S, g, P * tt:P * tt + P].rearrange("p (c m) -> p c m", m=S)
                                last = mm(o[:, :, 0:m], QT[rows, par, t0:t0 + S], KBLK[par][rows, :, t0:t0 + m])
                    last.then_inc(s_made.sem, 1)
                elif k == "pt":
                    U, tt = n // 2, n % 2
                    pe.wait_ge(prob.sem, prob.after(U))
                    turn4(b, lambda g: PR[:, U % 3, g, NC * tt:NC * tt + NC, :].rearrange("p c m -> p (c m)"))\
                        .then_inc(made.sem, 1)
                elif k in ("o", "o2"):
                    U = n if k == "o" else n + 8
                    call, u = UNITS[U]
                    pe.wait_ge(pt_r.sem, pt_r.after(2 * U + 1))
                    pe.wait_ge(v_r.sem, v_r.after(PROJECT_AT[call, u // 2]))
                    for tt in range(2):
                        for j in range(BPT):
                            vblk = VBLK[call // 3][:, 8 * u + 4 * tt + j]
                            for g in range(NG):
                                last = mm(b[S * g:S * g + S, P * tt + S * j:P * tt + S * j + S],
                                          vblk[:, g].rearrange("p c f -> p (c f)"),
                                          PTS[:, U % 2, tt, g, S * j:S * j + S])
                    last.then_inc(made.sem, 1)
                elif k == "y":
                    pe.wait_ge(o_r.sem, o_r.after(n))
                    for tt in range(2):
                        last = mm(b[:, P * tt:P * tt + P], OT[:, n % 2, P * tt:P * tt + P],
                                  w("l0_wp" if n < 4 else "l1_wo"))
                    last.then_inc(made.sem, 1)
                elif k == "up":
                    h, c = n // NCH, n % NCH
                    if n == 0:
                        pe.wait_ge(vz.sem, vz.after(1))
                    pe.wait_ge(modul.sem, modul.after(4 + h))
                    mm(b[:, :], w("l1_w1", P * c, P), HTb[:, half(h)]).then_inc(made.sem, 1)
                elif k == "down":
                    pe.wait_ge(gelu.sem, gelu.after(NCH * n + NCH - 1))
                    for t in range(4):
                        for c in range(NCH):
                            t0 = HT * n + P * t
                            last = mm(b[:, P * t:P * t + P], HIDb[:, c, t0:t0 + P], w("l1_w2", P * c, P),
                                      c == 0, c == NCH - 1)
                    last.then_inc(made.sem, 1)
                elif k == "xT":
                    pe.wait_ge(xm_r.sem, xm_r.after(n))
                    turn4(b, lambda i: X[:, 4 * n + i, :]).then_inc(made.sem, 1)
                elif k == "nz":
                    pe.wait_ge(nz_r.sem, nz_r.after(n))
                    for t in range(4):
                        last = mm(b[:, P * t:P * t + P], NZ[:, n, 1, t:t + 1].broadcast_to([P, P]), ident)
                    last.then_inc(made.sem, 1)
                elif k == "self":
                    if n == 0:
                        pe.wait_ge(load_l2.sem, load_l2.after())
                    pe.wait_ge(xT_r.sem, xT_r.after(n))
                    mm(b[:, :], w("l2_ws1"), TM[:, 0, half(n)], True, False)
                    pe.wait_ge(qe_r.sem, qe_r.after(n))
                    mm(b[:, :], w("l2_ws2"), HTb[:, half(n)], False, True).then_inc(made.sem, 1)
                elif k == "back":
                    pe.wait_ge(rel_r.sem, rel_r.after(2 * n + 1))
                    turn4(b, lambda i: ACC[:, HT * n + P * i:HT * n + P * i + P]).then_inc(made.sem, 1)
                elif k in ("qk3", "v3"):
                    t, i = divmod(n, 4 if k == "qk3" else 2)
                    pe.wait_ge(h3_r.sem, h3_r.after(t // 4))
                    if k == "qk3" and n < 4:
                        pe.wait_ge(wc_r.sem, wc_r.after(0, i // 2 + 1))
                    mm(b[:, :], HTb[:, P * t:P * t + P], w("l3_wqkv", (0 if k == "qk3" else 2048) + 512 * i, 512))\
                        .then_inc(made.sem, 1)
                elif k == "qkT3":
                    pe.wait_ge(qn_r.sem, qn_r.after(n))
                    turn4(b, lambda c: QN3[:, n % 4, P * c:P * c + P]).then_inc(made.sem, 1)
                elif k == "scores3":
                    t = n
                    if t == 0:
                        pe.wait_ge(masked.sem, masked.after(NUNIT - 5))
                    else:
                        pe.wait_ge(ssub.sem, ssub.after(NUNIT + t - 1))
                    pe.wait_ge(qk_r.sem, qk_r.after(4 * t + 3))
                    for c in range(8):
                        for j in range(BPT):
                            for r in range(2):
                                rows = slice(HD3 * r, HD3 * r + HD3)
                                last = mm(Sps[S * j:S * j + S, r, S * c:S * c + S],
                                          QK3[rows, t % 2, 0, c, S * j:S * j + S],
                                          QK3[rows, t % 2, 1, c, S * j:S * j + S])
                    last.then_inc(s_made.sem, 1)
                elif k == "o3":
                    t, i = divmod(n, 2)
                    pe.wait_ge(v3_r.sem, v3_r.after(n))
                    pe.wait_ge(pb_r.sem, pb_r.after(t))
                    for c in range(4 * i, 4 * i + 4):
                        for r in range(2):
                            last = mm(b[HD3 * r:HD3 * r + HD3, P * (c % 4):P * (c % 4) + P],
                                      V3[:, t % 2, HD3 * (2 * c + r):HD3 * (2 * c + r) + HD3],
                                      PBD[:, t % 2, 8 * r + c, :])
                    last.then_inc(made.sem, 1)
                elif k == "y3":
                    pe.wait_ge(o3_r.sem, o3_r.after(2 * n + 1))
                    for c in range(8):
                        last = mm(b[:, 0:D], OT3[:, n % 2, c, :], w("l3_wout", P * c, P), c == 0, c == 7)
                    last.then_inc(made.sem, 1)
                elif k == "tokT":
                    pe.wait_ge(x3_r.sem, x3_r.after(4 * n + 3))
                    turn4(b, lambda i: X[:, 4 * n + i, :]).then_inc(made.sem, 1)
                elif k == "logit":
                    pe.wait_ge(tt_r.sem, tt_r.after(1))
                    for t in range(NT):
                        last = mm(b[:, NE * t:NE * t + NE], TOKT[:, P * t:P * t + P], w("l3_gate"))
                    last.then_inc(made.sem, 1)
                elif k == "gates":
                    pe.wait_ge(rt.sem, RT_GATE + 1)
                    turn4(b, lambda t: JUNK[:, P * (4 * n + t):P * (4 * n + t) + P]).then_inc(made.sem, 1)
                elif k == "counts":
                    pe.wait_ge(rt.sem, RT_ROUND[n] + 3)
                    mm(Sps[:, 0, 0:1], konst("group16"), RT[:, 1:2]).then_inc(cnt.sem, 1)
                elif k == "thr":
                    pe.wait_ge(rt.sem, RT_ROUND[ROUNDS])
                    pe.transpose(b[:, 0:P], RTI[:, 0:1].bitcast(F32).broadcast_to([P, P]), ident).then_inc(made.sem, 1)
                elif k == "prefix":
                    pe.wait_ge(rt.sem, RT_EQ)
                    flags = RGB[:, 0:2, :].rearrange("p i (t e) -> p i t e", e=NE)
                    o = b[:, 0:2 * NT * NE].rearrange("p (i t e) -> p i t e", i=2, e=NE)
                    mm(b[:, 0:2 * NT * NE], konst_b("before"), RGB[:, 0:2, :], True, False)
                    for t in range(NT - 1):
                        for i in range(2):
                            last = mm(o[:, i, t + 1:NT, :], konst_b("ones"), stack(flags[:, i, t, :], NT - 1 - t),
                                      False, t == NT - 2 and i == 1)
                    last.then_inc(made.sem, 1)
                elif k == "total":
                    flags = RGB[:, 0, :].rearrange("p (t e) -> p t e", e=NE)
                    pe.wait_ge(rt.sem, RT_EQ)
                    for t in range(NT):
                        last = mm(b[:, 0:NE], konst_b("ones"), flags[:, t, :], t == 0, t == NT - 1)
                    last.then_inc(made.sem, 1)
                elif k == "pickT":
                    pe.wait_ge(pic_v.sem, pic_v.after(4 * (n % 2) + 3))
                    for t in range(4):
                        last = mm(b[:, P * t:P * t + P], PIC[:, 4 * (n % 2) + t, CAP * (n // 2):CAP * (n // 2) + CAP],
                                  konst_b("ident"))
                    last.then_inc(made.sem, 1)
                elif k == "gather":
                    t, i = n // 2, n % 2
                    if n == 0:
                        pe.wait_ge(xs_v.sem, xs_v.after(1))
                        pe.wait_ge(xs_a.sem, xs_a.after(1))
                    pe.wait_ge(pic_v.sem, pic_v.after(t))
                    for c in range(3):
                        last = mm(Sps[:, i, :], XSP[:, t, c, :], PIC[:, t, 512 * i:512 * i + 512],
                                  t == 0 and c == 0, t == NT - 1 and c == 2)
                    if t == NT - 1:
                        last.then_inc(g_made.sem, 1)
                elif k == "weight":
                    pe.wait_ge(sg_r.sem, sg_r.after())
                    pe.wait_ge(pic_v.sem, pic_v.after(NT - 1))
                    for e in range(NE):
                        for t in range(NT):
                            last = mm(b[:, 3 * e:3 * e + 3], PIC[:, t, CAP * e:CAP * e + CAP],
                                      RGB[:, 3:6, NE * t + e], t == 0, t == NT - 1)
                    last.then_inc(made.sem, 1)
                elif k == "fc1":
                    if n == 0:
                        pe.wait_ge(load_fc.sem, load_fc.after())
                    pe.wait_ge(gt_r.sem, gt_r.after(n // 4))
                    for c in range(NCH):
                        last = mm(b[:, P * c:P * c + P], w("fc1", HID * n + P * c, P), GTT[:, CAP * n:CAP * n + CAP])
                    last.then_inc(made.sem, 1)
                elif k == "fc2":
                    pe.wait_ge(he_r.sem, he_r.after(n))
                    for c in range(NCH):
                        last = mm(b[:, 0:D], HE[:, n % 2, c, :], w("fc2", HID * n + P * c, P), c == 0, c == NCH - 1)
                    last.then_inc(made.sem, 1)
                elif k == "scatter":
                    first, h = 4 * (n // 2), n % 2
                    pe.wait_ge(pict_r.sem, pict_r.after(2 * (first + 3) + h))
                    pe.wait_ge(y_r.sem, y_r.after(first + 3))
                    for t in range(4 * h, 4 * h + 4):
                        for e in range(first, first + 4):
                            for c in range(3):
                                last = mm(b[:, P * (t % 4):P * (t % 4) + P], PICT[:, e, P * t:P * t + P],
                                          YSP[:, e, c, :], e == first and c == 0, e == first + 3 and c == 2)
                    last.then_inc(made.sem, 1)
                else:
                    raise ValueError(k)


def heads_cgf(a):
    return np.ascontiguousarray(a.reshape(NG, NC, HD, -1).transpose(1, 0, 2, 3)).reshape(D, -1)


def pack(parts, pieces):
    for name, n in parts:
        assert pieces[name].shape[1] == n, (name, pieces[name].shape)
    return np.ascontiguousarray(np.concatenate([pieces[name] for name, _ in parts], axis=1))


def packed_inputs(v):
    def T(a):
        return a.T

    def chunks(a):
        return a.reshape(-1, P, a.shape[1]).transpose(1, 0, 2).reshape(P, -1)

    def column(a):
        return a.reshape(-1, P).T

    qkv0 = v["L0_cond_Wqkv"].reshape(D, 3, D)
    bqkv0 = v["L0_cond_bqkv"].reshape(D, 3)
    weights = {
        "condT": T(v["cond_1024"]), "l0_wg": T(v["L0_cond_Wg"]), "l0_wb": T(v["L0_cond_Wb"]),
        "l1_ad1": T(v["L1_cond_w_adaln1"]), "l1_ad2": T(v["L1_cond_w_adaln2"]), "l3_ada": T(v["L3_cond_W_ada"]),
        "l0_wq": T(qkv0[:, 0]), "l0_wk": T(qkv0[:, 1]), "l0_wv": T(heads_cgf(qkv0[:, 2])), "l0_wp": T(v["L0_cond_Wp"]),
        "l1_wq": T(v["L1_cond_wq"]), "l1_wk": T(v["L1_cond_wk"]), "l1_wv": T(heads_cgf(v["L1_cond_wv"])),
        "l1_wo": T(v["L1_cond_wo"]), "l1_w1": T(v["L1_cond_w1"]), "l1_w2": chunks(T(v["L1_cond_w2"])),
        "l2_ws1": T(v["L2_cond_W_self"][:, :D]), "l2_ws2": T(v["L2_cond_W_self"][:, D:]),
        "l3_wqkv": T(v["L3_cond_Wqkv"]), "l3_wout": chunks(T(v["L3_cond_Wout"])), "l3_gate": T(v["L3_cond_Wgate"]),
        "fc1": v["L3_cond_fc1s"].transpose(2, 0, 1).reshape(D, -1),
        "fc2": v["L3_cond_fc2s"].reshape(NE, D, NCH, P).transpose(3, 0, 2, 1).reshape(P, -1),
    }
    for d in range(2):
        weights[f"l2_wq{d}"] = T(v["L2_cond_Wq"][d])
        weights[f"l2_wk{d}"] = T(v["L2_cond_Wk"][d])
        weights[f"l2_wv{d}"] = T(heads_cgf(v["L2_cond_Wout"][d].reshape(D, D)))
    twice = lambda a: np.concatenate([a, a])
    columns = {
        "ln_g": v["L0_cond_ln_g"], "ln_b": v["L0_cond_ln_b"], "bg": v["L0_cond_bg"], "bb": v["L0_cond_bb"],
        "bq0": bqkv0[:, 0], "bk0": bqkv0[:, 1], "bv0": bqkv0[:, 2],
        "ad1": v["L1_cond_b_adaln1"], "ad2": v["L1_cond_b_adaln2"], "bq1": v["L1_cond_bq"], "bk1": v["L1_cond_bk"],
        "bv1": v["L1_cond_bv"], "b1": v["L1_cond_b1"], "bself": v["L2_cond_b_self"],
        "bq2": v["L2_cond_bq"][0], "bq3": v["L2_cond_bq"][1], "bk2": v["L2_cond_bk"][0], "bk3": v["L2_cond_bk"][1],
        "bo2": v["L2_cond_bout"][0], "bo3": v["L2_cond_bout"][1],
        "b_ada": v["L3_cond_b_ada"], "ln1_g": v["L3_cond_ln1_g"], "ln1_b": v["L3_cond_ln1_b"],
        "qn_g": twice(v["L3_cond_qn_g"]), "qn_b": twice(v["L3_cond_qn_b"]),
        "kn_g": twice(v["L3_cond_kn_g"]), "kn_b": twice(v["L3_cond_kn_b"]),
        "mlp_g": v["L3_cond_mlp_g"], "mlp_b": v["L3_cond_mlp_b"], "b1s": v["L3_cond_b1s"].reshape(-1),
    }
    rows = {
        "bp": v["L0_cond_bp"], "bo": v["L1_cond_bo"], "b2": v["L1_cond_b2"], "w_bias": v["L2_cond_w_bias"],
        "b_bias": v["L2_cond_b_bias"].reshape(1), "b2s": v["L3_cond_b2s"].reshape(-1),
    }
    return (pack(W_PARTS, weights), pack(C_PARTS, {n: column(a) for n, a in columns.items()}),
            pack(R_PARTS, {n: a.reshape(1, -1) for n, a in rows.items()}))


def constants():
    p = np.arange(P)
    eye = np.eye(P, dtype=np.float32)
    k = {
        "ident": eye, "head_mask": (p[:, None] // HD % NC == np.arange(NC)).astype(np.float32),
        "group16": (p[:, None] // 16 == p // 16).astype(np.float32), "mhalf": np.full((P, 32), -0.5, np.float32),
    }
    kb = {"ident": eye, "before": (p[:, None] < p).astype(np.float32), "ones": np.ones((P, P), np.float32),
          "iota_row": np.broadcast_to(p, (P, P)).astype(np.float32)}
    ki = np.stack([(p % 16) << s if s < 28 else np.where(p % 16 < 4, (p % 16) << s, 0x7F000000) for s in SHIFTS], 1)
    return pack(K_PARTS, k), pack(KB_PARTS, kb), ki.astype(np.int32)


def kernel(**inputs):
    import ml_dtypes
    import concourse.bacc as bacc
    from concourse.bass_utils import run_bass_kernel_spmd

    v = {n: np.asarray(a) for n, a in inputs.items()}
    w, c, r = packed_inputs(v)
    k, kb, ki = constants()
    pad = v["mask_BxS_bf0"].reshape(NT, BPT, 1, S)
    pad = np.ascontiguousarray(np.broadcast_to(pad, (NT, BPT, S, S)).reshape(NT, P, S).transpose(1, 0, 2))
    arrays = {
        "x": np.ascontiguousarray(v["x"]), "weights": w, "columns": c, "rows": r, "constants": k,
        "constants_bf16": kb.astype(ml_dtypes.bfloat16), "candidates": ki, "padding": pad,
        "adjacency": np.ascontiguousarray(v["mask_BxSxSx11_ik0"]),
    }
    nc = bacc.Bacc("TRN2", target_bir_lowering=False, num_devices=1)
    aps = [nc.dram_tensor(f"{n}_in", a.shape, U8 if a.dtype == bool else mybir.dt.from_np(a.dtype),
                          kind="ExternalInput").ap()
           for n, a in arrays.items()]
    out = nc.dram_tensor("result", (B, S, D), F32, kind="ExternalOutput").ap()
    conditional_blocks(nc, *aps, out)
    r = run_bass_kernel_spmd(nc, [{f"{n}_in": a for n, a in arrays.items()}], core_ids=[0])
    return r.results[0]["result"]
```
